# Optimizing a Trainium2 kernel written in Bass

```python
import numpy as np
import jax
import jax.numpy as jnp

def _softmax(x, axis=-1):
    return jax.nn.softmax(x, axis=axis)

def _gelu(x):
    return jax.nn.gelu(x, approximate=True)

def _silu(x):
    return jax.nn.silu(x)

def _sigmoid(x):
    return jax.nn.sigmoid(x)

def _layernorm(x, axis=-1, eps=1e-05):
    m = jnp.mean(x, axis=axis, keepdims=True)
    v = jnp.var(x, axis=axis, keepdims=True)
    return (x - m) / jnp.sqrt(v + eps)

def _scatter_add(tgt, idx, src, axis=0):
    return tgt.at[idx].add(src)

def _segment_sum(src, seg, n):
    return jax.ops.segment_sum(src, seg, n)
kernel_name = 'mk_gnn_preln_d4_gnn_r8_5560a7'

def setup_inputs(seed: int=0):
    np.random.seed(seed)
    _w = jnp.asarray

    def _rec_inputs():
        import jax
        import jax.numpy as jnp
        _gk = jax.random.key(seed)
        x = -0.0003713 + 1 * jax.random.normal(jax.random.fold_in(_gk, 1), (6250, 128), jnp.float32)
        src = jax.random.randint(jax.random.fold_in(_gk, 2), (100000,), 0, 6250, jnp.int32)
        dst = jax.random.randint(jax.random.fold_in(_gk, 3), (100000,), 0, 6250, jnp.int32)
        _o = jnp.argsort(dst, stable=True)
        src = src[_o]
        dst = dst[_o]
        edge_type_8 = jax.random.randint(jax.random.fold_in(_gk, 13), (100000,), 0, 8, jnp.int32)
        return (x, src, dst, edge_type_8)
    x, src, dst, edge_type_8 = _rec_inputs()

    def _L0_gnn_setup():
        import jax, jax.numpy as jnp
        import numpy as np
        N_NODES = 12500
        N_EDGES = 75000
        H = 128
        T = 8
        L = 2

        def _gru_cell(x, h, wih, whh, bih, bhh):
            gi = x @ wih.T + bih
            gh = h @ whh.T + bhh
            i_r, i_z, i_n = jnp.split(gi, 3, axis=-1)
            h_r, h_z, h_n = jnp.split(gh, 3, axis=-1)
            r = jax.nn.sigmoid(i_r + h_r)
            z = jax.nn.sigmoid(i_z + h_z)
            n = jnp.tanh(i_n + r * h_n)
            return (1.0 - z) * n + z * h
        key = jax.random.key(seed)
        ks = jax.random.split(key, 12)
        s = 1.0 / np.sqrt(H)
        inp = {'node_features': jax.random.normal(ks[0], (N_NODES, H), dtype=jnp.float32), 'edge_index': jax.random.randint(ks[1], (2, N_EDGES), 0, N_NODES, dtype=jnp.int64), 'edge_type': jax.random.randint(ks[2], (N_EDGES,), 0, T, dtype=jnp.int64), 'node_proj_w': jax.random.uniform(ks[3], (H, H), jnp.float32, -s, s), 'node_proj_b': jax.random.uniform(ks[4], (H,), jnp.float32, -s, s), 'edge_W': jax.random.uniform(ks[5], (L, T, H, H), jnp.float32, -s, s), 'edge_b': jax.random.uniform(ks[6], (L, T, H), jnp.float32, -s, s), 'gru_wih': jax.random.uniform(ks[7], (L, 3 * H, H), jnp.float32, -s, s), 'gru_whh': jax.random.uniform(ks[8], (L, 3 * H, H), jnp.float32, -s, s), 'gru_bih': jax.random.uniform(ks[9], (L, 3 * H), jnp.float32, -s, s), 'gru_bhh': jax.random.uniform(ks[10], (L, 3 * H), jnp.float32, -s, s), 'out_w': jax.random.uniform(ks[11], (H, H), jnp.float32, -s, s), 'out_b': jnp.zeros((H,), jnp.float32)}
        return inp
    _L0_gnn_all = _L0_gnn_setup()
    _L0_gnn_in = {k: v for k, v in _L0_gnn_all.items() if k in ('node_proj_w', 'node_proj_b', 'edge_W', 'edge_b', 'gru_wih', 'gru_whh', 'gru_bih', 'gru_bhh', 'out_w', 'out_b')}
    del _L0_gnn_all

    def _L1_gnn_setup():
        import jax, jax.numpy as jnp
        import numpy as np
        N, E, F = (6250, 100000, 128)
        DELTA = 1.0
        EPS = 1e-05

        def _pna_forward(x, edge_index, W_pre, b_pre, W_post, b_post, W_lin, b_lin):
            src, dst = (edge_index[0], edge_index[1])
            n = x.shape[0]
            h = jnp.concatenate([x[dst], x[src]], axis=-1)
            m = h @ W_pre.T + b_pre
            deg = jax.ops.segment_sum(jnp.ones((m.shape[0],), m.dtype), dst, num_segments=n)
            deg_c = jnp.maximum(deg, 1.0)[:, None]
            has_edge = (deg > 0)[:, None]
            mx = jax.ops.segment_max(m, dst, num_segments=n)
            mx = jnp.where(has_edge, mx, 0.0)
            mn = jax.ops.segment_min(m, dst, num_segments=n)
            mn = jnp.where(has_edge, mn, 0.0)
            s1 = jax.ops.segment_sum(m, dst, num_segments=n)
            s2 = jax.ops.segment_sum(m * m, dst, num_segments=n)
            mean = s1 / deg_c
            var = s2 / deg_c - mean * mean
            std = jnp.sqrt(jax.nn.relu(var) + EPS)
            agg = jnp.concatenate([mx, mn, mean, std], axis=-1)
            log_deg = jnp.log(deg_c + 1.0)
            amp = log_deg / DELTA
            att = DELTA / log_deg
            scaled = jnp.concatenate([agg, agg * amp, agg * att], axis=-1)
            out = jnp.concatenate([x, scaled], axis=-1) @ W_post.T + b_post
            return out @ W_lin.T + b_lin
        key = jax.random.key(seed)
        ks = jax.random.split(key, 6)
        x = jax.random.normal(ks[0], (N, F), dtype=jnp.float32)
        edge_index = jax.random.randint(ks[1], (2, E), 0, N, dtype=jnp.int32)
        W_pre = jax.random.normal(ks[2], (F, 2 * F), dtype=jnp.float32) * (2 * F) ** (-0.5)
        b_pre = jnp.zeros((F,), jnp.float32)
        W_post = jax.random.normal(ks[3], (F, 13 * F), dtype=jnp.float32) * (13 * F) ** (-0.5)
        b_post = jnp.zeros((F,), jnp.float32)
        W_lin = jax.random.normal(ks[4], (F, F), dtype=jnp.float32) * F ** (-0.5)
        b_lin = jnp.zeros((F,), jnp.float32)
        return {'x': x, 'edge_index': edge_index, 'W_pre': W_pre, 'b_pre': b_pre, 'W_post': W_post, 'b_post': b_post, 'W_lin': W_lin, 'b_lin': b_lin}
    _L1_gnn_all = _L1_gnn_setup()
    _L1_gnn_in = {k: v for k, v in _L1_gnn_all.items() if k in ('W_pre', 'b_pre', 'W_post', 'b_post', 'W_lin', 'b_lin')}
    del _L1_gnn_all

    def _L2_gnn_setup():
        import jax, jax.numpy as jnp
        import numpy as np
        N_NODES = 6250
        N_EDGES = 100000
        IN_FEATS = 128
        OUT_FEATS = 128
        key = jax.random.key(seed)
        k_x, k_s, k_d, k_w, k_b = jax.random.split(key, 5)
        x = jax.random.normal(k_x, (N_NODES, IN_FEATS), dtype=jnp.float32)
        src = jax.random.randint(k_s, (N_EDGES,), 0, N_NODES, dtype=jnp.int32)
        dst = jax.random.randint(k_d, (N_EDGES,), 0, N_NODES, dtype=jnp.int32)
        W = jax.random.normal(k_w, (IN_FEATS, OUT_FEATS), dtype=jnp.float32) / np.sqrt(IN_FEATS)
        b = jax.random.normal(k_b, (OUT_FEATS,), dtype=jnp.float32) * 0.01
        return {'x': x, 'src': src, 'dst': dst, 'W': W, 'b': b}
    _L2_gnn_all = _L2_gnn_setup()
    _L2_gnn_in = {k: v for k, v in _L2_gnn_all.items() if k in ('W', 'b')}
    del _L2_gnn_all

    def _L3_gnn_setup():
        import jax, jax.numpy as jnp
        import numpy as np
        N_NODES = 6250
        N_EDGES = 75000
        DIM = 128
        key = jax.random.key(seed)
        ks = jax.random.split(key, 8)
        node_feats = jax.random.normal(ks[0], (N_NODES, DIM), dtype=jnp.float32)
        edge_src = jax.random.randint(ks[1], (N_EDGES,), 0, N_NODES, dtype=jnp.int64)
        edge_dst = jax.random.randint(ks[2], (N_EDGES,), 0, N_NODES, dtype=jnp.int64)
        sc = 1.0 / np.sqrt(DIM)
        W_self = jax.random.normal(ks[3], (DIM, DIM), dtype=jnp.float32) * sc
        b_self = jax.random.normal(ks[4], (DIM,), dtype=jnp.float32) * sc
        W_neigh = jax.random.normal(ks[5], (DIM, DIM), dtype=jnp.float32) * sc
        b_neigh = jax.random.normal(ks[6], (DIM,), dtype=jnp.float32) * sc
        return {'node_feats': node_feats, 'edge_src': edge_src, 'edge_dst': edge_dst, 'W_self': W_self, 'b_self': b_self, 'W_neigh': W_neigh, 'b_neigh': b_neigh}
    _L3_gnn_all = _L3_gnn_setup()
    _L3_gnn_in = {k: v for k, v in _L3_gnn_all.items() if k in ('W_self', 'b_self', 'W_neigh', 'b_neigh')}
    del _L3_gnn_all
    return {'x': x, 'src': src, 'dst': dst, 'edge_type_8': edge_type_8, 'L0_gnn_node_proj_w': _L0_gnn_in['node_proj_w'], 'L0_gnn_node_proj_b': _L0_gnn_in['node_proj_b'], 'L0_gnn_edge_W': _L0_gnn_in['edge_W'], 'L0_gnn_edge_b': _L0_gnn_in['edge_b'], 'L0_gnn_gru_wih': _L0_gnn_in['gru_wih'], 'L0_gnn_gru_whh': _L0_gnn_in['gru_whh'], 'L0_gnn_gru_bih': _L0_gnn_in['gru_bih'], 'L0_gnn_gru_bhh': _L0_gnn_in['gru_bhh'], 'L0_gnn_out_w': _L0_gnn_in['out_w'], 'L0_gnn_out_b': _L0_gnn_in['out_b'], 'L1_gnn_W_pre': _L1_gnn_in['W_pre'], 'L1_gnn_b_pre': _L1_gnn_in['b_pre'], 'L1_gnn_W_post': _L1_gnn_in['W_post'], 'L1_gnn_b_post': _L1_gnn_in['b_post'], 'L1_gnn_W_lin': _L1_gnn_in['W_lin'], 'L1_gnn_b_lin': _L1_gnn_in['b_lin'], 'L2_gnn_W': _L2_gnn_in['W'], 'L2_gnn_b': _L2_gnn_in['b'], 'L3_gnn_W_self': _L3_gnn_in['W_self'], 'L3_gnn_b_self': _L3_gnn_in['b_self'], 'L3_gnn_W_neigh': _L3_gnn_in['W_neigh'], 'L3_gnn_b_neigh': _L3_gnn_in['b_neigh']}

def reference(x, src, dst, edge_type_8, L0_gnn_node_proj_w, L0_gnn_node_proj_b, L0_gnn_edge_W, L0_gnn_edge_b, L0_gnn_gru_wih, L0_gnn_gru_whh, L0_gnn_gru_bih, L0_gnn_gru_bhh, L0_gnn_out_w, L0_gnn_out_b, L1_gnn_W_pre, L1_gnn_b_pre, L1_gnn_W_post, L1_gnn_b_post, L1_gnn_W_lin, L1_gnn_b_lin, L2_gnn_W, L2_gnn_b, L3_gnn_W_self, L3_gnn_b_self, L3_gnn_W_neigh, L3_gnn_b_neigh):
    import jax
    import jax.numpy as jnp

    def _L0_gnn_ref(node_features, edge_index, edge_type, node_proj_w, node_proj_b, edge_W, edge_b, gru_wih, gru_whh, gru_bih, gru_bhh, out_w, out_b):
        import jax, jax.numpy as jnp
        import numpy as np
        N_NODES = 12500
        N_EDGES = 75000
        H = 128
        T = 8
        L = 2

        def _gru_cell(x, h, wih, whh, bih, bhh):
            gi = x @ wih.T + bih
            gh = h @ whh.T + bhh
            i_r, i_z, i_n = jnp.split(gi, 3, axis=-1)
            h_r, h_z, h_n = jnp.split(gh, 3, axis=-1)
            r = jax.nn.sigmoid(i_r + h_r)
            z = jax.nn.sigmoid(i_z + h_z)
            n = jnp.tanh(i_n + r * h_n)
            return (1.0 - z) * n + z * h
        num_nodes = node_features.shape[0]
        src, dst = (edge_index[0], edge_index[1])
        h = jax.nn.relu(node_features @ node_proj_w.T + node_proj_b)
        for l in range(L):
            trans = jnp.einsum('nh,tdh->tnd', h, edge_W[l])
            msgs = trans[edge_type, src]
            agg = jax.ops.segment_sum(msgs, dst, num_segments=num_nodes)
            h = _gru_cell(agg, h, gru_wih[l], gru_whh[l], gru_bih[l], gru_bhh[l])
            h = jax.nn.relu(h)
        return h @ out_w.T + out_b

    def _L1_gnn_ref(x, edge_index, W_pre, b_pre, W_post, b_post, W_lin, b_lin):
        import jax, jax.numpy as jnp
        import numpy as np
        N, E, F = (6250, 100000, 128)
        DELTA = 1.0
        EPS = 1e-05

        def _pna_forward(x, edge_index, W_pre, b_pre, W_post, b_post, W_lin, b_lin):
            src, dst = (edge_index[0], edge_index[1])
            n = x.shape[0]
            h = jnp.concatenate([x[dst], x[src]], axis=-1)
            m = h @ W_pre.T + b_pre
            deg = jax.ops.segment_sum(jnp.ones((m.shape[0],), m.dtype), dst, num_segments=n)
            deg_c = jnp.maximum(deg, 1.0)[:, None]
            has_edge = (deg > 0)[:, None]
            mx = jax.ops.segment_max(m, dst, num_segments=n)
            mx = jnp.where(has_edge, mx, 0.0)
            mn = jax.ops.segment_min(m, dst, num_segments=n)
            mn = jnp.where(has_edge, mn, 0.0)
            s1 = jax.ops.segment_sum(m, dst, num_segments=n)
            s2 = jax.ops.segment_sum(m * m, dst, num_segments=n)
            mean = s1 / deg_c
            var = s2 / deg_c - mean * mean
            std = jnp.sqrt(jax.nn.relu(var) + EPS)
            agg = jnp.concatenate([mx, mn, mean, std], axis=-1)
            log_deg = jnp.log(deg_c + 1.0)
            amp = log_deg / DELTA
            att = DELTA / log_deg
            scaled = jnp.concatenate([agg, agg * amp, agg * att], axis=-1)
            out = jnp.concatenate([x, scaled], axis=-1) @ W_post.T + b_post
            return out @ W_lin.T + b_lin
        return _pna_forward(x, edge_index, W_pre, b_pre, W_post, b_post, W_lin, b_lin)

    def _L2_gnn_ref(x, src, dst, W, b):
        import jax, jax.numpy as jnp
        import numpy as np
        N_NODES = 6250
        N_EDGES = 100000
        IN_FEATS = 128
        OUT_FEATS = 128
        n = x.shape[0]
        msg = x[src]
        summed = jax.ops.segment_sum(msg, dst, num_segments=n)
        deg = jax.ops.segment_sum(jnp.ones((src.shape[0],), x.dtype), dst, num_segments=n)
        h = summed / jnp.maximum(deg, 1.0)[:, None]
        return h @ W + b

    def _L3_gnn_ref(node_feats, edge_src, edge_dst, W_self, b_self, W_neigh, b_neigh):
        import jax, jax.numpy as jnp
        import numpy as np
        N_NODES = 6250
        N_EDGES = 75000
        DIM = 128
        N = node_feats.shape[0]
        gathered = node_feats[edge_src]
        neigh_sum = jax.ops.segment_sum(gathered, edge_dst, num_segments=N)
        deg = jax.ops.segment_sum(jnp.ones_like(edge_dst, dtype=node_feats.dtype), edge_dst, num_segments=N)
        neigh_mean = neigh_sum / jnp.maximum(deg, 1.0)[:, None]
        out = node_feats @ W_self.T + b_self + (neigh_mean @ W_neigh.T + b_neigh)
        return jax.nn.relu(out)
    edge_index = jnp.stack([src, dst])
    h = jnp.maximum(_layernorm(x, axis=-1), 0.0)
    x = x + _L0_gnn_ref(h, edge_index, edge_type_8, L0_gnn_node_proj_w, L0_gnn_node_proj_b, L0_gnn_edge_W, L0_gnn_edge_b, L0_gnn_gru_wih, L0_gnn_gru_whh, L0_gnn_gru_bih, L0_gnn_gru_bhh, L0_gnn_out_w, L0_gnn_out_b)
    h = jnp.maximum(_layernorm(x, axis=-1), 0.0)
    x = x + _L1_gnn_ref(h, edge_index, L1_gnn_W_pre, L1_gnn_b_pre, L1_gnn_W_post, L1_gnn_b_post, L1_gnn_W_lin, L1_gnn_b_lin)
    h = jnp.maximum(_layernorm(x, axis=-1), 0.0)
    x = x + _L2_gnn_ref(h, src, dst, L2_gnn_W, L2_gnn_b)
    h = jnp.maximum(_layernorm(x, axis=-1), 0.0)
    x = x + _L3_gnn_ref(h, src, dst, L3_gnn_W_self, L3_gnn_b_self, L3_gnn_W_neigh, L3_gnn_b_neigh)
    return x

_drawn_inputs = setup_inputs


def setup_inputs(seed=0):
    import zlib

    import numpy as np

    out = dict(_drawn_inputs(seed))
    spreads = {'L0_gnn_out_b': (0.0, 0.1),
     'L1_gnn_b_pre': (0.0, 0.1),
     'L1_gnn_b_post': (0.0, 0.1),
     'L1_gnn_b_lin': (0.0, 0.1)}
    factors = {'L0_gnn_node_proj_b': 5.989,
     'L0_gnn_gru_whh': 3.759,
     'L0_gnn_gru_bih': 5.635,
     'L0_gnn_gru_bhh': 8.0,
     'L2_gnn_b': 8.0}
    for name, (base, spread) in spreads.items():
        noise = np.random.default_rng([zlib.crc32(name.encode()), seed]).standard_normal(out[name].shape)
        drawn = base * np.exp(spread * noise) if base else spread * noise
        out[name] = jnp.asarray(drawn.astype(out[name].dtype))
    for name, factor in factors.items():
        out[name] = (out[name] * factor).astype(out[name].dtype)
    return out
```

```python
import numpy as np
import concourse.bass as bass
from concourse import mybir
from contextlib import ExitStack

F32 = mybir.dt.float32
I32 = mybir.dt.int32
ALU = mybir.AluOpType
ACT = mybir.ActivationFunctionType
AX = mybir.AxisListType

P = 128
D = 128
N = 6250
E = 100000
T = 8
NT = -(-N // P)
TAIL = N - (NT - 1) * P
GT = 7
NG = NT // GT
GC = GT * D
HC = GC // 2
STEPS = 784
LAST = E - (P - 1) * STEPS
K = 8
ITERS = STEPS // (2 * K)
NO_NODE = NT * P
BIG = 3.0e38
EPS = 1e-5
SEM_DMA = 16
TS = 4
assert NG * GT == NT and ITERS * 2 * K == STEPS and 0 < LAST <= STEPS

W_PROJ, W_EDGE, W_IH, W_HH, W_OUT, W_SRC, W_DST, W_X, W_LIN, W_SELF, W_NEIGH, W_SLOTS = (
    0, 1, 17, 23, 29, 30, 31, 32, 33, 34, 35, 36)

ROUNDS = [("typed", False), ("typed", False), ("node", True), ("node", False), ("node", False)]


def gnn_kernel(nc, a, out):
    table_typed = nc.dram_tensor("table_typed", (NT * P * T, D), F32, kind="Internal").ap()
    table_node = nc.dram_tensor("table_node", (NT * P, D), F32, kind="Internal").ap()
    history = nc.dram_tensor("history", (P * STEPS, D), F32, kind="Internal").ap()
    history4 = nc.dram_tensor("history4", (P * STEPS, 4 * D), F32, kind="Internal").ap()
    dst_rows = nc.dram_tensor("dst_rows", (P, STEPS), F32, kind="Internal").ap()
    typed_tiles = table_typed.rearrange("(t p e) d -> p t (e d)", p=P, e=T)
    node_tiles = table_node.rearrange("(t p) d -> p t d", p=P)
    x_in = a["x"]

    ctx = ExitStack()
    with ctx:
        ctx.enter_context(nc.allow_non_contiguous_dma(reason="bias columns, 4 bytes a partition"))

        def sb(name, shape, dt=F32):
            return ctx.enter_context(nc.sbuf_tensor(name, shape, dt))

        def sem(name):
            return ctx.enter_context(nc.semaphore(name))

        def sems(phase, *names):
            return {n: sem(f"{phase}_{n}") for n in names}

        x = sb("x_res", [P, NT, D])
        hT = sb("hT", [P, NT * P])
        node_term = hT[:, :].rearrange("p (t d) -> p t d", t=NT)
        rows = sb("rows", [P, 2 * GT * 4 * D])
        rows1 = rows[:, 0:NT * D].rearrange("p (t d) -> p t d", t=NT)
        rows4 = rows[:, :].rearrange("p (h t c d) -> p h t c d", h=2, t=GT, c=4)
        near = rows[:, 0:GT * STEPS].rearrange("p (t s) -> p t s", t=GT)
        fetched = sb("fetched", [P, 2 * K * 2 * D])
        fetched1 = fetched[:, 0:2 * K * D].rearrange("p (h k d) -> p h k d", h=2, k=K)
        fetched2 = fetched[:, :].rearrange("p (h k c d) -> p h k c d", h=2, k=K, c=2)
        gates = fetched[:, 0:8 * HC].rearrange("p (h g c) -> p h g c", h=2, g=4)
        hist = sb("hist", [P, 2 * K * 4 * D])
        hist1 = hist[:, 0:2 * K * D].rearrange("p (h k d) -> p h k d", h=2, k=K)
        hist4 = hist[:, :].rearrange("p (h k c d) -> p h k c d", h=2, k=K, c=4)
        wnat = hist[:, 0:W_SLOTS * D].rearrange("p (s d) -> p s d", s=W_SLOTS)
        hn = hist[:, 0:2 * GC].rearrange("p (h t d) -> p h t d", h=2, t=GT)
        aT = hist[:, 2 * GC:4 * GC].rearrange("p (h c) -> p h c", h=2)
        tstage = hist[:, 4 * GC:4 * GC + TS * T * D].rearrange("p (h c) -> p h c", h=TS)
        bT = hist[:, 4 * GC:6 * GC].rearrange("p (h c) -> p h c", h=2)
        bstage = hist[:, 6 * GC:8 * GC].rearrange("p (h t d) -> p h t d", h=2, t=GT)
        tmpA = hist[:, 4 * GC:5 * GC].rearrange("p (t d) -> p t d", t=GT)
        tmpB = hist[:, 5 * GC:6 * GC].rearrange("p (t d) -> p t d", t=GT)
        wpost = hT[:, 0:13 * D].rearrange("p (c i) -> p c i", c=13)
        wT = sb("wT", [P, W_SLOTS, D])
        wcomb = sb("wcomb", [P, 4, 3, D])
        l2w = sb("l2w", [P, D])
        proj_b = sb("proj_b", [P, 1])
        b_ih = sb("b_ih", [P, 6])
        b_hh = sb("b_hh", [P, 6])
        b_rz = sb("b_rz", [P, 6])
        post_b = sb("post_b", [P, 1])
        post_bb = sb("post_bb", [P, D])
        bias_rows = sb("bias_rows", [P, 6, D])
        OUT_B, PRE_B, LIN_B, L2_B, SELF_B, NEIGH_B = range(6)
        ident = sb("ident", [P, P])
        ones = sb("ones", [P, P])
        prev_lane = sb("prev_lane", [P, P])
        next_lane = sb("next_lane", [P, P])
        corner = sb("corner", [P, P])
        idx_src = sb("idx_src", [P, STEPS + 2 * K], I32)
        idx_typ = sb("idx_typ", [P, STEPS + 2 * K], I32)
        masks = sb("masks", [P, STEPS, 2])
        idx_now = sb("idx_now", [P, 2, K], I32)
        mask_now = sb("mask_now", [P, 2, K, 2])
        dst_i = fetched[:, 0:STEPS].bitcast(I32)
        dstf = fetched[:, STEPS:2 * STEPS]
        e_tmp = fetched[:, 2 * STEPS:3 * STEPS]
        e_tmp2 = fetched[:, 3 * STEPS:4 * STEPS]
        node_i = sb("node_i", [P, NT], I32)
        node_f = sb("node_f", [P, NT])
        lane_i = sb("lane_i", [P, 1], I32)
        lane_f = sb("lane_f", [P, 1])
        heads = sb("heads", [P, P])
        diag = sb("diag", [P, P])
        g_mul = sb("g_mul", [P, P])
        g_max = sb("g_max", [P, P])
        g_min = sb("g_min", [P, P])
        col = sb("col", [P, 12])
        C_CNT, C_WHOLE, C_LAST1, C_HEAD1, C_CONT, C_CONTM, C_G, C_FE, C_FE1 = range(9)
        first_end = sb("first_end", [P, 1], I32)
        near_row = sb("near_row", [P, NT], I32)
        near_f = sb("near_f", [P, NT])
        near_cnt = sb("near_cnt", [P, NT])
        starts = sb("starts", [P, NT + 1])
        ends = sb("ends", [P, NT])
        end_f = sb("end_f", [P, NT])
        end_row = sb("end_row", [P, NT], I32)
        deg = sb("deg", [P, NT])
        has = sb("has", [P, NT])
        degc = sb("degc", [P, NT])
        deg1 = sb("deg1", [P, NT])
        rdeg = sb("rdeg", [P, NT])
        amp = sb("amp", [P, NT])
        att = sb("att", [P, NT])
        bn6 = sb("bn6", [P, GT, 6])
        mv = sb("mv", [P, GT, 2])
        var_e = sb("var_e", [P, GT])
        std_l = sb("std_l", [P, GT])
        rstd = sb("rstd", [P, 2, GT])
        nmr = sb("nmr", [P, 2, GT])
        mend = sb("mend", [P, 4, D])
        scan = sb("scan", [P, 4, P + 1])
        aggT4 = sb("aggT4", [P, 2, 4 * D])

        def ps(name, banks):
            return ctx.enter_context(nc.psum_tensor(name, [P, banks * 512], F32))

        pT = ps("pT", 2)
        pO = ps("pO", 2)
        pG = ps("pG", 4)

        s_clear = sem("s_clear")
        s_edges = sem("s_edges")
        s_x = sem("s_x")
        s_w = sem("s_w")
        s_const = sem("s_const")
        s_pc = sem("s_pc")
        s_dstf = sem("s_dstf")
        s_dstd = sem("s_dstd")
        s_wtr = sem("s_wtr")
        s_wcp = sem("s_wcp")
        s_wc = sem("s_wc")
        s_bpost = sem("s_bpost")
        s_wready = sem("s_wready")
        s_lane = sem("s_lane")
        s_lanep = sem("s_lanep")
        s_nearix = sem("s_nearix")
        s_near = [sem(f"s_near{j}") for j in range(GT)]
        s_near_used = sem("s_near_used")
        s_starts = sem("s_starts")
        s_ends = sem("s_ends")
        s_degs = sem("s_degs")
        s_log = sem("s_log")
        s_nodes = sem("s_nodes")
        s_v = sem("s_v")
        s_rows = [sem(f"s_rows{g}") for g in range(NG)]
        s_rows4 = [sem(f"s_rows4_{h}") for h in range(2)]
        s_out = sem("s_out")
        R = dict(
            fetched=[sem(f"fetched{h}") for h in range(2)],
            staged=sem("staged"),
            state=sem("state"),
            saved=[sem(f"saved{h}") for h in range(2)],
            squared=sem("squared"), go=sem("go"),
            tails=sem("tails"), scanned=sem("scanned"), carries=sem("carries"),
            mend_in=sem("mend_in"), mended=sem("mended"), mend_out=sem("mend_out"),
        )

        def state_per_batch(r):
            return 1 + K * (3 if ROUNDS[r][1] else 1)

        BASE = [dict(
            fetched=r * ITERS * K * SEM_DMA, staged=r * (2 * ITERS + 2), saved=r * ITERS * SEM_DMA,
            state=sum(2 * ITERS * state_per_batch(q) for q in range(r)),
            once=r, dma=r * SEM_DMA,
        ) for r in range(len(ROUNDS))]
        LN = ("var", "std", "norm", "hn")
        TR = ("mm0", "mm1", "ev0", "ev1", "tb0", "tb1", "tb2", "tb3")
        GRU = ("agg", "tr", "cp", "gate", "rz", "hadd", "tanh", "hnew")
        A = sems("A", *LN, *TR, "tr", "cp", "proj", "h")
        B = sems("B", *GRU, *TR)
        C = sems("C", *GRU, *LN, "om", "xo", "tr2", "cp2", "bac", "bev", "aev", "tn0", "tn1")
        Dp = sems("D", *LN, "agg", "pre", "std4", "tr", "cp", "fm", "xo", "rfree", "tn0", "tn1")
        Ep = sems("E", *LN, "agg", "tr", "cp", "om", "xo", "tr2", "cp2", "sm", "sev", "tn0", "tn1")
        Fp = sems("F", "agg", "tr", "cp", "om", "fin")

        block = ctx.enter_context(nc.Block())

        def wait_table(eng, r):
            if ROUNDS[r][0] == "typed":
                ph = (A, B)[r]
                for k in range(TS):
                    eng.wait_ge(ph[f"tb{k}"], SEM_DMA * len(range(k, NT, TS)))
            else:
                ph = (C, Dp, Ep)[r - 2]
                for k in range(2):
                    eng.wait_ge(ph[f"tn{k}"], SEM_DMA * len(range(k, NG, 2)))

        def bc(colap):
            return colap.unsqueeze(2).to_broadcast([P, GT, D])

        def rowbc(i):
            return bias_rows[:, i:i + 1, :].to_broadcast([P, GT, D])

        def tiles(g):
            return x[:, g * GT:(g + 1) * GT, :]

        @block.sync
        def _(sp):
            sp.wait_ge(s_clear, 4)
            for name, tile in (("dst", dst_i), ("src", idx_src), ("edge_type_8", idx_typ)):
                sp.dma_start(tile[0:P - 1, 0:STEPS],
                             a[name][0:(P - 1) * STEPS].rearrange("(p s) -> p s", s=STEPS)).then_inc(s_edges, SEM_DMA)
                sp.dma_start(tile[P - 1:P, 0:LAST],
                             a[name][(P - 1) * STEPS:E].rearrange("(p s) -> p s", p=1)).then_inc(s_edges, SEM_DMA)
            sp.dma_start(x[:, 0:NT - 1, :], x_in[0:(NT - 1) * P, :].rearrange("(t p) d -> p t d", p=P)).then_inc(s_x, SEM_DMA)
            sp.dma_start(x[0:TAIL, NT - 1, :], x_in[(NT - 1) * P:N, :]).then_inc(s_x, SEM_DMA)
            sp.wait_ge(s_dstf, 1)
            sp.dma_start(dst_rows, dstf).then_inc(s_dstd, SEM_DMA)

            def store_typed(ph, g):
                for j in range(GT):
                    t = g * GT + j
                    sp.wait_ge(ph["ev0"], t + 1)
                    sp.wait_ge(ph["ev1"], t + 1)
                    sp.dma_start(typed_tiles[:, t, :], tstage[:, t % TS, :]).then_inc(ph[f"tb{t % TS}"], SEM_DMA)

            def save_history(r):
                h4 = ROUNDS[r][1]
                view = (history4 if h4 else history).rearrange("(p s) w -> p s w", p=P)
                per = state_per_batch(r)
                with sp.Fori(0, ITERS) as it:
                    for h in range(2):
                        sp.wait_ge(R["state"], it * (2 * per) + (BASE[r]["state"] + (h + 1) * per))
                        src = hist4[:, h].rearrange("p k c d -> p k (c d)") if h4 else hist1[:, h]
                        sp.dma_start(view[:, bass.ds(it * (2 * K) + h * K, K), :], src).then_inc(R["saved"][h], SEM_DMA)

            def store_node(ph, g, ready, src):
                sp.wait_ge(ready[0], ready[1])
                sp.dma_start(node_tiles[:, g * GT:(g + 1) * GT, :], src).then_inc(ph[f"tn{g % 2}"], SEM_DMA)

            for g in range(NG):
                store_typed(A, g)
            save_history(0)
            for g in range(NG):
                store_typed(B, g)
            save_history(1)
            for g in range(NG):
                store_node(C, g, (C["bev"], GT * (g + 1)), bstage[:, g % 2])
            save_history(2)
            for g in range(NG):
                store_node(Dp, g, (Dp["hn"], g + 1), hn[:, g % 2])
            save_history(3)
            for g in range(NG):
                store_node(Ep, g, (Ep["hn"], g + 1), hn[:, g % 2])
            save_history(4)
            for g in range(NG):
                sp.wait_ge(Fp["fin"], g + 1)
                full = min((g + 1) * GT, NT - 1)
                sp.dma_start(out[g * GT * P:full * P, :].rearrange("(t p) d -> p t d", p=P),
                             x[:, g * GT:full, :]).then_inc(s_out, SEM_DMA)
            sp.dma_start(out[(NT - 1) * P:N, :], x[0:TAIL, NT - 1, :]).then_inc(s_out, SEM_DMA)
            sp.wait_ge(s_out, SEM_DMA * (NG + 1))

        @block.gpsimd
        def _(pool):
            nc.gpsimd.iota(node_i[:, :], pattern=[[P, NT]], base=0, channel_multiplier=1)
            nc.gpsimd.iota(lane_i[:, :], pattern=[[0, 1]], base=0, channel_multiplier=1)
            nc.gpsimd.memset(ones[:, :], 1.0)
            nc.gpsimd.memset(scan[:, :, 0:1], 0.0).then_inc(s_const, 1)
            for n, (m, base, step) in enumerate(((ident, 0, 1), (prev_lane, 1, 1), (next_lane, -1, 1), (corner, P - 1, P))):
                nc.gpsimd.memset(m[:, :], 0.0).then_inc(s_pc, 1)
                pool.wait_ge(s_pc, n + 1)
                nc.gpsimd.affine_select(out=m[:, :], in_=m[:, :], compare_op=ALU.not_equal, fill=1.0,
                                        base=base, pattern=[[-1, P]], channel_multiplier=step).then_inc(s_const, 1)
            pool.wait_ge(s_dstd, SEM_DMA)
            pool.wait_ge(s_nearix, 1)
            for t in range(NT):
                if t >= GT:
                    pool.wait_ge(s_near_used, t - GT + 1)
                pool.indirect_dma_start(near[:, t % GT, :], None, dst_rows,
                                        bass.IndirectOffsetOnAxis(ap=near_row[:, t:t + 1], axis=0)
                                        ).then_inc(s_near[t % GT], SEM_DMA)

            def gather_round(r):
                wait_table(pool, r)
                table = table_typed if ROUNDS[r][0] == "typed" else table_node
                with pool.Fori(0, ITERS) as it:
                    for h in range(2):
                        pool.wait_ge(R["staged"], it * 2 + (BASE[r]["staged"] + h + 1))
                        pool.sem_inc(R["go"], 1)
                        for k in range(K):
                            dest = fetched2[:, h, k, 0, :] if ROUNDS[r][1] else fetched1[:, h, k, :]
                            pool.indirect_dma_start(dest, None, table,
                                                    bass.IndirectOffsetOnAxis(ap=idx_now[:, h, k:k + 1], axis=0)
                                                    ).then_inc(R["fetched"][h], SEM_DMA)
                hd = history4 if ROUNDS[r][1] else history
                w = 4 * D if ROUNDS[r][1] else D
                m = mend[:, :, :].rearrange("p c d -> p (c d)")[:, 0:w]
                for h in range(2):
                    pool.wait_ge(R["saved"][h], BASE[r]["saved"] + SEM_DMA * ITERS)
                pool.indirect_dma_start(m, None, hd, bass.IndirectOffsetOnAxis(ap=first_end[:, 0:1], axis=0)
                                        ).then_inc(R["mend_in"], SEM_DMA)
                pool.wait_ge(R["mended"], BASE[r]["once"] + 1)
                pool.indirect_dma_start(hd, bass.IndirectOffsetOnAxis(ap=first_end[:, 0:1], axis=0), m, None
                                        ).then_inc(R["mend_out"], SEM_DMA)
                pool.wait_ge(R["mend_out"], BASE[r]["dma"] + SEM_DMA)

            def gather_nodes(r):
                for t in range(NT):
                    pool.indirect_dma_start(rows1[:, t, :], None, history,
                                            bass.IndirectOffsetOnAxis(ap=end_row[:, t:t + 1], axis=0)
                                            ).then_inc(s_rows[t // GT], SEM_DMA)

            gather_round(0)
            pool.wait_ge(s_nodes, 1)
            gather_nodes(0)
            gather_round(1)
            gather_nodes(1)
            gather_round(2)
            for t in range(NT):
                g = t // GT
                if g >= 2 and t % GT == 0:
                    pool.wait_ge(Dp["rfree"], g - 1)
                pool.indirect_dma_start(rows4[:, g % 2, t % GT].rearrange("p c d -> p (c d)"), None, history4,
                                        bass.IndirectOffsetOnAxis(ap=end_row[:, t:t + 1], axis=0)
                                        ).then_inc(s_rows4[g % 2], SEM_DMA)
            gather_round(3)
            gather_nodes(3)
            gather_round(4)
            gather_nodes(4)

        @block.scalar
        def _(act):
            def load(dst, src):
                act.dma_start(dst, src).then_inc(s_w, SEM_DMA)

            load(wnat[:, W_PROJ, :], a["L0_gnn_node_proj_w"])
            load(wnat[:, W_EDGE:W_IH, :], a["L0_gnn_edge_W"].rearrange("l t d h -> d (l t) h"))
            load(wnat[:, W_IH:W_HH, :], a["L0_gnn_gru_wih"].rearrange("l (c o) h -> o (l c) h", c=3))
            load(wnat[:, W_HH:W_OUT, :], a["L0_gnn_gru_whh"].rearrange("l (c o) h -> o (l c) h", c=3))
            load(wnat[:, W_OUT, :], a["L0_gnn_out_w"])
            load(wnat[:, W_SRC, :], a["L1_gnn_W_pre"][:, D:2 * D])
            load(wnat[:, W_DST, :], a["L1_gnn_W_pre"][:, 0:D])
            load(wnat[:, W_LIN, :], a["L1_gnn_W_lin"])
            load(wnat[:, W_SELF, :], a["L3_gnn_W_self"])
            load(wnat[:, W_NEIGH, :], a["L3_gnn_W_neigh"])
            load(wpost, a["L1_gnn_W_post"].rearrange("o (c i) -> o c i", c=13))
            load(l2w[:, :], a["L2_gnn_W"])
            load(proj_b[:, :], a["L0_gnn_node_proj_b"].rearrange("(o a) -> o a", a=1))
            load(post_b[:, :], a["L1_gnn_b_post"].rearrange("(o a) -> o a", a=1))
            load(b_ih[:, :], a["L0_gnn_gru_bih"].rearrange("l (c o) -> o (l c)", c=3))
            load(b_hh[:, :], a["L0_gnn_gru_bhh"].rearrange("l (c o) -> o (l c)", c=3))
            for i, n in enumerate(("L0_gnn_out_b", "L1_gnn_b_pre", "L1_gnn_b_lin", "L2_gnn_b", "L3_gnn_b_self", "L3_gnn_b_neigh")):
                load(bias_rows[:, i, :], a[n].rearrange("(o a) -> o a", o=1).to_broadcast([P, D]))

            def ln_norm(ph, g, stored):
                act.wait_ge(ph["var"], g + 1)
                if g >= 1:
                    act.wait_ge(ph["norm"], g)
                nc.scalar.activation(std_l[:, :], var_e[:, :], ACT.Sqrt).then_inc(ph["std"], 1)
                act.wait_ge(ph["norm"], g + 1)
                if g >= 2:
                    if "tr2" in ph:
                        act.wait_ge(ph["tr2"], g - 1)
                    elif not stored:
                        act.wait_ge(ph["tr"], g - 1)
                    if stored:
                        act.wait_ge(ph[f"tn{g % 2}"], SEM_DMA * (g // 2))
                for j in range(GT):
                    last = nc.scalar.activation(hn[:, g % 2, j, :], x[:, g * GT + j, :], ACT.Relu,
                                                bias=nmr[:, g % 2, j:j + 1], scale=rstd[:, g % 2, j:j + 1])
                last.then_inc(ph["hn"], 1)

            def copy_T(ph, tr, cp, g, dst):
                act.wait_ge(ph[tr], g + 1)
                nc.scalar.activation(dst[:, g % 2, :], pT[:, 0:GC], ACT.Copy).then_inc(ph[cp], 1)

            def evict_typed(ph, g):
                for j in range(GT):
                    t = g * GT + j
                    act.wait_ge(ph["mm0"], t + 1)
                    if t >= TS:
                        act.wait_ge(ph[f"tb{t % TS}"], SEM_DMA * (t // TS))
                    nc.scalar.activation(tstage[:, t % TS, 0:512], pO[:, 0:512], ACT.Copy).then_inc(ph["ev0"], 1)

            def gru(ph, layer, g):
                if g >= 2:
                    act.wait_ge(ph["gate"], 2 * (g - 1))
                copy_T(ph, "tr", "cp", g, aT)
                for h in range(2):
                    u = 2 * g + h
                    act.wait_ge(ph["gate"], u + 1)
                    if u >= 2:
                        act.wait_ge(ph["hnew"], u - 1)
                    nc.scalar.activation(gates[:, h, 0, :], pG[:, 0:HC], ACT.Sigmoid, bias=b_rz[:, 3 * layer:3 * layer + 1])
                    nc.scalar.activation(gates[:, h, 1, :], pG[:, 512:512 + HC], ACT.Sigmoid,
                                         bias=b_rz[:, 3 * layer + 1:3 * layer + 2]).then_inc(ph["rz"], 1)
                for h in range(2):
                    u = 2 * g + h
                    act.wait_ge(ph["hadd"], u + 1)
                    nc.scalar.activation(gates[:, h, 2, :], gates[:, h, 2, :], ACT.Tanh,
                                         bias=b_ih[:, 3 * layer + 2:3 * layer + 3]).then_inc(ph["tanh"], 1)

            def squares():
                with act.Fori(0, ITERS) as it:
                    for h in range(2):
                        act.wait_ge(R["fetched"][h], it * (K * SEM_DMA) + (BASE[2]["fetched"] + K * SEM_DMA))
                        nc.scalar.activation(fetched2[:, h, :, 1, :], fetched2[:, h, :, 0, :], ACT.Square
                                             ).then_inc(R["squared"], 1)

            for i in range(NG + 1):
                if i < NG:
                    ln_norm(A, i, False)
                    if i >= 2:
                        act.wait_ge(A["proj"], 2 * (i - 1))
                    copy_T(A, "tr", "cp", i, aT)
                    for h in range(2):
                        act.wait_ge(A["proj"], 2 * i + h + 1)
                        nc.scalar.activation(hT[:, i * GC + h * HC:i * GC + (h + 1) * HC], pG[:, h * 512:h * 512 + HC],
                                             ACT.Relu, bias=proj_b[:, 0:1]).then_inc(A["h"], 1)
                if i >= 1:
                    evict_typed(A, i - 1)
            act.wait_ge(s_degs, 1)
            nc.scalar.activation(amp[:, :], deg1[:, :], ACT.Ln).then_inc(s_log, 1)
            for i in range(NG + 1):
                if i < NG:
                    gru(B, 0, i)
                if i >= 1:
                    evict_typed(B, i - 1)
            for i in range(NG + 2):
                if i < NG:
                    gru(C, 1, i)
                if 1 <= i <= NG:
                    ln_norm(C, i - 1, False)
                if i >= 2:
                    g = i - 2
                    if g >= 2:
                        act.wait_ge(C["bac"], GT * (g - 1))
                    copy_T(C, "tr2", "cp2", g, bT)
                    if g >= 2:
                        act.wait_ge(C[f"tn{g % 2}"], SEM_DMA * (g // 2))
                    for j in range(GT):
                        act.wait_ge(C["bac"], g * GT + j + 1)
                        bank = ((g * GT + j) % 4) * 512
                        nc.scalar.activation(bstage[:, g % 2, j, :], pG[:, bank:bank + D], ACT.Copy
                                             ).then_inc(C["bev"], 1)
            squares()
            for i in range(NG + 1):
                if i < NG:
                    act.wait_ge(Dp["pre"], i + 1)
                    nc.scalar.activation(rows4[:, i % 2, :, 1, :], rows4[:, i % 2, :, 1, :], ACT.Sqrt).then_inc(Dp["std4"], 1)
                if i >= 1:
                    g = i - 1
                    for j in range(GT):
                        t = g * GT + j
                        act.wait_ge(Dp["tr"], t + 1)
                        if t >= 2:
                            act.wait_ge(Dp["fm"], t - 1)
                        nc.scalar.activation(aggT4[:, t % 2, :], pT[:, (t % 2) * 512:(t % 2) * 512 + 512], ACT.Copy
                                             ).then_inc(Dp["cp"], 1)
                    ln_norm(Dp, g, True)
            for i in range(NG + 1):
                if i < NG:
                    if i >= 2:
                        act.wait_ge(Ep["om"], i - 1)
                    copy_T(Ep, "tr", "cp", i, aT)
                    ln_norm(Ep, i, True)
                if i >= 1:
                    g = i - 1
                    if g >= 2:
                        act.wait_ge(Ep["sm"], g - 1)
                    copy_T(Ep, "tr2", "cp2", g, bT)
            for i in range(NG):
                if i >= 2:
                    act.wait_ge(Fp["om"], i - 1)
                copy_T(Fp, "tr", "cp", i, aT)

        @block.tensor
        def _(pe):
            mm = nc.tensor.matmul
            n_w = 22
            pe.wait_ge(s_const, 5)
            pe.wait_ge(s_lane, 1)
            mm(pO[:, 0:1], prev_lane[:, :], col[:, C_LAST1:C_LAST1 + 1], start=True, stop=True)
            mm(pO[:, 512:512 + P], ones[:, :], diag[:, :], start=True, stop=True).then_inc(s_lanep, 1)
            pe.wait_ge(s_lane, 2)
            mm(pO[:, 0:P], ones[:, :], diag[:, :], start=True, stop=True).then_inc(s_lanep, 1)
            pe.wait_ge(s_w, SEM_DMA * n_w)
            slots = [s for s in range(W_SLOTS) if s != W_X]
            for b in range(9):
                if b >= 4:
                    pe.wait_ge(s_wcp, b - 3)
                part = slots[4 * b:4 * b + 4]
                for n, s in enumerate(part):
                    last = nc.tensor.transpose(pG[:, (b % 4) * 512 + n * D:(b % 4) * 512 + n * D + D], wnat[:, s, :], ident[:, :])
                last.then_inc(s_wtr, 1)
            pe.wait_ge(s_wcp, 9)
            pe.wait_ge(s_bpost, 1)
            for c in range(12):
                mm(pG[:, (c // 4) * 512 + (c % 4) * D:(c // 4) * 512 + (c % 4) * D + D], wpost[:, 1 + c, :], wT[:, W_LIN, :],
                   start=True, stop=True)
            mm(pG[:, 3 * 512:3 * 512 + D], wpost[:, 0, :], wT[:, W_LIN, :], start=True, stop=True)
            mm(pG[:, 3 * 512 + D:3 * 512 + 2 * D], post_bb[:, :], wT[:, W_LIN, :], start=True, stop=True).then_inc(s_wc, 1)
            pe.wait_ge(s_wready, 1)

            def transposes(src, g):
                for j in range(GT):
                    last = nc.tensor.transpose(pT[:, j * D:(j + 1) * D], src(j), ident[:, :])
                return last

            def typed(ph, layer, g, ready):
                pe.wait_ge(ready, 2 * g + 2)
                w = wT[:, W_EDGE + T * layer:W_EDGE + T * (layer + 1), :].rearrange("p t d -> p (t d)")
                for j in range(GT):
                    t = g * GT + j
                    for b in range(2):
                        if t >= 1:
                            pe.wait_ge(ph[f"ev{b}"], t)
                        mm(pO[:, b * 512:(b + 1) * 512], hT[:, t * P:(t + 1) * P], w[:, b * 512:(b + 1) * 512],
                           start=True, stop=True).then_inc(ph[f"mm{b}"], 1)

            def gru(ph, layer, g, before=None):
                pe.wait_ge(ph["agg"], g + 1)
                if g >= 1:
                    pe.wait_ge(ph["cp"], g)
                transposes(lambda j: rows1[:, g * GT + j, :], g).then_inc(ph["tr"], 1)
                pe.wait_ge(ph["cp"], g + 1)
                ih, hh = W_IH + 3 * layer, W_HH + 3 * layer
                for h in range(2):
                    u = 2 * g + h
                    if u >= 1:
                        pe.wait_ge(ph["rz"], u)
                        pe.wait_ge(ph["hadd"], u)
                    ag = aT[:, g % 2, h * HC:(h + 1) * HC]
                    hh_in = hT[:, g * GC + h * HC:g * GC + (h + 1) * HC]
                    for c in range(2):
                        mm(pG[:, c * 512:c * 512 + HC], wT[:, ih + c, :], ag, start=True, stop=False)
                        mm(pG[:, c * 512:c * 512 + HC], wT[:, hh + c, :], hh_in, start=False, stop=True)
                    mm(pG[:, 2 * 512:2 * 512 + HC], wT[:, ih + 2, :], ag, start=True, stop=True)
                    mm(pG[:, 3 * 512:3 * 512 + HC], wT[:, hh + 2, :], hh_in, start=True, stop=True).then_inc(ph["gate"], 1)

            def carry(r):
                nb = 4 if ROUNDS[r][1] else 1
                pe.wait_ge(R["state"], BASE[r]["state"] + state_per_batch(r) * 2 * ITERS)
                for b in range(nb):
                    src = hist4[:, 1, K - 1, b, :] if nb == 4 else hist1[:, 1, K - 1, :]
                    last = nc.tensor.transpose(pT[:, b * D:(b + 1) * D], src, ident[:, :])
                last.then_inc(R["tails"], 1)
                pe.wait_ge(R["scanned"], BASE[r]["once"] + 1)
                for b in range(nb):
                    last = nc.tensor.transpose(pT[:, 512 + b * D:512 + (b + 1) * D], scan[:, b, 0:P], ident[:, :])
                last.then_inc(R["carries"], 1)

            for i in range(NG + 1):
                if i < NG:
                    pe.wait_ge(A["hn"], i + 1)
                    if i >= 1:
                        pe.wait_ge(A["cp"], i)
                    transposes(lambda j: hn[:, i % 2, j, :], i).then_inc(A["tr"], 1)
                    pe.wait_ge(A["cp"], i + 1)
                    for h in range(2):
                        if i >= 1:
                            pe.wait_ge(A["h"], 2 * (i - 1) + h + 1)
                        mm(pG[:, h * 512:h * 512 + HC], wT[:, W_PROJ, :], aT[:, i % 2, h * HC:(h + 1) * HC],
                           start=True, stop=True).then_inc(A["proj"], 1)
                if i >= 1:
                    typed(A, 0, i - 1, A["h"])
            pe.wait_ge(s_starts, 1)
            mm(pG[:, 0:NT], next_lane[:, :], starts[:, 0:NT], start=True, stop=False)
            mm(pG[:, 0:NT], corner[:, :], starts[:, 1:NT + 1], start=False, stop=True).then_inc(s_ends, 1)
            carry(0)
            for i in range(NG + 1):
                if i < NG:
                    gru(B, 0, i)
                if i >= 1:
                    typed(B, 1, i - 1, B["hnew"])
            carry(1)
            for i in range(NG + 2):
                if i < NG:
                    if i >= 3:
                        pe.wait_ge(C["cp2"], i - 2)
                        pe.wait_ge(C["bev"], GT * (i - 2))
                        pe.wait_ge(C["aev"], GT * (i - 2))
                    gru(C, 1, i)
                if 1 <= i <= NG:
                    g = i - 1
                    pe.wait_ge(C["hnew"], 2 * g + 2)
                    if g >= 1:
                        pe.wait_ge(C["xo"], g)
                    for j in range(GT):
                        last = mm(pO[:, j * D:(j + 1) * D], hT[:, (g * GT + j) * P:(g * GT + j + 1) * P], wT[:, W_OUT, :],
                                  start=True, stop=True)
                    last.then_inc(C["om"], 1)
                if i >= 2:
                    g = i - 2
                    pe.wait_ge(C["hn"], g + 1)
                    pe.wait_ge(C["cp"], min(i + 1, NG))
                    if g >= 1:
                        pe.wait_ge(C["cp2"], g)
                    transposes(lambda j: hn[:, g % 2, j, :], g).then_inc(C["tr2"], 1)
                    pe.wait_ge(C["cp2"], g + 1)
                    pe.wait_ge(C["rz"], 2 * min(i + 1, NG))
                    pe.wait_ge(C["hadd"], 2 * min(i + 1, NG))
                    for j in range(GT):
                        t = g * GT + j
                        if t >= 4:
                            pe.wait_ge(C["bev"], t - 3)
                            pe.wait_ge(C["aev"], t - 3)
                        mm(pG[:, (t % 4) * 512:(t % 4) * 512 + 3 * D], bT[:, g % 2, j * D:(j + 1) * D],
                           wT[:, W_SRC:W_X + 1, :].rearrange("p s d -> p (s d)"), start=True, stop=True).then_inc(C["bac"], 1)
            carry(2)

            def dtrans(t):
                g, j = divmod(t, GT)
                if j == 0:
                    pe.wait_ge(Dp["agg"], g + 1)
                    pe.wait_ge(Dp["std4"], g + 1)
                if t >= 2:
                    pe.wait_ge(Dp["cp"], t - 1)
                for n, c in enumerate((2, 3, 0, 1)):
                    last = nc.tensor.transpose(pT[:, (t % 2) * 512 + n * D:(t % 2) * 512 + (n + 1) * D],
                                               rows4[:, g % 2, j, c, :], ident[:, :])
                last.then_inc(Dp["tr"], 1)

            dtrans(0)
            for t in range(NT):
                if t + 1 < NT:
                    dtrans(t + 1)
                pe.wait_ge(Dp["cp"], t + 1)
                if t >= 4:
                    pe.wait_ge(Dp["xo"], t - 3)
                for c in range(4):
                    last = mm(pG[:, (t % 4) * 512:(t % 4) * 512 + 3 * D], aggT4[:, t % 2, c * D:(c + 1) * D],
                              wcomb[:, c].rearrange("p v d -> p (v d)"), start=(c == 0), stop=(c == 3))
                last.then_inc(Dp["fm"], 1)
            carry(3)
            for i in range(NG + 1):
                if i < NG:
                    pe.wait_ge(Ep["agg"], i + 1)
                    if i >= 1:
                        pe.wait_ge(Ep["cp"], i)
                    if i >= 2:
                        pe.wait_ge(Ep["cp2"], i - 1)
                    transposes(lambda j: rows1[:, i * GT + j, :], i).then_inc(Ep["tr"], 1)
                    pe.wait_ge(Ep["cp"], i + 1)
                    if i >= 1:
                        pe.wait_ge(Ep["xo"], i)
                    for j in range(GT):
                        last = mm(pO[:, j * D:(j + 1) * D], aT[:, i % 2, j * D:(j + 1) * D], l2w[:, :], start=True, stop=True)
                    last.then_inc(Ep["om"], 1)
                if i >= 1:
                    g = i - 1
                    pe.wait_ge(Ep["hn"], g + 1)
                    transposes(lambda j: hn[:, g % 2, j, :], g).then_inc(Ep["tr2"], 1)
                    pe.wait_ge(Ep["cp2"], g + 1)
                    if g >= 1:
                        pe.wait_ge(Ep["sev"], g)
                    for j in range(GT):
                        last = mm(pG[:, j * D:(j + 1) * D], bT[:, g % 2, j * D:(j + 1) * D], wT[:, W_SELF, :], start=True, stop=True)
                    last.then_inc(Ep["sm"], 1)
            carry(4)
            for i in range(NG):
                pe.wait_ge(Fp["agg"], i + 1)
                if i >= 1:
                    pe.wait_ge(Fp["cp"], i)
                transposes(lambda j: rows1[:, i * GT + j, :], i).then_inc(Fp["tr"], 1)
                pe.wait_ge(Fp["cp"], i + 1)
                if i >= 1:
                    pe.wait_ge(Fp["fin"], i)
                for j in range(GT):
                    last = mm(pO[:, j * D:(j + 1) * D], aT[:, i % 2, j * D:(j + 1) * D], wT[:, W_NEIGH, :], start=True, stop=True)
                last.then_inc(Fp["om"], 1)

        @block.vector
        def _(dve):
            v = nc.vector
            chain = [0]

            def link(ins):
                chain[0] += 1
                ins.then_inc(s_v, 1)
                dve.wait_ge(s_v, chain[0])

            v.memset(dst_i[:, :], NO_NODE).then_inc(s_clear, 1)
            v.memset(idx_src[:, :], 0).then_inc(s_clear, 1)
            v.memset(idx_typ[:, :], 0).then_inc(s_clear, 1)
            v.memset(x[:, NT - 1, :], 0.0).then_inc(s_clear, 1)
            v.memset(starts[:, NT:NT + 1], float(E))
            link(v.memset(masks[:, 0, 0:1], 0.0))
            dve.wait_ge(s_const, 1)
            v.tensor_copy(node_f[:, :], node_i[:, :])
            v.tensor_copy(lane_f[:, :], lane_i[:, :])
            dve.wait_ge(s_edges, 6 * SEM_DMA)
            chain[0] += 1
            v.tensor_copy(dstf, dst_i[:, :]).then_inc(s_v, 1)
            dve.wait_ge(s_v, chain[0])
            dve.sem_inc(s_dstf, 1)
            c = lambda n: col[:, n:n + 1]
            v.tensor_scalar(e_tmp, dstf, dstf[:, 0:1], None, ALU.is_equal, ALU.add, accum_out=c(C_CNT))
            v.tensor_scalar_add(c(C_LAST1), dstf[:, STEPS - 1:STEPS], 1.0)
            v.tensor_scalar_add(c(C_HEAD1), dstf[:, 0:1], 1.0)
            dve.wait_ge(s_const, 5)
            v.tensor_scalar(diag[:, :], ident[:, :], dstf[:, 0:1], None, ALU.mult).then_inc(s_lane, 1)
            link(v.tensor_tensor(masks[:, 1:STEPS, 0], dstf[:, 1:STEPS], dstf[:, 0:STEPS - 1], ALU.is_equal))
            v.tensor_scalar(masks[:, :, 1], masks[:, :, 0], -1.0, BIG, ALU.add, ALU.mult)
            v.tensor_copy(e_tmp, idx_src[:, 0:STEPS])
            link(v.tensor_copy(e_tmp2, idx_typ[:, 0:STEPS]))
            link(v.scalar_tensor_tensor(e_tmp2, e_tmp, float(T), e_tmp2, ALU.mult, ALU.add))
            v.tensor_copy(idx_typ[:, 0:STEPS], e_tmp2)
            v.tensor_scalar(c(C_WHOLE), c(C_CNT), float(STEPS), None, ALU.is_equal)
            link(v.scalar_tensor_tensor(c(C_FE), lane_f[:, :], float(STEPS), c(C_CNT), ALU.mult, ALU.add))
            link(v.tensor_scalar_add(c(C_FE1), c(C_FE), -1.0))
            v.tensor_copy(first_end[:, :], c(C_FE1))
            dve.wait_ge(s_lanep, 1)
            v.tensor_copy(heads[:, :], pO[:, 512:512 + P])
            link(v.tensor_tensor(c(C_CONT), pO[:, 0:1], c(C_HEAD1), ALU.is_equal))
            v.tensor_scalar(c(C_CONTM), c(C_CONT), -1.0, BIG, ALU.add, ALU.mult)
            link(v.tensor_tensor(c(C_G), c(C_CONT), c(C_WHOLE), ALU.mult))
            v.tensor_scalar(diag[:, :], ident[:, :], c(C_G), None, ALU.mult).then_inc(s_lane, 1)
            less = rows1
            link(v.tensor_tensor(less, heads[:, :].unsqueeze(1).to_broadcast([P, NT, P]),
                                 node_f[:, :].unsqueeze(2).to_broadcast([P, NT, P]), ALU.is_lt))
            link(v.tensor_reduce(near_cnt[:, :], less, AX.X, ALU.add))
            link(v.tensor_scalar(near_f[:, :], near_cnt[:, :], -1.0, 0.0, ALU.add, ALU.max))
            v.tensor_copy(near_row[:, :], near_f[:, :]).then_inc(s_nearix, 1)
            dve.wait_ge(s_lanep, 2)
            link(v.tensor_copy(g_mul[:, :], pO[:, 0:P]))
            v.tensor_scalar(g_max[:, :], g_mul[:, :], -1.0, BIG, ALU.add, ALU.mult)
            v.tensor_scalar(g_min[:, :], g_mul[:, :], -1.0, -BIG, ALU.add, ALU.mult)
            dve.wait_ge(s_w, 22 * SEM_DMA)
            v.tensor_copy(post_bb[:, :], post_b[:, 0:1].to_broadcast([P, D])).then_inc(s_bpost, 1)
            v.tensor_tensor(b_rz[:, :], b_ih[:, :], b_hh[:, :], ALU.add)
            v.tensor_tensor(bias_rows[:, SELF_B, :], bias_rows[:, SELF_B, :], bias_rows[:, NEIGH_B, :], ALU.add)
            for b in range(9):
                dve.wait_ge(s_wtr, b + 1)
                src = pG[:, (b % 4) * 512:(b % 4) * 512 + 4 * D].rearrange("p (s d) -> p s d", s=4)
                if b < 8:
                    v.tensor_copy(wT[:, 4 * b:4 * b + 4, :], src).then_inc(s_wcp, 1)
                else:
                    v.tensor_copy(wT[:, W_LIN:W_SLOTS, :], src[:, 0:3, :]).then_inc(s_wcp, 1)
            dve.wait_ge(s_wc, 1)
            for q in range(3):
                v.tensor_copy(wcomb[:, :, q, :], pG[:, q * 512:(q + 1) * 512].rearrange("p (c d) -> p c d", c=4))
            v.tensor_copy(wT[:, W_X, :], pG[:, 3 * 512:3 * 512 + D])
            v.tensor_tensor(bias_rows[:, LIN_B, :], bias_rows[:, LIN_B, :], pG[:, 3 * 512 + D:3 * 512 + 2 * D], ALU.add
                            ).then_inc(s_wready, 1)
            dve.wait_ge(s_x, 2 * SEM_DMA)

            def ln_stats(ph, g):
                for j in range(GT):
                    last = v.bn_stats(bn6[:, j, :], x[:, g * GT + j, :])
                link(last)
                for j in range(GT):
                    last = v.bn_aggr(mv[:, j, :], bn6[:, j, :])
                link(last)
                v.tensor_scalar_add(var_e[:, :], mv[:, :, 1], EPS).then_inc(ph["var"], 1)
                dve.wait_ge(ph["std"], g + 1)
                if g >= 2:
                    dve.wait_ge(ph["hn"], g - 1)
                link(v.reciprocal(rstd[:, g % 2, :], std_l[:, :]))
                v.scalar_tensor_tensor(nmr[:, g % 2, :], mv[:, :, 0], -1.0, rstd[:, g % 2, :], ALU.mult, ALU.mult
                                       ).then_inc(ph["norm"], 1)

            def evict_typed(ph, g):
                for j in range(GT):
                    t = g * GT + j
                    dve.wait_ge(ph["mm1"], t + 1)
                    if t >= TS:
                        dve.wait_ge(ph[f"tb{t % TS}"], SEM_DMA * (t // TS))
                    v.tensor_copy(tstage[:, t % TS, 512:1024], pO[:, 512:1024]).then_inc(ph["ev1"], 1)

            def count_starts(g):
                for j in range(GT):
                    t = g * GT + j
                    dve.wait_ge(s_near[j], SEM_DMA * (g + 1))
                    v.tensor_scalar(near[:, j, :], near[:, j, :], node_f[:, t:t + 1], None, ALU.is_lt, ALU.add,
                                    accum_out=near_cnt[:, t:t + 1]).then_inc(s_near_used, 1)

            def gru(ph, layer, g, rnd):
                dve.wait_ge(s_rows[g], GT * SEM_DMA * rnd)
                sl = rows1[:, g * GT:(g + 1) * GT, :]
                v.tensor_tensor(sl, sl, bc(has[:, g * GT:(g + 1) * GT]), ALU.mult).then_inc(ph["agg"], 1)
                for h in range(2):
                    u = 2 * g + h
                    dve.wait_ge(ph["rz"], u + 1)
                    link(v.scalar_tensor_tensor(gates[:, h, 2, :], pG[:, 3 * 512:3 * 512 + HC],
                                                b_hh[:, 3 * layer + 2:3 * layer + 3], gates[:, h, 0, :], ALU.add, ALU.mult))
                    v.tensor_tensor(gates[:, h, 2, :], gates[:, h, 2, :], pG[:, 2 * 512:2 * 512 + HC], ALU.add
                                    ).then_inc(ph["hadd"], 1)
                for h in range(2):
                    u = 2 * g + h
                    hs = hT[:, g * GC + h * HC:g * GC + (h + 1) * HC]
                    d = gates[:, h, 3, :]
                    dve.wait_ge(ph["tanh"], u + 1)
                    link(v.tensor_tensor(d, hs, gates[:, h, 2, :], ALU.subtract))
                    link(v.tensor_tensor(d, d, gates[:, h, 1, :], ALU.mult))
                    link(v.tensor_tensor(d, d, gates[:, h, 2, :], ALU.add))
                    v.tensor_scalar_max(hs, d, 0.0).then_inc(ph["hnew"], 1)

            def walk(r):
                s, at, many = R, BASE[r], ROUNDS[r][1]
                idx = idx_typ if ROUNDS[r][0] == "typed" else idx_src
                per = state_per_batch(r)
                wait_table(dve, r)
                if many:
                    first = hist4[:, 1, K - 1].rearrange("p c d -> p (c d)")
                else:
                    first = hist1[:, 1, K - 1, :]
                link(v.memset(first, 0.0))
                for h in range(2):
                    v.tensor_copy(idx_now[:, h, :], idx[:, h * K:(h + 1) * K]).then_inc(s["staged"], 1)

                def turn(it, again):
                    for h in range(2):
                        base = it * (2 * per) + (at["state"] + h * per)
                        v.tensor_copy(mask_now[:, h], masks[:, bass.ds(it * (2 * K) + h * K, K), :]).then_inc(s["state"], 1)
                        if many:
                            dve.wait_ge(s["squared"], it * 2 + h + 1)
                        else:
                            dve.wait_ge(s["fetched"][h], it * (K * SEM_DMA) + (at["fetched"] + K * SEM_DMA))
                        if again:
                            dve.wait_ge(s["saved"][h], it * SEM_DMA + at["saved"])
                        dve.wait_ge(s["state"], base + 1)
                        for k in range(K):
                            ph, pk = (h, k - 1) if k else (1 - h, K - 1)
                            keep, low = mask_now[:, h, k, 0:1], mask_now[:, h, k, 1:2]
                            if not many:
                                if k:
                                    dve.wait_ge(s["state"], base + 1 + k)
                                v.scalar_tensor_tensor(hist1[:, h, k, :], hist1[:, ph, pk, :], keep, fetched1[:, h, k, :],
                                                       ALU.mult, ALU.add).then_inc(s["state"], 1)
                                continue
                            if k:
                                dve.wait_ge(s["state"], base + 3 * k - 1)
                            v.scalar_tensor_tensor(hist4[:, h, k, 0:2, :], hist4[:, ph, pk, 0:2, :], keep, fetched2[:, h, k],
                                                   ALU.mult, ALU.add).then_inc(s["state"], 1)
                            if k:
                                dve.wait_ge(s["state"], base + 3 * k)
                            v.scalar_tensor_tensor(hist4[:, h, k, 2, :], hist4[:, ph, pk, 2, :], low, fetched2[:, h, k, 0, :],
                                                   ALU.add, ALU.max).then_inc(s["state"], 1)
                            if k:
                                dve.wait_ge(s["state"], base + 3 * k + 1)
                            v.scalar_tensor_tensor(hist4[:, h, k, 3, :], hist4[:, ph, pk, 3, :], low, fetched2[:, h, k, 0, :],
                                                   ALU.subtract, ALU.min).then_inc(s["state"], 1)
                        dve.wait_ge(s["state"], base + per)
                        v.tensor_copy(idx_now[:, h, :], idx[:, bass.ds(it * (2 * K) + (h + 2) * K, K)]).then_inc(s["staged"], 1)

                turn(0, False)
                with dve.Fori(1, ITERS) as it:
                    turn(it, True)

                nb = 4 if many else 1
                dve.wait_ge(s["tails"], at["once"] + 1)
                for b in range(nb):
                    mask, op0, op1 = ((g_mul, ALU.mult, ALU.add), (g_mul, ALU.mult, ALU.add),
                                      (g_max, ALU.add, ALU.max), (g_min, ALU.add, ALU.min))[b]
                    last = v.tensor_tensor_scan(scan[:, b, 1:P + 1], mask[:, :], pT[:, b * D:(b + 1) * D], 0.0, op0, op1)
                last.then_inc(s["scanned"], 1)
                dve.wait_ge(s["carries"], at["once"] + 1)
                dve.wait_ge(s["mend_in"], at["dma"] + SEM_DMA)
                for b in range(nb):
                    scal, op0, op1 = ((c(C_CONT), ALU.mult, ALU.add), (c(C_CONT), ALU.mult, ALU.add),
                                      (c(C_CONTM), ALU.add, ALU.max), (c(C_CONTM), ALU.subtract, ALU.min))[b]
                    last = v.scalar_tensor_tensor(mend[:, b, :], pT[:, 512 + b * D:512 + (b + 1) * D], scal, mend[:, b, :], op0, op1)
                last.then_inc(s["mended"], 1)

            for i in range(NG + 1):
                if i < NG:
                    ln_stats(A, i)
                    count_starts(i)
                if i >= 1:
                    evict_typed(A, i - 1)
            dve.wait_ge(s_near_used, NT)
            v.scalar_tensor_tensor(starts[:, 0:NT], near_f[:, :], float(STEPS), near_cnt[:, :], ALU.mult, ALU.add
                                   ).then_inc(s_starts, 1)
            dve.wait_ge(s_starts, 1)
            dve.wait_ge(s_ends, 1)
            link(v.tensor_copy(ends[:, :], pG[:, 0:NT]))
            v.tensor_scalar(end_f[:, :], ends[:, :], -1.0, 0.0, ALU.add, ALU.max)
            link(v.tensor_tensor(deg[:, :], ends[:, :], starts[:, 0:NT], ALU.subtract))
            v.tensor_copy(end_row[:, :], end_f[:, :])
            v.tensor_scalar_min(has[:, :], deg[:, :], 1.0)
            link(v.tensor_scalar_max(degc[:, :], deg[:, :], 1.0))
            v.tensor_scalar_add(deg1[:, :], degc[:, :], 1.0).then_inc(s_degs, 1)
            link(v.reciprocal(deg[:, :], degc[:, :]))
            v.tensor_tensor(rdeg[:, :], deg[:, :], has[:, :], ALU.mult)
            dve.wait_ge(s_log, 1)
            v.reciprocal(att[:, :], amp[:, :]).then_inc(s_nodes, 1)
            walk(0)
            for i in range(NG + 1):
                if i < NG:
                    gru(B, 0, i, 1)
                if i >= 1:
                    evict_typed(B, i - 1)
            walk(1)
            for i in range(NG + 2):
                if i < NG:
                    gru(C, 1, i, 2)
                if 1 <= i <= NG:
                    g = i - 1
                    dve.wait_ge(C["om"], g + 1)
                    chain[0] += 1
                    v.tensor_tensor(tiles(g), tiles(g), pO[:, 0:GC].rearrange("p (t d) -> p t d", t=GT), ALU.add).then_inc(s_v, 1)
                    dve.wait_ge(s_v, chain[0])
                    dve.sem_inc(C["xo"], 1)
                    link(v.tensor_tensor(tiles(g), tiles(g), rowbc(OUT_B), ALU.add))
                    ln_stats(C, g)
                if i >= 2:
                    g = i - 2
                    dve.wait_ge(C["hn"], g + 1)
                    for j in range(GT):
                        t = g * GT + j
                        dve.wait_ge(C["bev"], t + 1)
                        bank = (t % 4) * 512
                        v.tensor_tensor(node_term[:, t, :], pG[:, bank + D:bank + 2 * D], bias_rows[:, PRE_B, :], ALU.add)
                        v.tensor_tensor(x[:, t, :], x[:, t, :], pG[:, bank + 2 * D:bank + 3 * D], ALU.add).then_inc(C["aev"], 1)
                    dve.wait_ge(C["aev"], GT * (g + 1))
                    v.tensor_tensor(tiles(g), tiles(g), rowbc(LIN_B), ALU.add)
            walk(2)

            def prepare(g):
                h = g % 2
                dve.wait_ge(s_rows4[h], GT * SEM_DMA * (g // 2 + 1))
                gs = slice(g * GT, (g + 1) * GT)
                r4 = lambda n: rows4[:, h, :, n, :]
                v.tensor_tensor(r4(0), r4(0), bc(rdeg[:, gs]), ALU.mult)
                link(v.tensor_tensor(r4(1), r4(1), bc(rdeg[:, gs]), ALU.mult))
                link(v.tensor_tensor(tmpB, r4(0), r4(0), ALU.mult))
                link(v.tensor_tensor(r4(1), r4(1), tmpB, ALU.subtract))
                v.tensor_scalar(r4(1), r4(1), 0.0, EPS, ALU.max, ALU.add).then_inc(Dp["pre"], 1)
                v.tensor_tensor(tmpA, node_term[:, gs, :], bc(has[:, gs]), ALU.mult)
                v.tensor_tensor(r4(2), r4(2), bc(has[:, gs]), ALU.mult)
                link(v.tensor_tensor(r4(3), r4(3), bc(has[:, gs]), ALU.mult))
                v.tensor_tensor(r4(0), r4(0), tmpA, ALU.add)
                v.tensor_tensor(r4(2), r4(2), tmpA, ALU.add)
                v.tensor_tensor(r4(3), r4(3), tmpA, ALU.add).then_inc(Dp["agg"], 1)
                dve.wait_ge(Dp["agg"], g + 1)

            for i in range(NG + 1):
                if i < NG:
                    prepare(i)
                if i >= 1:
                    g = i - 1
                    for j in range(GT):
                        t = g * GT + j
                        dve.wait_ge(Dp["fm"], t + 1)
                        if j == GT - 1:
                            dve.sem_inc(Dp["rfree"], 1)
                        bank = (t % 4) * 512
                        xt = x[:, t, :]
                        link(v.tensor_tensor(xt, xt, pG[:, bank:bank + D], ALU.add))
                        link(v.scalar_tensor_tensor(xt, pG[:, bank + D:bank + 2 * D], amp[:, t:t + 1], xt, ALU.mult, ALU.add))
                        v.scalar_tensor_tensor(xt, pG[:, bank + 2 * D:bank + 3 * D], att[:, t:t + 1], xt, ALU.mult, ALU.add
                                               ).then_inc(Dp["xo"], 1)
                    dve.wait_ge(Dp["xo"], GT * (g + 1))
                    ln_stats(Dp, g)
            walk(3)

            def mean(ph, g, rnd):
                dve.wait_ge(s_rows[g], GT * SEM_DMA * rnd)
                sl = rows1[:, g * GT:(g + 1) * GT, :]
                v.tensor_tensor(sl, sl, bc(rdeg[:, g * GT:(g + 1) * GT]), ALU.mult).then_inc(ph["agg"], 1)

            mean(Ep, 0, 3)
            for i in range(NG + 1):
                if i < NG:
                    if i + 1 < NG:
                        mean(Ep, i + 1, 3)
                    dve.wait_ge(Ep["om"], i + 1)
                    chain[0] += 1
                    v.tensor_tensor(tiles(i), tiles(i), pO[:, 0:GC].rearrange("p (t d) -> p t d", t=GT), ALU.add).then_inc(s_v, 1)
                    dve.wait_ge(s_v, chain[0])
                    dve.sem_inc(Ep["xo"], 1)
                    link(v.tensor_tensor(tiles(i), tiles(i), rowbc(L2_B), ALU.add))
                    ln_stats(Ep, i)
                if i >= 1:
                    g = i - 1
                    dve.wait_ge(Ep["sm"], g + 1)
                    v.tensor_tensor(node_term[:, g * GT:(g + 1) * GT, :], pG[:, 0:GC].rearrange("p (t d) -> p t d", t=GT),
                                    rowbc(SELF_B), ALU.add).then_inc(Ep["sev"], 1)
            walk(4)
            mean(Fp, 0, 4)
            for i in range(NG):
                if i + 1 < NG:
                    mean(Fp, i + 1, 4)
                dve.wait_ge(Fp["om"], i + 1)
                nt = node_term[:, i * GT:(i + 1) * GT, :]
                link(v.tensor_tensor(nt, nt, pO[:, 0:GC].rearrange("p (t d) -> p t d", t=GT), ALU.add))
                v.scalar_tensor_tensor(tiles(i), nt, 0.0, tiles(i), ALU.max, ALU.add).then_inc(Fp["fin"], 1)


_INS = ["x", "src", "dst", "edge_type_8", "L0_gnn_node_proj_w", "L0_gnn_node_proj_b", "L0_gnn_edge_W",
        "L0_gnn_gru_wih", "L0_gnn_gru_whh", "L0_gnn_gru_bih", "L0_gnn_gru_bhh", "L0_gnn_out_w", "L0_gnn_out_b",
        "L1_gnn_W_pre", "L1_gnn_b_pre", "L1_gnn_W_post", "L1_gnn_b_post", "L1_gnn_W_lin", "L1_gnn_b_lin",
        "L2_gnn_W", "L2_gnn_b", "L3_gnn_W_self", "L3_gnn_b_self", "L3_gnn_W_neigh", "L3_gnn_b_neigh"]


def kernel(**inputs):
    import numpy as _np
    import concourse.bacc as _bacc
    from concourse import mybir as _mybir
    from concourse.bass_utils import run_bass_kernel_spmd as _run

    nc = _bacc.Bacc("TRN2", target_bir_lowering=False, num_devices=1)
    arrays, args = {}, {}
    for name in _INS:
        arr = _np.ascontiguousarray(inputs[name])
        arrays[f"in_{name}"] = arr
        args[name] = nc.dram_tensor(f"in_{name}", arr.shape, _mybir.dt.from_np(arr.dtype), kind="ExternalInput").ap()
    out = nc.dram_tensor("out_0", (N, D), _mybir.dt.float32, kind="ExternalOutput").ap()
    gnn_kernel(nc, args, out)
    r = _run(nc, [arrays], core_ids=[0])
    return r.results[0]["out_0"]
```

```python
import numpy as np
import concourse.bass as bass
from concourse import mybir
from contextlib import ExitStack

F32 = mybir.dt.float32
I32 = mybir.dt.int32
ALU = mybir.AluOpType
ACT = mybir.ActivationFunctionType
AX = mybir.AxisListType

P = 128
D = 128
N = 6250
E = 100000
T = 8
NT = -(-N // P)
TAIL = N - (NT - 1) * P
GT = 7
NG = NT // GT
GC = GT * D
HC = GC // 2
STEPS = 784
LAST = E - (P - 1) * STEPS
K = 8
HK = K // 2
ITERS = STEPS // (2 * K)
NO_NODE = NT * P
ZERO_ROW = P * STEPS
BIG = 3.0e38
EPS = 1e-5
SEM_DMA = 16
TS = 4
assert NG * GT == NT and ITERS * 2 * K == STEPS and 0 < LAST <= STEPS

W_PROJ, W_EDGE, W_IH, W_HH, W_OUT, W_SRC, W_DST, W_X, W_LIN, W_SELF, W_NEIGH, W_SLOTS = (
    0, 1, 17, 23, 29, 30, 31, 32, 33, 34, 35, 36)

ROUNDS = [("typed", False), ("typed", False), ("node", True), ("node", False), ("node", False)]


def gnn_kernel(nc, a, out):
    table_typed = nc.dram_tensor("table_typed", (NT * P * T, D), F32, kind="Internal").ap()
    table_node = nc.dram_tensor("table_node", (NT * P, D), F32, kind="Internal").ap()
    history = nc.dram_tensor("history", (ZERO_ROW + 1, D), F32, kind="Internal").ap()
    history4 = nc.dram_tensor("history4", (ZERO_ROW + 1, 4 * D), F32, kind="Internal").ap()
    dst_rows = nc.dram_tensor("dst_rows", (P, STEPS), F32, kind="Internal").ap()
    typed_tiles = table_typed.rearrange("(t p e) d -> p t (e d)", p=P, e=T)
    node_tiles = table_node.rearrange("(t p) d -> p t d", p=P)
    x_in = a["x"]

    ctx = ExitStack()
    with ctx:
        ctx.enter_context(nc.allow_non_contiguous_dma(reason="bias columns, 4 bytes a partition"))

        def sb(name, shape, dt=F32):
            return ctx.enter_context(nc.sbuf_tensor(name, shape, dt))

        def sem(name):
            return ctx.enter_context(nc.semaphore(name))

        def sems(phase, *names):
            return {n: sem(f"{phase}_{n}") for n in names}

        x = sb("x_res", [P, NT, D])
        hT = sb("hT", [P, NT * P])
        node_term = hT[:, :].rearrange("p (t d) -> p t d", t=NT)
        rows = sb("rows", [P, 2 * GT * 4 * D])
        rows1 = rows[:, 0:NT * D].rearrange("p (t d) -> p t d", t=NT)
        rows4 = rows[:, :].rearrange("p (h t c d) -> p h t c d", h=2, t=GT, c=4)
        near = rows[:, 0:GT * STEPS].rearrange("p (t s) -> p t s", t=GT)
        fetched = sb("fetched", [P, 2 * K * 2 * D])
        fetched1 = fetched[:, 0:2 * K * D].rearrange("p (h k d) -> p h k d", h=2, k=K)
        fetched2 = fetched[:, :].rearrange("p (h k c d) -> p h k c d", h=2, k=K, c=2)
        gates = fetched[:, 0:8 * HC].rearrange("p (h g c) -> p h g c", h=2, g=4)
        hist = sb("hist", [P, 2 * K * 4 * D])
        hist1 = hist[:, 0:2 * K * D].rearrange("p (h k d) -> p h k d", h=2, k=K)
        hist4 = hist[:, :].rearrange("p (h k c d) -> p h k c d", h=2, k=K, c=4)
        wnat = hist[:, 4 * GC:4 * GC + W_IH * D].rearrange("p (s d) -> p s d", s=W_IH)
        hn = hist[:, 0:2 * GC].rearrange("p (h t d) -> p h t d", h=2, t=GT)
        aT = hist[:, 2 * GC:4 * GC].rearrange("p (h c) -> p h c", h=2)
        tstage = hist[:, 4 * GC:4 * GC + TS * T * D].rearrange("p (h c) -> p h c", h=TS)
        bT = hist[:, 4 * GC:6 * GC].rearrange("p (h c) -> p h c", h=2)
        bstage = hist[:, 6 * GC:8 * GC].rearrange("p (h t d) -> p h t d", h=2, t=GT)
        tmpA = hist[:, 4 * GC:5 * GC].rearrange("p (t d) -> p t d", t=GT)
        tmpB = hist[:, 5 * GC:6 * GC].rearrange("p (t d) -> p t d", t=GT)
        wlate = rows[:, 0:(W_SLOTS - W_IH) * D].rearrange("p (s d) -> p s d", d=D)
        wpost = rows[:, W_SLOTS * D:(W_SLOTS + 13) * D].rearrange("p (c i) -> p c i", c=13)
        wT = sb("wT", [P, W_SLOTS, D])
        wcomb = sb("wcomb", [P, 4, 3, D])
        l2w = sb("l2w", [P, D])
        proj_b = sb("proj_b", [P, 1])
        b_ih = sb("b_ih", [P, 6])
        b_hh = sb("b_hh", [P, 6])
        b_rz = sb("b_rz", [P, 6])
        post_b = sb("post_b", [P, 1])
        post_bb = sb("post_bb", [P, D])
        bias_rows = sb("bias_rows", [P, 6, D])
        OUT_B, PRE_B, LIN_B, L2_B, SELF_B, NEIGH_B = range(6)
        ident = sb("ident", [P, P])
        ones = sb("ones", [P, P])
        prev_lane = sb("prev_lane", [P, P])
        next_lane = sb("next_lane", [P, P])
        corner = sb("corner", [P, P])
        idx_src = sb("idx_src", [P, STEPS + 2 * K], I32)
        idx_typ = sb("idx_typ", [P, STEPS + 2 * K], I32)
        masks = sb("masks", [P, STEPS + K, 2])
        idx_now = sb("idx_now", [P, 2, K], I32)
        mask_now = sb("mask_now", [P, 2, K, 2])
        dst_i = fetched[:, 0:STEPS].bitcast(I32)
        dstf = fetched[:, STEPS:2 * STEPS]
        e_tmp = fetched[:, 2 * STEPS:3 * STEPS]
        e_tmp2 = fetched[:, 3 * STEPS:4 * STEPS]
        node_i = sb("node_i", [P, NT], I32)
        node_f = sb("node_f", [P, NT])
        lane_i = sb("lane_i", [P, 1], I32)
        lane_f = sb("lane_f", [P, 1])
        heads = sb("heads", [P, P])
        diag = sb("diag", [P, P])
        g_mul = sb("g_mul", [P, P])
        g_max = sb("g_max", [P, P])
        g_min = sb("g_min", [P, P])
        col = sb("col", [P, 12])
        C_CNT, C_WHOLE, C_LAST1, C_HEAD1, C_CONT, C_CONTM, C_G, C_FE, C_FE1 = range(9)
        first_end = sb("first_end", [P, 1], I32)
        near_row = sb("near_row", [P, NT], I32)
        near_f = sb("near_f", [P, NT])
        near_cnt = sb("near_cnt", [P, NT])
        starts = sb("starts", [P, NT + 1])
        ends = sb("ends", [P, NT])
        end_f = sb("end_f", [P, NT])
        end_row = sb("end_row", [P, NT], I32)
        deg = sb("deg", [P, NT])
        has = sb("has", [P, NT])
        degc = sb("degc", [P, NT])
        deg1 = sb("deg1", [P, NT])
        rdeg = sb("rdeg", [P, NT])
        amp = sb("amp", [P, NT])
        att = sb("att", [P, NT])
        bn6 = sb("bn6", [P, GT, 6])
        mv = sb("mv", [P, NT, 2])
        var_e = sb("var_e", [P, NT])
        std_l = sb("std_l", [P, NT])
        rstd = sb("rstd", [P, NT])
        mend = sb("mend", [P, 4, D])
        scan = sb("scan", [P, 4, P + 1])
        aggT4 = sb("aggT4", [P, 2, 4 * D])

        def ps(name, banks):
            return ctx.enter_context(nc.psum_tensor(name, [P, banks * 512], F32))

        pT = ps("pT", 2)
        pO = ps("pO", 2)
        pG = ps("pG", 4)

        s_clear = sem("s_clear")
        s_edges = sem("s_edges")
        s_x = sem("s_x")
        s_w = sem("s_w")
        s_b = sem("s_b")
        s_wl = sem("s_wl")
        s_const = sem("s_const")
        s_pc = sem("s_pc")
        s_zero = sem("s_zero")
        s_dstf = sem("s_dstf")
        s_dstd = sem("s_dstd")
        s_wtr = sem("s_wtr")
        s_wcp = sem("s_wcp")
        s_wc = sem("s_wc")
        s_bpost = sem("s_bpost")
        s_wready = sem("s_wready")
        s_lane = sem("s_lane")
        s_lanep = sem("s_lanep")
        s_lanec = sem("s_lanec")
        s_nearix = sem("s_nearix")
        s_near = [sem(f"s_near{j}") for j in range(GT)]
        s_near_used = sem("s_near_used")
        s_starts = sem("s_starts")
        s_ends = sem("s_ends")
        s_degs = sem("s_degs")
        s_log = sem("s_log")
        s_nodes = sem("s_nodes")
        s_v = sem("s_v")
        s_rows = [sem(f"s_rows{g}") for g in range(NG)]
        s_rows4 = [sem(f"s_rows4_{h}") for h in range(2)]
        s_out = sem("s_out")
        R = dict(
            fetched=[sem(f"fetched{h}{q}") for h in range(2) for q in range(2)],
            staged=sem("staged"),
            state=sem("state"),
            saved=[sem(f"saved{h}") for h in range(2)],
            squared=sem("squared"), go=sem("go"),
            tails=sem("tails"), scanned=sem("scanned"), carries=sem("carries"),
            mend_in=sem("mend_in"), mended=sem("mended"), mend_out=sem("mend_out"),
        )

        def state_per_batch(r):
            return 1 + K * (3 if ROUNDS[r][1] else 1)

        BASE = [dict(
            fetched=r * ITERS * HK * SEM_DMA, staged=r * (4 * ITERS + 3), saved=r * ITERS * SEM_DMA,
            state=sum(2 * ITERS * state_per_batch(q) for q in range(r)),
            once=r, dma=r * SEM_DMA,
        ) for r in range(len(ROUNDS))]
        LN = ("var", "std", "hn")
        TR = ("mm0", "mm1", "ev0", "ev1", "tb0", "tb1", "tb2", "tb3")
        GRU = ("tr", "cp", "gate_r", "gate_z", "gate_nh", "gate", "rz", "hmul", "hadd", "tanh", "hnew")
        A = sems("A", *LN, *TR, "tr", "cp", "proj", "h")
        B = sems("B", *GRU, *TR)
        C = sems("C", *GRU, *LN, "om", "xo", "tr2", "cp2", "bac", "bev", "aev", "tn0", "tn1")
        Dp = sems("D", *LN, "scaled", "sq", "agg", "pre", "std4", "tr", "cp", "fm", "xo", "tn0", "tn1")
        Ep = sems("E", *LN, "agg", "tr", "cp", "om", "xo", "tr2", "cp2", "sm", "sev", "tn0", "tn1")
        Fp = sems("F", "agg", "tr", "cp", "om", "om_read", "fin")

        block = ctx.enter_context(nc.Block())

        def wait_table(eng, r):
            if ROUNDS[r][0] == "typed":
                ph = (A, B)[r]
                for k in range(TS):
                    eng.wait_ge(ph[f"tb{k}"], SEM_DMA * len(range(k, NT, TS)))
            else:
                ph = (C, Dp, Ep)[r - 2]
                for k in range(2):
                    eng.wait_ge(ph[f"tn{k}"], SEM_DMA * len(range(k, NG, 2)))

        def bc(colap):
            return colap.unsqueeze(2).to_broadcast([P, GT, D])

        def tiles(g):
            return x[:, g * GT:(g + 1) * GT, :]

        EARLY = [list(range(s, min(s + 4, W_IH))) for s in range(0, W_IH, 4)]
        LATE = [list(range(s, min(s + 4, W_X))) for s in range(W_IH, W_X, 4)] + [list(range(W_LIN, W_SLOTS))]

        @block.sync
        def _(sp):
            sp.wait_ge(s_clear, 5)

            def load_edges(name, tile):
                sp.dma_start(tile[0:P - 1, 0:STEPS],
                             a[name][0:(P - 1) * STEPS].rearrange("(p s) -> p s", s=STEPS)).then_inc(s_edges, SEM_DMA)
                sp.dma_start(tile[P - 1:P, 0:LAST],
                             a[name][(P - 1) * STEPS:E].rearrange("(p s) -> p s", p=1)).then_inc(s_edges, SEM_DMA)

            load_edges("dst", dst_i)
            sp.dma_start(x[:, 0:NT - 1, :], x_in[0:(NT - 1) * P, :].rearrange("(t p) d -> p t d", p=P)).then_inc(s_x, SEM_DMA)
            sp.dma_start(x[0:TAIL, NT - 1, :], x_in[(NT - 1) * P:N, :]).then_inc(s_x, SEM_DMA)
            load_edges("src", idx_src)
            load_edges("edge_type_8", idx_typ)
            for hd, w in ((history, D), (history4, 4 * D)):
                sp.dma_start(hd[ZERO_ROW:ZERO_ROW + 1, :], mend[0:1].rearrange("p c d -> p (c d)")[:, 0:w]).then_inc(s_zero, SEM_DMA)
            sp.wait_ge(s_dstf, 1)
            sp.dma_start(dst_rows, dstf).then_inc(s_dstd, SEM_DMA)
            sp.dma_start(post_b[:, :], a["L1_gnn_b_post"].rearrange("(o a) -> o a", a=1)).then_inc(s_b, SEM_DMA)
            sp.dma_start(b_ih[:, :], a["L0_gnn_gru_bih"].rearrange("l (c o) -> o (l c)", c=3)).then_inc(s_b, SEM_DMA)
            sp.dma_start(b_hh[:, :], a["L0_gnn_gru_bhh"].rearrange("l (c o) -> o (l c)", c=3)).then_inc(s_b, SEM_DMA)
            for i, n in enumerate(("L0_gnn_out_b", "L1_gnn_b_pre", "L1_gnn_b_lin", "L2_gnn_b", "L3_gnn_b_self", "L3_gnn_b_neigh")):
                sp.dma_start(bias_rows[:, i, :], a[n].rearrange("(o a) -> o a", o=1).to_broadcast([P, D])).then_inc(s_b, SEM_DMA)

            def store_typed(ph, g):
                for j in range(GT):
                    t = g * GT + j
                    sp.wait_ge(ph["ev0"], t + 1)
                    sp.wait_ge(ph["ev1"], t + 1)
                    sp.dma_start(typed_tiles[:, t, :], tstage[:, t % TS, :]).then_inc(ph[f"tb{t % TS}"], SEM_DMA)

            def save_history(r):
                h4 = ROUNDS[r][1]
                view = (history4 if h4 else history)[0:ZERO_ROW, :].rearrange("(p s) w -> p s w", p=P)
                per = state_per_batch(r)
                with sp.Fori(0, ITERS) as it:
                    for h in range(2):
                        sp.wait_ge(R["state"], it * (2 * per) + (BASE[r]["state"] + (h + 1) * per))
                        src = hist4[:, h].rearrange("p k c d -> p k (c d)") if h4 else hist1[:, h]
                        sp.dma_start(view[:, bass.ds(it * (2 * K) + h * K, K), :], src).then_inc(R["saved"][h], SEM_DMA)

            def store_node(ph, g, ready, src):
                sp.wait_ge(ready[0], ready[1])
                sp.dma_start(node_tiles[:, g * GT:(g + 1) * GT, :], src).then_inc(ph[f"tn{g % 2}"], SEM_DMA)

            for g in range(NG):
                store_typed(A, g)
            save_history(0)
            for g in range(NG):
                store_typed(B, g)
            save_history(1)
            for g in range(NG):
                store_node(C, g, (C["bev"], GT * (g + 1)), bstage[:, g % 2])
            save_history(2)
            for g in range(NG):
                store_node(Dp, g, (Dp["hn"], g + 1), hn[:, g % 2])
            save_history(3)
            for g in range(NG):
                store_node(Ep, g, (Ep["hn"], g + 1), hn[:, g % 2])
            save_history(4)
            for g in range(NG):
                sp.wait_ge(Fp["fin"], g + 1)
                full = min((g + 1) * GT, NT - 1)
                sp.dma_start(out[g * GT * P:full * P, :].rearrange("(t p) d -> p t d", p=P),
                             x[:, g * GT:full, :]).then_inc(s_out, SEM_DMA)
            sp.dma_start(out[(NT - 1) * P:N, :], x[0:TAIL, NT - 1, :]).then_inc(s_out, SEM_DMA)
            sp.wait_ge(s_out, SEM_DMA * (NG + 1))

        @block.gpsimd
        def _(pool):
            nc.gpsimd.iota(node_i[:, :], pattern=[[P, NT]], base=0, channel_multiplier=1)
            nc.gpsimd.iota(lane_i[:, :], pattern=[[0, 1]], base=0, channel_multiplier=1)
            nc.gpsimd.memset(ones[:, :], 1.0)
            nc.gpsimd.memset(scan[:, :, 0:1], 0.0).then_inc(s_const, 1)
            for n, (m, base, step) in enumerate(((ident, 0, 1), (prev_lane, 1, 1), (next_lane, -1, 1), (corner, P - 1, P))):
                nc.gpsimd.memset(m[:, :], 0.0).then_inc(s_pc, 1)
                pool.wait_ge(s_pc, n + 1)
                nc.gpsimd.affine_select(out=m[:, :], in_=m[:, :], compare_op=ALU.not_equal, fill=1.0,
                                        base=base, pattern=[[-1, P]], channel_multiplier=step).then_inc(s_const, 1)
            pool.wait_ge(s_dstd, SEM_DMA)
            pool.wait_ge(s_nearix, 1)
            pool.wait_ge(s_zero, 2 * SEM_DMA)
            for t in range(NT):
                if t >= GT:
                    pool.wait_ge(s_near_used, t - GT + 1)
                pool.indirect_dma_start(near[:, t % GT, :], None, dst_rows,
                                        bass.IndirectOffsetOnAxis(ap=near_row[:, t:t + 1], axis=0)
                                        ).then_inc(s_near[t % GT], SEM_DMA)

            def gather_round(r):
                wait_table(pool, r)
                table = table_typed if ROUNDS[r][0] == "typed" else table_node
                with pool.Fori(0, ITERS) as it:
                    for h in range(2):
                        for k in range(K):
                            if k % HK == 0:
                                pool.wait_ge(R["staged"], it * 4 + (BASE[r]["staged"] + 2 * h + k // HK + 1))
                                pool.sem_inc(R["go"], 1)
                            dest = fetched2[:, h, k, 0, :] if ROUNDS[r][1] else fetched1[:, h, k, :]
                            pool.indirect_dma_start(dest, None, table,
                                                    bass.IndirectOffsetOnAxis(ap=idx_now[:, h, k:k + 1], axis=0)
                                                    ).then_inc(R["fetched"][2 * h + k // HK], SEM_DMA)
                hd = history4 if ROUNDS[r][1] else history
                w = 4 * D if ROUNDS[r][1] else D
                m = mend[:, :, :].rearrange("p c d -> p (c d)")[:, 0:w]
                for h in range(2):
                    pool.wait_ge(R["saved"][h], BASE[r]["saved"] + SEM_DMA * ITERS)
                pool.indirect_dma_start(m, None, hd, bass.IndirectOffsetOnAxis(ap=first_end[:, 0:1], axis=0)
                                        ).then_inc(R["mend_in"], SEM_DMA)
                pool.wait_ge(R["mended"], BASE[r]["once"] + 1)
                pool.indirect_dma_start(hd, bass.IndirectOffsetOnAxis(ap=first_end[:, 0:1], axis=0), m, None
                                        ).then_inc(R["mend_out"], SEM_DMA)
                pool.wait_ge(R["mend_out"], BASE[r]["dma"] + SEM_DMA)

            def gather_nodes(r):
                for t in range(NT):
                    pool.indirect_dma_start(rows1[:, t, :], None, history,
                                            bass.IndirectOffsetOnAxis(ap=end_row[:, t:t + 1], axis=0)
                                            ).then_inc(s_rows[t // GT], SEM_DMA)

            gather_round(0)
            pool.wait_ge(s_nodes, 1)
            pool.wait_ge(s_wready, 1)
            gather_nodes(0)
            gather_round(1)
            gather_nodes(1)
            gather_round(2)
            for t in range(NT):
                g, j = divmod(t, GT)
                if g >= 2 and j == 0:
                    pool.wait_ge(Dp["tr"], t - 2 * GT + 4)
                if g >= 2 and j == 4:
                    pool.wait_ge(Dp["tr"], (g - 1) * GT)
                pool.indirect_dma_start(rows4[:, g % 2, t % GT].rearrange("p c d -> p (c d)"), None, history4,
                                        bass.IndirectOffsetOnAxis(ap=end_row[:, t:t + 1], axis=0)
                                        ).then_inc(s_rows4[g % 2], SEM_DMA)
            gather_round(3)
            gather_nodes(3)
            gather_round(4)
            gather_nodes(4)

        @block.scalar
        def _(act):
            def load(signal, dst, src):
                act.dma_start(dst, src).then_inc(signal, SEM_DMA)

            load(s_w, wnat[:, W_PROJ, :], a["L0_gnn_node_proj_w"])
            load(s_w, wnat[:, W_EDGE:W_IH, :], a["L0_gnn_edge_W"].rearrange("l t d h -> d (l t) h"))
            load(s_w, proj_b[:, :], a["L0_gnn_node_proj_b"].rearrange("(o a) -> o a", a=1))

            def late_weights():
                o = W_IH
                act.wait_ge(s_near_used, NT)
                load(s_wl, wlate[:, W_IH - o:W_HH - o, :], a["L0_gnn_gru_wih"].rearrange("l (c o) h -> o (l c) h", c=3))
                load(s_wl, wlate[:, W_HH - o:W_OUT - o, :], a["L0_gnn_gru_whh"].rearrange("l (c o) h -> o (l c) h", c=3))
                load(s_wl, wlate[:, W_OUT - o, :], a["L0_gnn_out_w"])
                load(s_wl, wlate[:, W_SRC - o, :], a["L1_gnn_W_pre"][:, D:2 * D])
                load(s_wl, wlate[:, W_DST - o, :], a["L1_gnn_W_pre"][:, 0:D])
                load(s_wl, wlate[:, W_LIN - o, :], a["L1_gnn_W_lin"])
                load(s_wl, wlate[:, W_SELF - o, :], a["L3_gnn_W_self"])
                load(s_wl, wlate[:, W_NEIGH - o, :], a["L3_gnn_W_neigh"])
                load(s_wl, wpost, a["L1_gnn_W_post"].rearrange("o (c i) -> o c i", c=13))
                load(s_wl, l2w[:, :], a["L2_gnn_W"])
                for b in range(len(EARLY), len(EARLY) + len(LATE)):
                    part = LATE[b - len(EARLY)]
                    act.wait_ge(s_wtr, b + 1)
                    nc.scalar.activation(wT[:, part[0]:part[-1] + 1, :], pG[:, (b % 4) * 512:(b % 4) * 512 + len(part) * D],
                                         ACT.Copy).then_inc(s_wcp, 1)
                act.wait_ge(s_wc, 1)
                for q in range(3):
                    nc.scalar.activation(wcomb[:, :, q, :], pG[:, q * 512:(q + 1) * 512].rearrange("p (c d) -> p c d", c=4), ACT.Copy)
                nc.scalar.activation(wT[:, W_X, :], pG[:, 3 * 512:3 * 512 + D], ACT.Copy)
                nc.scalar.activation(bias_rows[:, LIN_B, :], pG[:, 3 * 512 + D:3 * 512 + 2 * D], ACT.Copy).then_inc(s_wready, 1)

            def ln_std(ph, n, lo, hi):
                act.wait_ge(ph["var"], n + 1)
                nc.scalar.activation(std_l[:, lo * GT:hi * GT], var_e[:, lo * GT:hi * GT], ACT.Sqrt).then_inc(ph["std"], 1)

            def copy_T(ph, tr, cp, g, dst, func=ACT.Copy):
                act.wait_ge(ph[tr], g + 1)
                nc.scalar.activation(dst[:, g % 2, :], pT[:, 0:GC], func).then_inc(ph[cp], 1)

            def evict_typed(ph, g, js):
                for j in js:
                    t = g * GT + j
                    act.wait_ge(ph["mm0"], t + 1)
                    if t >= TS:
                        act.wait_ge(ph[f"tb{t % TS}"], SEM_DMA * (t // TS))
                    nc.scalar.activation(tstage[:, t % TS, 0:512], pO[:, 0:512], ACT.Copy).then_inc(ph["ev0"], 1)

            def copy_agg(ph, g):
                if g >= 2:
                    act.wait_ge(ph["gate"], 2 * (g - 1))
                copy_T(ph, "tr", "cp", g, aT)

            def gates_rz(ph, layer, g, h):
                u = 2 * g + h
                act.wait_ge(ph["gate_r"], u + 1)
                if u >= 2:
                    act.wait_ge(ph["hnew"], u - 1)
                nc.scalar.activation(gates[:, h, 0, :], pG[:, 0:HC], ACT.Sigmoid, bias=b_rz[:, 3 * layer:3 * layer + 1]
                                     ).then_inc(ph["rz"], 1)
                act.wait_ge(ph["gate_z"], u + 1)
                nc.scalar.activation(gates[:, h, 1, :], pG[:, 512:512 + HC], ACT.Sigmoid,
                                     bias=b_rz[:, 3 * layer + 1:3 * layer + 2]).then_inc(ph["rz"], 1)

            def gate_n(ph, layer, g, h):
                act.wait_ge(ph["hadd"], 2 * g + h + 1)
                nc.scalar.activation(gates[:, h, 2, :], gates[:, h, 2, :], ACT.Tanh,
                                     bias=b_ih[:, 3 * layer + 2:3 * layer + 3]).then_inc(ph["tanh"], 1)

            def gru_first(ph, layer):
                copy_agg(ph, 0)
                gates_rz(ph, layer, 0, 0)
                copy_agg(ph, 1)
                gate_n(ph, layer, 0, 0)
                gates_rz(ph, layer, 0, 1)
                gate_n(ph, layer, 0, 1)

            def squares():
                with act.Fori(0, ITERS) as it:
                    for n in range(4):
                        h, ks = n // 2, slice((n % 2) * HK, (n % 2 + 1) * HK)
                        act.wait_ge(R["fetched"][n], it * (HK * SEM_DMA) + (BASE[2]["fetched"] + HK * SEM_DMA))
                        nc.scalar.activation(fetched2[:, h, ks, 1, :], fetched2[:, h, ks, 0, :], ACT.Square
                                             ).then_inc(R["squared"], 1)

            def project(g):
                for h in range(2):
                    act.wait_ge(A["proj"], 2 * g + h + 1)
                    nc.scalar.activation(hT[:, g * GC + h * HC:g * GC + (h + 1) * HC], pG[:, h * 512:h * 512 + HC],
                                         ACT.Relu, bias=proj_b[:, 0:1]).then_inc(A["h"], 1)

            def copy_hn(g):
                if g >= 2:
                    act.wait_ge(A["proj"], 2 * (g - 1))
                copy_T(A, "tr", "cp", g, aT, ACT.Relu)

            ln_std(A, 0, 0, NG)
            copy_hn(0)
            project(0)
            for i in range(NG):
                if i + 1 < NG:
                    copy_hn(i + 1)
                evict_typed(A, i, range(4))
                if i + 1 < NG:
                    project(i + 1)
                evict_typed(A, i, range(4, GT))
            late_weights()
            act.wait_ge(s_degs, 1)
            nc.scalar.activation(amp[:, :], deg1[:, :], ACT.Ln).then_inc(s_log, 1)
            gru_first(B, 0)
            for i in range(NG):
                n = i + 1
                if n < NG:
                    gates_rz(B, 0, n, 0)
                evict_typed(B, i, range(0, 1))
                if n < NG:
                    gate_n(B, 0, n, 0)
                evict_typed(B, i, range(1, 4))
                if n + 1 < NG:
                    copy_agg(B, n + 1)
                if n < NG:
                    gates_rz(B, 0, n, 1)
                evict_typed(B, i, range(4, 5))
                if n < NG:
                    gate_n(B, 0, n, 1)
                evict_typed(B, i, range(5, GT))
            gru_first(C, 1)
            for i in range(NG - 1):
                n = i + 1
                gates_rz(C, 1, n, 0)
                gate_n(C, 1, n, 0)
                if n + 1 < NG:
                    copy_agg(C, n + 1)
                else:
                    ln_std(C, 0, 0, NG - 1)
                gates_rz(C, 1, n, 1)
                gate_n(C, 1, n, 1)

            def copy_normed(b):
                if b >= 2:
                    act.wait_ge(C["bac"], GT * (b - 1))
                copy_T(C, "tr2", "cp2", b, bT, ACT.Relu)

            copy_normed(0)
            ln_std(C, 1, NG - 1, NG)
            for b in range(NG):
                if b + 1 < NG:
                    copy_normed(b + 1)
                if b >= 2:
                    act.wait_ge(C[f"tn{b % 2}"], SEM_DMA * (b // 2))
                for j in range(GT):
                    t = b * GT + j
                    bank = (t % 4) * 512
                    act.wait_ge(C["bac"], t + 1)
                    nc.scalar.activation(bstage[:, b % 2, j, :], pG[:, bank:bank + D], ACT.Copy)
                    nc.scalar.activation(node_term[:, t, :], pG[:, bank + D:bank + 2 * D], ACT.Copy).then_inc(C["bev"], 1)
            squares()
            def scale_sums(g, js):
                act.wait_ge(s_rows4[g % 2], GT * SEM_DMA * (g // 2 + 1))
                for j in js:
                    t = g * GT + j
                    last = nc.scalar.activation(rows4[:, g % 2, j, 0:2, :], rows4[:, g % 2, j, 0:2, :], ACT.Copy,
                                                scale=rdeg[:, t:t + 1])
                last.then_inc(Dp["scaled"], 1)

            def square_mean(g):
                act.wait_ge(Dp["scaled"], 2 * (g + 1))
                if g >= 1:
                    act.wait_ge(Dp["pre"], g)
                nc.scalar.activation(tmpB, rows4[:, g % 2, :, 0, :], ACT.Square).then_inc(Dp["sq"], 1)

            def deviation(g):
                act.wait_ge(Dp["pre"], g + 1)
                nc.scalar.activation(rows4[:, g % 2, :, 1, :], rows4[:, g % 2, :, 1, :], ACT.Sqrt).then_inc(Dp["std4"], 1)

            scale_sums(0, range(4))
            scale_sums(0, range(4, GT))
            square_mean(0)
            deviation(0)
            for g in range(NG):
                n = g + 1
                for j in range(GT):
                    t = g * GT + j
                    act.wait_ge(Dp["tr"], t + 1)
                    if t >= 2:
                        act.wait_ge(Dp["fm"], t - 1)
                    nc.scalar.activation(aggT4[:, t % 2, :], pT[:, (t % 2) * 512:(t % 2) * 512 + 512], ACT.Copy
                                         ).then_inc(Dp["cp"], 1)
                    if j == 0 and g >= 1:
                        ln_std(Dp, g - 1, g - 1, g)
                    if n < NG:
                        if j == 2:
                            scale_sums(n, range(4))
                        elif j == 3:
                            scale_sums(n, range(4, GT))
                            square_mean(n)
                        elif j == 5:
                            deviation(n)
            ln_std(Dp, NG - 1, NG - 1, NG)
            copy_T(Ep, "tr", "cp", 0, aT)
            for i in range(NG + 1):
                if i + 1 < NG:
                    if i >= 1:
                        act.wait_ge(Ep["om"], i)
                    copy_T(Ep, "tr", "cp", i + 1, aT)
                if i < NG:
                    ln_std(Ep, i, i, i + 1)
                if i >= 1:
                    g = i - 1
                    if g >= 2:
                        act.wait_ge(Ep["sm"], g - 1)
                    copy_T(Ep, "tr2", "cp2", g, bT)
            for i in range(NG):
                if i >= 2:
                    act.wait_ge(Fp["om"], i - 1)
                copy_T(Fp, "tr", "cp", i, aT)

        @block.tensor
        def _(pe):
            mm = nc.tensor.matmul
            pe.wait_ge(s_const, 5)
            pe.wait_ge(s_lane, 1)
            mm(pO[:, 0:1], prev_lane[:, :], col[:, C_LAST1:C_LAST1 + 1], start=True, stop=True)
            mm(pO[:, 512:512 + P], ones[:, :], diag[:, :], start=True, stop=True).then_inc(s_lanep, 1)
            pe.wait_ge(s_w, SEM_DMA * 3)

            def transpose_weights(banks, first, src, s0):
                for b, part in enumerate(banks, first):
                    if b >= 4:
                        pe.wait_ge(s_wcp, b - 3)
                    for n, s in enumerate(part):
                        last = nc.tensor.transpose(pG[:, (b % 4) * 512 + n * D:(b % 4) * 512 + n * D + D], src[:, s - s0, :], ident[:, :])
                    last.then_inc(s_wtr, 1)

            transpose_weights(EARLY, 0, wnat, 0)
            pe.wait_ge(s_lane, 2)
            mm(pO[:, 0:P], ones[:, :], diag[:, :], start=True, stop=True).then_inc(s_lanep, 1)
            pe.wait_ge(s_wcp, len(EARLY))
            pe.wait_ge(s_lanec, 1)

            def late_weights():
                pe.wait_ge(s_wl, SEM_DMA * 10)
                transpose_weights(LATE, len(EARLY), wlate, W_IH)
                pe.wait_ge(s_wcp, len(EARLY) + len(LATE))
                pe.wait_ge(s_bpost, 1)
                for c in range(12):
                    mm(pG[:, (c // 4) * 512 + (c % 4) * D:(c // 4) * 512 + (c % 4) * D + D], wpost[:, 1 + c, :], wT[:, W_LIN, :],
                       start=True, stop=True)
                mm(pG[:, 3 * 512:3 * 512 + D], wpost[:, 0, :], wT[:, W_LIN, :], start=True, stop=True)
                mm(pG[:, 3 * 512 + D:3 * 512 + 2 * D], post_bb[:, :], wT[:, W_LIN, :], start=True, stop=False)
                mm(pG[:, 3 * 512 + D:3 * 512 + 2 * D], ident[:, :], bias_rows[:, LIN_B, :], start=False, stop=True).then_inc(s_wc, 1)
                pe.wait_ge(s_wready, 1)

            def transposes(src, g):
                for j in range(GT):
                    last = nc.tensor.transpose(pT[:, j * D:(j + 1) * D], src(j), ident[:, :])
                return last

            def typed(ph, layer, g, js, ready):
                if js[0] == 0:
                    pe.wait_ge(ready, 2 * g + 2)
                w = wT[:, W_EDGE + T * layer:W_EDGE + T * (layer + 1), :].rearrange("p t d -> p (t d)")
                for j in js:
                    t = g * GT + j
                    for b in range(2):
                        if t >= 1:
                            pe.wait_ge(ph[f"ev{b}"], t)
                        mm(pO[:, b * 512:(b + 1) * 512], hT[:, t * P:(t + 1) * P], w[:, b * 512:(b + 1) * 512],
                           start=True, stop=True).then_inc(ph[f"mm{b}"], 1)

            def transpose_agg(ph, rnd, g):
                pe.wait_ge(s_rows[g], GT * SEM_DMA * rnd)
                if g >= 1:
                    pe.wait_ge(ph["cp"], g)
                transposes(lambda j: rows1[:, g * GT + j, :], g).then_inc(ph["tr"], 1)

            def gru_gates(ph, layer, g, h):
                ih, hh = W_IH + 3 * layer, W_HH + 3 * layer
                u = 2 * g + h
                if h == 0:
                    pe.wait_ge(ph["cp"], g + 1)
                ag = aT[:, g % 2, h * HC:(h + 1) * HC]
                hh_in = hT[:, g * GC + h * HC:g * GC + (h + 1) * HC]
                for c, signal in enumerate(("gate_r", "gate_z")):
                    if u >= 1:
                        pe.wait_ge(ph["rz"], 2 * u - 1 + c)
                    mm(pG[:, c * 512:c * 512 + HC], wT[:, hh + c, :], hh_in, start=True, stop=False)
                    mm(pG[:, c * 512:c * 512 + HC], wT[:, ih + c, :], ag, start=False, stop=True).then_inc(ph[signal], 1)
                if u >= 1:
                    pe.wait_ge(ph["hmul"], u)
                mm(pG[:, 3 * 512:3 * 512 + HC], wT[:, hh + 2, :], hh_in, start=True, stop=True).then_inc(ph["gate_nh"], 1)
                if u >= 1:
                    pe.wait_ge(ph["hadd"], u)
                mm(pG[:, 2 * 512:2 * 512 + HC], wT[:, ih + 2, :], ag, start=True, stop=True).then_inc(ph["gate"], 1)

            def gru_first(ph, layer):
                transpose_agg(ph, layer + 1, 0)
                gru_gates(ph, layer, 0, 0)
                transpose_agg(ph, layer + 1, 1)
                gru_gates(ph, layer, 0, 1)

            def carry(r):
                nb = 4 if ROUNDS[r][1] else 1
                pe.wait_ge(R["state"], BASE[r]["state"] + state_per_batch(r) * 2 * ITERS)
                for b in range(nb):
                    src = hist4[:, 1, K - 1, b, :] if nb == 4 else hist1[:, 1, K - 1, :]
                    last = nc.tensor.transpose(pT[:, b * D:(b + 1) * D], src, ident[:, :])
                last.then_inc(R["tails"], 1)
                pe.wait_ge(R["scanned"], BASE[r]["once"] + 1)
                for b in range(nb):
                    last = nc.tensor.transpose(pT[:, 512 + b * D:512 + (b + 1) * D], scan[:, b, 0:P], ident[:, :])
                last.then_inc(R["carries"], 1)

            def transpose_hn(g):
                pe.wait_ge(A["hn"], g + 1)
                if g >= 1:
                    pe.wait_ge(A["cp"], g)
                transposes(lambda j: hn[:, g % 2, j, :], g).then_inc(A["tr"], 1)

            def project(g):
                pe.wait_ge(A["cp"], g + 1)
                for h in range(2):
                    if g >= 1:
                        pe.wait_ge(A["h"], 2 * (g - 1) + h + 1)
                    mm(pG[:, h * 512:h * 512 + HC], wT[:, W_PROJ, :], aT[:, g % 2, h * HC:(h + 1) * HC],
                       start=True, stop=True).then_inc(A["proj"], 1)

            transpose_hn(0)
            project(0)
            for i in range(NG):
                if i + 1 < NG:
                    transpose_hn(i + 1)
                typed(A, 0, i, range(4), A["h"])
                if i + 1 < NG:
                    project(i + 1)
                typed(A, 0, i, range(4, GT), A["h"])
            pe.wait_ge(s_starts, 1)
            pe.wait_ge(A["ev0"], NT)
            mm(pO[:, 0:NT], next_lane[:, :], starts[:, 0:NT], start=True, stop=False)
            mm(pO[:, 0:NT], corner[:, :], starts[:, 1:NT + 1], start=False, stop=True).then_inc(s_ends, 1)
            late_weights()
            carry(0)
            gru_first(B, 0)
            for i in range(NG):
                n = i + 1
                if n < NG:
                    gru_gates(B, 0, n, 0)
                typed(B, 1, i, range(4), B["hnew"])
                if n + 1 < NG:
                    transpose_agg(B, 1, n + 1)
                if n < NG:
                    gru_gates(B, 0, n, 1)
                typed(B, 1, i, range(4, GT), B["hnew"])
            carry(1)
            def bac(b):
                pe.wait_ge(C["cp2"], b + 1)
                if b == 0:
                    pe.wait_ge(C["hadd"], 2 * NG)
                    pe.wait_ge(C["rz"], 4 * NG)
                for j in range(GT):
                    t = b * GT + j
                    if t >= 4:
                        pe.wait_ge(C["aev"], t - 3)
                    mm(pG[:, (t % 4) * 512:(t % 4) * 512 + 3 * D], bT[:, b % 2, j * D:(j + 1) * D],
                       wT[:, W_SRC:W_X + 1, :].rearrange("p s d -> p (s d)"), start=True, stop=True).then_inc(C["bac"], 1)

            gru_first(C, 1)

            def out_product(g):
                pe.wait_ge(C["hnew"], 2 * g + 2)
                if g >= 1:
                    pe.wait_ge(C["xo"], g)
                for j in range(GT):
                    last = mm(pO[:, j * D:(j + 1) * D], hT[:, (g * GT + j) * P:(g * GT + j + 1) * P], wT[:, W_OUT, :],
                              start=True, stop=True)
                last.then_inc(C["om"], 1)

            for i in range(NG - 1):
                n = i + 1
                gru_gates(C, 1, n, 0)
                out_product(i)
                if n + 1 < NG:
                    transpose_agg(C, 2, n + 1)
                gru_gates(C, 1, n, 1)
            for b in range(NG + 1):
                if b < NG:
                    pe.wait_ge(C["hn"], b + 1)
                    if b >= 1:
                        pe.wait_ge(C["cp2"], b)
                    transposes(lambda j: hn[:, b % 2, j, :], b).then_inc(C["tr2"], 1)
                if b == 0:
                    out_product(NG - 1)
                else:
                    bac(b - 1)
            carry(2)

            def dtrans(t):
                g, j = divmod(t, GT)
                if j == 0:
                    pe.wait_ge(Dp["agg"], g + 1)
                    pe.wait_ge(Dp["std4"], g + 1)
                if t >= 2:
                    pe.wait_ge(Dp["cp"], t - 1)
                for n, c in enumerate((2, 3, 0, 1)):
                    last = nc.tensor.transpose(pT[:, (t % 2) * 512 + n * D:(t % 2) * 512 + (n + 1) * D],
                                               rows4[:, g % 2, j, c, :], ident[:, :])
                last.then_inc(Dp["tr"], 1)

            dtrans(0)
            for t in range(NT):
                if t + 1 < NT:
                    dtrans(t + 1)
                pe.wait_ge(Dp["cp"], t + 1)
                if t >= 4:
                    pe.wait_ge(Dp["xo"], t - 3)
                for c in range(4):
                    last = mm(pG[:, (t % 4) * 512:(t % 4) * 512 + 3 * D], aggT4[:, t % 2, c * D:(c + 1) * D],
                              wcomb[:, c].rearrange("p v d -> p (v d)"), start=(c == 0), stop=(c == 3))
                last.then_inc(Dp["fm"], 1)
            carry(3)
            def transpose_rows(ph, g, other=None):
                pe.wait_ge(ph["agg"], g + 1)
                if g >= 1:
                    pe.wait_ge(ph["cp"], g)
                transposes(lambda j: rows1[:, g * GT + j, :], g).then_inc(ph["tr"], 1)

            transpose_rows(Ep, 0)
            for i in range(NG + 1):
                if i + 1 < NG:
                    if i >= 2:
                        pe.wait_ge(Ep["cp2"], i - 1)
                    transpose_rows(Ep, i + 1)
                if i < NG:
                    pe.wait_ge(Ep["cp"], i + 1)
                    if i >= 1:
                        pe.wait_ge(Ep["xo"], i)
                    for j in range(GT):
                        last = mm(pO[:, j * D:(j + 1) * D], aT[:, i % 2, j * D:(j + 1) * D], l2w[:, :], start=True, stop=True)
                    last.then_inc(Ep["om"], 1)
                if i >= 1:
                    g = i - 1
                    pe.wait_ge(Ep["hn"], g + 1)
                    pe.wait_ge(Ep["cp"], min(i + 2, NG))
                    if g >= 1:
                        pe.wait_ge(Ep["cp2"], g)
                    transposes(lambda j: hn[:, g % 2, j, :], g).then_inc(Ep["tr2"], 1)
                    pe.wait_ge(Ep["cp2"], g + 1)
                    if g >= 1:
                        pe.wait_ge(Ep["sev"], g)
                    for j in range(GT):
                        last = mm(pG[:, j * D:(j + 1) * D], bT[:, g % 2, j * D:(j + 1) * D], wT[:, W_SELF, :], start=True, stop=True)
                    last.then_inc(Ep["sm"], 1)
            carry(4)
            transpose_rows(Fp, 0)
            for i in range(NG):
                if i + 1 < NG:
                    transpose_rows(Fp, i + 1)
                pe.wait_ge(Fp["cp"], i + 1)
                if i >= 1:
                    pe.wait_ge(Fp["om_read"], i)
                for j in range(GT):
                    last = mm(pO[:, j * D:(j + 1) * D], aT[:, i % 2, j * D:(j + 1) * D], wT[:, W_NEIGH, :], start=True, stop=True)
                last.then_inc(Fp["om"], 1)

        @block.vector
        def _(dve):
            v = nc.vector
            chain = [0]

            def link(ins):
                chain[0] += 1
                ins.then_inc(s_v, 1)
                dve.wait_ge(s_v, chain[0])

            v.memset(dst_i[:, :], NO_NODE).then_inc(s_clear, 1)
            v.memset(idx_src[:, :], 0).then_inc(s_clear, 1)
            v.memset(idx_typ[:, :], 0).then_inc(s_clear, 1)
            v.memset(x[:, NT - 1, :], 0.0).then_inc(s_clear, 1)
            v.memset(mend[0:1], 0.0).then_inc(s_clear, 1)
            v.memset(masks[:, STEPS:STEPS + K, 0], 0.0)
            v.memset(starts[:, NT:NT + 1], float(E))
            link(v.memset(masks[:, 0, 0:1], 0.0))
            dve.wait_ge(s_const, 1)
            v.tensor_copy(node_f[:, :], node_i[:, :])
            v.tensor_copy(lane_f[:, :], lane_i[:, :])
            dve.wait_ge(s_edges, 6 * SEM_DMA)
            chain[0] += 1
            v.tensor_copy(dstf, dst_i[:, :]).then_inc(s_v, 1)
            dve.wait_ge(s_v, chain[0])
            dve.sem_inc(s_dstf, 1)
            c = lambda n: col[:, n:n + 1]
            v.tensor_scalar(e_tmp, dstf, dstf[:, 0:1], None, ALU.is_equal, ALU.add, accum_out=c(C_CNT))
            v.tensor_scalar_add(c(C_LAST1), dstf[:, STEPS - 1:STEPS], 1.0)
            v.tensor_scalar_add(c(C_HEAD1), dstf[:, 0:1], 1.0)
            dve.wait_ge(s_const, 5)
            v.tensor_scalar(diag[:, :], ident[:, :], dstf[:, 0:1], None, ALU.mult).then_inc(s_lane, 1)

            def edge_masks():
                link(v.tensor_tensor(masks[:, 1:STEPS, 0], dstf[:, 1:STEPS], dstf[:, 0:STEPS - 1], ALU.is_equal))
                v.tensor_scalar(masks[:, :, 1], masks[:, :, 0], -1.0, BIG, ALU.add, ALU.mult)
                dve.wait_ge(s_edges, 6 * SEM_DMA)
                v.tensor_copy(e_tmp, idx_src[:, 0:STEPS])
                link(v.tensor_copy(e_tmp2, idx_typ[:, 0:STEPS]))
                link(v.scalar_tensor_tensor(e_tmp2, e_tmp, float(T), e_tmp2, ALU.mult, ALU.add))
                link(v.tensor_copy(idx_typ[:, 0:STEPS], e_tmp2))

            def lane_columns():
                v.tensor_scalar(c(C_WHOLE), c(C_CNT), float(STEPS), None, ALU.is_equal)
                link(v.scalar_tensor_tensor(c(C_FE), lane_f[:, :], float(STEPS), c(C_CNT), ALU.mult, ALU.add))
                link(v.tensor_scalar_add(c(C_FE1), c(C_FE), -1.0))
                v.tensor_copy(first_end[:, :], c(C_FE1))
                dve.wait_ge(s_lanep, 1)
                v.tensor_copy(heads[:, :], pO[:, 512:512 + P])
                link(v.tensor_tensor(c(C_CONT), pO[:, 0:1], c(C_HEAD1), ALU.is_equal))
                v.tensor_scalar(c(C_CONTM), c(C_CONT), -1.0, BIG, ALU.add, ALU.mult)
                link(v.tensor_tensor(c(C_G), c(C_CONT), c(C_WHOLE), ALU.mult))
                v.tensor_scalar(diag[:, :], ident[:, :], c(C_G), None, ALU.mult).then_inc(s_lane, 1)

            def near_rows():
                less = rows1
                link(v.tensor_tensor(less, heads[:, :].unsqueeze(1).to_broadcast([P, NT, P]),
                                     node_f[:, :].unsqueeze(2).to_broadcast([P, NT, P]), ALU.is_lt))
                link(v.tensor_reduce(near_cnt[:, :], less, AX.X, ALU.add))
                link(v.tensor_scalar(near_f[:, :], near_cnt[:, :], -1.0, 0.0, ALU.add, ALU.max))
                v.tensor_copy(near_row[:, :], near_f[:, :]).then_inc(s_nearix, 1)

            def early_weights():
                for b, part in enumerate(EARLY):
                    dve.wait_ge(s_wtr, b + 1)
                    v.tensor_copy(wT[:, part[0]:part[-1] + 1, :],
                                  pG[:, (b % 4) * 512:(b % 4) * 512 + len(part) * D].rearrange("p (s d) -> p s d", d=D)
                                  ).then_inc(s_wcp, 1)

            def ln_stats(g):
                for j in range(GT):
                    last = v.bn_stats(bn6[:, j, :], x[:, g * GT + j, :])
                link(last)
                for j in range(GT):
                    last = v.bn_aggr(mv[:, g * GT + j, :], bn6[:, j, :])
                link(last)

            def ln_rstd(ph, n, lo, hi):
                ts = slice(lo * GT, hi * GT)
                v.tensor_scalar_add(var_e[:, ts], mv[:, ts, 1], EPS).then_inc(ph["var"], 1)
                dve.wait_ge(ph["std"], n + 1)
                link(v.reciprocal(rstd[:, ts], std_l[:, ts]))

            def ln_norm(ph, g, stored, read):
                if g >= 2:
                    dve.wait_ge(ph[read], g - 1)
                    if stored:
                        dve.wait_ge(ph[f"tn{g % 2}"], SEM_DMA * (g // 2))
                for j in range(GT):
                    t = g * GT + j
                    last = v.tensor_scalar(hn[:, g % 2, j, :], x[:, t, :], mv[:, t, 0:1], rstd[:, t:t + 1], ALU.subtract, ALU.mult)
                if stored:
                    link(last)
                    last = v.tensor_scalar_max(hn[:, g % 2], hn[:, g % 2], 0.0)
                last.then_inc(ph["hn"], 1)

            def evict_typed(ph, g, js):
                for j in js:
                    t = g * GT + j
                    dve.wait_ge(ph["mm1"], t + 1)
                    if t >= TS:
                        dve.wait_ge(ph[f"tb{t % TS}"], SEM_DMA * (t // TS))
                    v.tensor_copy(tstage[:, t % TS, 512:1024], pO[:, 512:1024]).then_inc(ph["ev1"], 1)

            def count_starts(g, js):
                for j in js:
                    t = g * GT + j
                    dve.wait_ge(s_near[j], SEM_DMA * (g + 1))
                    v.tensor_scalar(near[:, j, :], near[:, j, :], node_f[:, t:t + 1], None, ALU.is_lt, ALU.add,
                                    accum_out=near_cnt[:, t:t + 1]).then_inc(s_near_used, 1)

            def means(ph, g, rnd):
                dve.wait_ge(s_rows[g], GT * SEM_DMA * rnd)
                sl = rows1[:, g * GT:(g + 1) * GT, :]
                v.tensor_tensor(sl, sl, bc(rdeg[:, g * GT:(g + 1) * GT]), ALU.mult).then_inc(ph["agg"], 1)

            def gru_add(ph, layer, g, h):
                u = 2 * g + h
                dve.wait_ge(ph["rz"], 2 * u + 1)
                dve.wait_ge(ph["gate_nh"], u + 1)
                v.scalar_tensor_tensor(gates[:, h, 2, :], pG[:, 3 * 512:3 * 512 + HC],
                                       b_hh[:, 3 * layer + 2:3 * layer + 3], gates[:, h, 0, :], ALU.add, ALU.mult
                                       ).then_inc(ph["hmul"], 1)
                dve.wait_ge(ph["hmul"], u + 1)
                dve.wait_ge(ph["gate"], u + 1)
                v.tensor_tensor(gates[:, h, 2, :], gates[:, h, 2, :], pG[:, 2 * 512:2 * 512 + HC], ALU.add
                                ).then_inc(ph["hadd"], 1)

            def gru_new(ph, g, h):
                hs = hT[:, g * GC + h * HC:g * GC + (h + 1) * HC]
                d = gates[:, h, 3, :]
                dve.wait_ge(ph["tanh"], 2 * g + h + 1)
                link(v.tensor_tensor(d, hs, gates[:, h, 2, :], ALU.subtract))
                link(v.tensor_tensor(d, d, gates[:, h, 1, :], ALU.mult))
                link(v.tensor_tensor(d, d, gates[:, h, 2, :], ALU.add))
                v.tensor_scalar_max(hs, d, 0.0).then_inc(ph["hnew"], 1)

            def gru_first(ph, layer):
                gru_add(ph, layer, 0, 0)
                gru_new(ph, 0, 0)
                gru_add(ph, layer, 0, 1)
                gru_new(ph, 0, 1)

            def add_bias(terms, i):
                link(v.tensor_tensor(terms, terms, bias_rows[:, i:i + 1, :].to_broadcast([P, NT, D]), ALU.add))

            def stage_first(r):
                idx = idx_typ if ROUNDS[r][0] == "typed" else idx_src
                for h in range(2):
                    for q in range(2):
                        v.tensor_copy(idx_now[:, h, q * HK:(q + 1) * HK], idx[:, h * K + q * HK:h * K + (q + 1) * HK]
                                      ).then_inc(R["staged"], 1)

            def walk(r, meanwhile=None):
                s, at, many = R, BASE[r], ROUNDS[r][1]
                idx = idx_typ if ROUNDS[r][0] == "typed" else idx_src
                per = state_per_batch(r)
                wait_table(dve, r)
                if many:
                    first = hist4[:, 1, K - 1].rearrange("p c d -> p (c d)")
                else:
                    first = hist1[:, 1, K - 1, :]
                link(v.memset(first, 0.0))

                link(v.tensor_copy(mask_now[:, 0], masks[:, 0:K, :]))
                ops = 3 if many else 1

                def stage(it, h, q):
                    v.tensor_copy(idx_now[:, h, q * HK:(q + 1) * HK], idx[:, bass.ds(it * (2 * K) + ((h + 2) * K + q * HK), HK)]
                                  ).then_inc(s["staged"], 1)

                def turn(it, again):
                    for h in range(2):
                        base = it * (2 * per) + (at["state"] + h * per)
                        if again:
                            dve.wait_ge(s["saved"][h], it * SEM_DMA + at["saved"])
                        for k in range(K):
                            if k % HK == 0:
                                n = 2 * h + k // HK
                                if many:
                                    dve.wait_ge(s["squared"], it * 4 + n + 1)
                                else:
                                    dve.wait_ge(s["fetched"][n], it * (HK * SEM_DMA) + (at["fetched"] + HK * SEM_DMA))
                            ph, pk = (h, k - 1) if k else (1 - h, K - 1)
                            keep, low = mask_now[:, h, k, 0:1], mask_now[:, h, k, 1:2]

                            def wait_before(op):
                                if k or h or again:
                                    dve.wait_ge(s["state"], base + (ops * (k - 1) + op + (1 if k - 1 > HK else 0)))

                            wait_before(1)
                            if not many:
                                v.scalar_tensor_tensor(hist1[:, h, k, :], hist1[:, ph, pk, :], keep, fetched1[:, h, k, :],
                                                       ALU.mult, ALU.add).then_inc(s["state"], 1)
                            else:
                                v.scalar_tensor_tensor(hist4[:, h, k, 0:2, :], hist4[:, ph, pk, 0:2, :], keep, fetched2[:, h, k],
                                                       ALU.mult, ALU.add).then_inc(s["state"], 1)
                                wait_before(2)
                                v.scalar_tensor_tensor(hist4[:, h, k, 2, :], hist4[:, ph, pk, 2, :], low, fetched2[:, h, k, 0, :],
                                                       ALU.add, ALU.max).then_inc(s["state"], 1)
                                wait_before(3)
                                v.scalar_tensor_tensor(hist4[:, h, k, 3, :], hist4[:, ph, pk, 3, :], low, fetched2[:, h, k, 0, :],
                                                       ALU.subtract, ALU.min).then_inc(s["state"], 1)
                            if k == 0 and h == 1:
                                stage(it, 0, 1)
                            elif k == 0 and again:
                                stage(it - 1, 1, 1)
                            elif k == HK:
                                stage(it, h, 0)
                                v.tensor_copy(mask_now[:, 1 - h], masks[:, bass.ds(it * (2 * K) + (h + 1) * K, K), :]
                                              ).then_inc(s["state"], 1)

                turn(0, False)
                with dve.Fori(1, ITERS) as it:
                    turn(it, True)

                nb = 4 if many else 1
                dve.wait_ge(s["tails"], at["once"] + 1)
                for b in range(nb):
                    mask, op0, op1 = ((g_mul, ALU.mult, ALU.add), (g_mul, ALU.mult, ALU.add),
                                      (g_max, ALU.add, ALU.max), (g_min, ALU.add, ALU.min))[b]
                    last = v.tensor_tensor_scan(scan[:, b, 1:P + 1], mask[:, :], pT[:, b * D:(b + 1) * D], 0.0, op0, op1)
                last.then_inc(s["scanned"], 1)
                if meanwhile:
                    meanwhile()
                dve.wait_ge(s["carries"], at["once"] + 1)
                dve.wait_ge(s["mend_in"], at["dma"] + SEM_DMA)
                for b in range(nb):
                    scal, op0, op1 = ((c(C_CONT), ALU.mult, ALU.add), (c(C_CONT), ALU.mult, ALU.add),
                                      (c(C_CONTM), ALU.add, ALU.max), (c(C_CONTM), ALU.subtract, ALU.min))[b]
                    last = v.scalar_tensor_tensor(mend[:, b, :], pT[:, 512 + b * D:512 + (b + 1) * D], scal, mend[:, b, :], op0, op1)
                last.then_inc(s["mended"], 1)

            dve.wait_ge(s_x, 2 * SEM_DMA)
            for g in range(NG):
                ln_stats(g)
            ln_rstd(A, 0, 0, NG)
            ln_norm(A, 0, False, "tr")
            ln_norm(A, 1, False, "tr")
            early_weights()
            lane_columns()
            near_rows()
            dve.wait_ge(s_lanep, 2)
            v.tensor_copy(g_mul[:, :], pO[:, 0:P]).then_inc(s_lanec, 1)
            dve.wait_ge(s_lanec, 1)
            v.tensor_scalar(g_max[:, :], g_mul[:, :], -1.0, BIG, ALU.add, ALU.mult)
            v.tensor_scalar(g_min[:, :], g_mul[:, :], -1.0, -BIG, ALU.add, ALU.mult)
            for i in range(NG):
                for j in range(GT):
                    evict_typed(A, i, range(j, j + 1))
                    if i >= 1:
                        count_starts(i - 1, range(j, j + 1))
                    if j == 0 and i + 2 < NG:
                        ln_norm(A, i + 2, False, "tr")
                if i == 0:
                    edge_masks()
                    stage_first(0)
            count_starts(NG - 1, range(GT))
            dve.wait_ge(s_near_used, NT)
            v.scalar_tensor_tensor(starts[:, 0:NT], near_f[:, :], float(STEPS), near_cnt[:, :], ALU.mult, ALU.add
                                   ).then_inc(s_starts, 1)
            dve.wait_ge(s_starts, 1)
            dve.wait_ge(s_b, 9 * SEM_DMA)
            v.tensor_copy(post_bb[:, :], post_b[:, 0:1].to_broadcast([P, D])).then_inc(s_bpost, 1)
            v.tensor_tensor(b_rz[:, :], b_ih[:, :], b_hh[:, :], ALU.add)
            v.tensor_tensor(bias_rows[:, SELF_B, :], bias_rows[:, SELF_B, :], bias_rows[:, NEIGH_B, :], ALU.add)
            dve.wait_ge(s_ends, 1)
            link(v.tensor_copy(ends[:, :], pO[:, 0:NT]))
            v.tensor_scalar_add(end_f[:, :], ends[:, :], -1.0 - ZERO_ROW)
            link(v.tensor_tensor(deg[:, :], ends[:, :], starts[:, 0:NT], ALU.subtract))
            v.tensor_scalar_min(has[:, :], deg[:, :], 1.0)
            link(v.tensor_scalar_max(degc[:, :], deg[:, :], 1.0))
            link(v.tensor_tensor(end_f[:, :], end_f[:, :], has[:, :], ALU.mult))
            link(v.tensor_scalar_add(end_f[:, :], end_f[:, :], float(ZERO_ROW)))
            v.tensor_copy(end_row[:, :], end_f[:, :])
            v.tensor_scalar_add(deg1[:, :], degc[:, :], 1.0).then_inc(s_degs, 1)
            link(v.reciprocal(deg[:, :], degc[:, :]))
            v.tensor_tensor(rdeg[:, :], deg[:, :], has[:, :], ALU.mult).then_inc(s_nodes, 1)
            walk(0)
            dve.wait_ge(s_log, 1)
            link(v.reciprocal(att[:, :], amp[:, :]))
            gru_first(B, 0)
            stage_first(1)
            for i in range(NG):
                n = i + 1
                if n < NG:
                    gru_add(B, 0, n, 0)
                evict_typed(B, i, range(0, 2))
                if n < NG:
                    gru_new(B, n, 0)
                evict_typed(B, i, range(2, 4))
                if n < NG:
                    gru_add(B, 0, n, 1)
                evict_typed(B, i, range(4, 6))
                if n < NG:
                    gru_new(B, n, 1)
                evict_typed(B, i, range(6, GT))
            add_bias(x[:, :, :], OUT_B)
            walk(1)
            gru_first(C, 1)
            stage_first(2)

            def add_out(g):
                dve.wait_ge(C["om"], g + 1)
                v.tensor_tensor(tiles(g), tiles(g), pO[:, 0:GC].rearrange("p (t d) -> p t d", t=GT), ALU.add
                                ).then_inc(C["xo"], 1)
                dve.wait_ge(C["xo"], g + 1)
                ln_stats(g)

            for i in range(NG - 1):
                n = i + 1
                gru_add(C, 1, n, 0)
                gru_new(C, n, 0)
                add_out(i)
                if n == NG - 1:
                    ln_rstd(C, 0, 0, NG - 1)
                gru_add(C, 1, n, 1)
                if n == NG - 1:
                    ln_norm(C, 0, False, "tr2")
                gru_new(C, n, 1)
            ln_norm(C, 1, False, "tr2")
            add_out(NG - 1)
            ln_rstd(C, 1, NG - 1, NG)
            for b in range(NG):
                for j in range(GT):
                    t = b * GT + j
                    dve.wait_ge(C["bev"], t + 1)
                    bank = (t % 4) * 512
                    v.tensor_tensor(x[:, t, :], x[:, t, :], pG[:, bank + 2 * D:bank + 3 * D], ALU.add).then_inc(C["aev"], 1)
                    if j == 1 and b + 2 < NG:
                        ln_norm(C, b + 2, False, "tr2")
                        dve.wait_ge(C["hn"], b + 3)

            def bias_terms():
                dve.wait_ge(C["aev"], NT)
                add_bias(node_term, PRE_B)
                add_bias(x[:, :, :], LIN_B)

            walk(2, bias_terms)

            def variance(g):
                r1 = rows4[:, g % 2, :, 1, :]
                dve.wait_ge(Dp["sq"], g + 1)
                link(v.tensor_tensor(r1, r1, tmpB, ALU.subtract))
                v.tensor_scalar(r1, r1, 0.0, EPS, ALU.max, ALU.add).then_inc(Dp["pre"], 1)

            def add_terms(g):
                nt = node_term[:, g * GT:(g + 1) * GT, :]
                for n in (0, 2, 3):
                    last = v.tensor_tensor(rows4[:, g % 2, :, n, :], rows4[:, g % 2, :, n, :], nt, ALU.add)
                last.then_inc(Dp["agg"], 1)

            link(v.tensor_tensor(node_term, node_term, has[:, :].unsqueeze(2).to_broadcast([P, NT, D]), ALU.mult))
            stage_first(3)
            variance(0)
            add_terms(0)
            for g in range(NG):
                n = g + 1
                for j in range(GT):
                    t = g * GT + j
                    dve.wait_ge(Dp["fm"], t + 1)
                    bank = (t % 4) * 512
                    xt = x[:, t, :]
                    link(v.tensor_tensor(xt, xt, pG[:, bank:bank + D], ALU.add))
                    link(v.scalar_tensor_tensor(xt, pG[:, bank + D:bank + 2 * D], amp[:, t:t + 1], xt, ALU.mult, ALU.add))
                    v.scalar_tensor_tensor(xt, pG[:, bank + 2 * D:bank + 3 * D], att[:, t:t + 1], xt, ALU.mult, ALU.add
                                           ).then_inc(Dp["xo"], 1)
                    if n < NG and j == 3:
                        variance(n)
                    if n < NG and j == 4:
                        add_terms(n)
                dve.wait_ge(Dp["xo"], GT * n)
                ln_stats(g)
                ln_rstd(Dp, g, g, n)
                ln_norm(Dp, g, True, "hn")
            dve.wait_ge(Dp["hn"], NG)
            add_bias(x[:, :, :], L2_B)
            walk(3)
            stage_first(4)
            means(Ep, 0, 3)
            means(Ep, 1, 3)
            for i in range(NG + 1):
                if i < NG:
                    dve.wait_ge(Ep["om"], i + 1)
                    v.tensor_tensor(tiles(i), tiles(i), pO[:, 0:GC].rearrange("p (t d) -> p t d", t=GT), ALU.add
                                    ).then_inc(Ep["xo"], 1)
                    dve.wait_ge(Ep["xo"], i + 1)
                    ln_stats(i)
                    ln_rstd(Ep, i, i, i + 1)
                    ln_norm(Ep, i, True, "tr2")
                    if i + 2 < NG:
                        means(Ep, i + 2, 3)
                if i >= 1:
                    g = i - 1
                    dve.wait_ge(Ep["sm"], g + 1)
                    v.tensor_copy(node_term[:, g * GT:(g + 1) * GT, :], pG[:, 0:GC].rearrange("p (t d) -> p t d", t=GT)
                                  ).then_inc(Ep["sev"], 1)
            dve.wait_ge(Ep["sev"], NG)
            add_bias(node_term, SELF_B)
            walk(4)
            means(Fp, 0, 4)
            for i in range(NG):
                if i + 1 < NG:
                    means(Fp, i + 1, 4)
                dve.wait_ge(Fp["om"], i + 1)
                nt = node_term[:, i * GT:(i + 1) * GT, :]
                v.tensor_tensor(nt, nt, pO[:, 0:GC].rearrange("p (t d) -> p t d", t=GT), ALU.add).then_inc(Fp["om_read"], 1)
                dve.wait_ge(Fp["om_read"], i + 1)
                v.scalar_tensor_tensor(tiles(i), nt, 0.0, tiles(i), ALU.max, ALU.add).then_inc(Fp["fin"], 1)


_INS = ["x", "src", "dst", "edge_type_8", "L0_gnn_node_proj_w", "L0_gnn_node_proj_b", "L0_gnn_edge_W",
        "L0_gnn_gru_wih", "L0_gnn_gru_whh", "L0_gnn_gru_bih", "L0_gnn_gru_bhh", "L0_gnn_out_w", "L0_gnn_out_b",
        "L1_gnn_W_pre", "L1_gnn_b_pre", "L1_gnn_W_post", "L1_gnn_b_post", "L1_gnn_W_lin", "L1_gnn_b_lin",
        "L2_gnn_W", "L2_gnn_b", "L3_gnn_W_self", "L3_gnn_b_self", "L3_gnn_W_neigh", "L3_gnn_b_neigh"]


def kernel(**inputs):
    import numpy as _np
    import concourse.bacc as _bacc
    from concourse import mybir as _mybir
    from concourse.bass_utils import run_bass_kernel_spmd as _run

    nc = _bacc.Bacc("TRN2", target_bir_lowering=False, num_devices=1)
    arrays, args = {}, {}
    for name in _INS:
        arr = _np.ascontiguousarray(inputs[name])
        arrays[f"in_{name}"] = arr
        args[name] = nc.dram_tensor(f"in_{name}", arr.shape, _mybir.dt.from_np(arr.dtype), kind="ExternalInput").ap()
    out = nc.dram_tensor("out_0", (N, D), _mybir.dt.float32, kind="ExternalOutput").ap()
    gnn_kernel(nc, args, out)
    r = _run(nc, [arrays], core_ids=[0])
    return r.results[0]["out_0"]
```

```python
import numpy as np
import concourse.bass as bass
from concourse import mybir
from contextlib import ExitStack

F32 = mybir.dt.float32
I32 = mybir.dt.int32
ALU = mybir.AluOpType
ACT = mybir.ActivationFunctionType
AX = mybir.AxisListType

P = 128
D = 128
N = 6250
E = 100000
T = 8
NT = -(-N // P)
TAIL = N - (NT - 1) * P
GT = 7
NG = NT // GT
GC = GT * D
HC = GC // 2
STEPS = 784
LAST = E - (P - 1) * STEPS
K = 8
HK = K // 2
ITERS = STEPS // (2 * K)
NO_NODE = NT * P
ZERO_ROW = P * STEPS
BIG = 3.0e38
EPS = 1e-5
SEM_DMA = 16
RUN = 196
LANE_RUNS = STEPS // RUN
RUNS = P * LANE_RUNS
NEAR = 4 * GT
TS = 4
assert ITERS == NT
assert LANE_RUNS * RUN == STEPS and RUNS <= 512 and NG * GT == NT and ITERS * 2 * K == STEPS and 0 < LAST <= STEPS

W_PROJ, W_EDGE, W_IH, W_HH, W_OUT, W_SRC, W_DST, W_X, W_LIN, W_SELF, W_NEIGH, W_SLOTS = (
    0, 1, 17, 23, 29, 30, 31, 32, 33, 34, 35, 36)

ROUNDS = [("typed", False), ("typed", False), ("node", True), ("node", False), ("node", False)]


def gnn_kernel(nc, a, out):
    table_typed = nc.dram_tensor("table_typed", (NT * P * T, D), F32, kind="Internal").ap()
    table_node = nc.dram_tensor("table_node", (NT * P, D), F32, kind="Internal").ap()
    history = nc.dram_tensor("history", (ZERO_ROW + 1, D), F32, kind="Internal").ap()
    history4 = nc.dram_tensor("history4", (ZERO_ROW + 1, 4 * D), F32, kind="Internal").ap()
    dst_rows = nc.dram_tensor("dst_rows", (RUNS, RUN), F32, kind="Internal").ap()
    typed_tiles = table_typed.rearrange("(t p e) d -> p t (e d)", p=P, e=T)
    node_tiles = table_node.rearrange("(t p) d -> p t d", p=P)
    x_in = a["x"]

    ctx = ExitStack()
    with ctx:
        ctx.enter_context(nc.allow_non_contiguous_dma(reason="bias columns, 4 bytes a partition"))

        def sb(name, shape, dt=F32):
            return ctx.enter_context(nc.sbuf_tensor(name, shape, dt))

        def sem(name):
            return ctx.enter_context(nc.semaphore(name))

        def sems(phase, *names):
            return {n: sem(f"{phase}_{n}") for n in names}

        x = sb("x_res", [P, NT, D])
        hT = sb("hT", [P, NT * P])
        node_term = hT[:, :].rearrange("p (t d) -> p t d", t=NT)
        rows = sb("rows", [P, 2 * GT * 4 * D])
        rows1 = rows[:, 0:NT * D].rearrange("p (t d) -> p t d", t=NT)
        rows4 = rows[:, :].rearrange("p (h t c d) -> p h t c d", h=2, t=GT, c=4)
        near = rows[:, 0:NEAR * RUN].rearrange("p (t s) -> p t s", t=NEAR)
        heads = rows[:, NEAR * RUN:NEAR * RUN + RUNS]
        normed = rows1
        normed_T = rows[:, NT * D:NT * D + GC]
        run_diag = rows[:, 0:RUNS].rearrange("p (j q) -> p j q", j=LANE_RUNS)
        fetched = sb("fetched", [P, 2 * K * 2 * D])
        fetched1 = fetched[:, 0:2 * K * D].rearrange("p (h k d) -> p h k d", h=2, k=K)
        fetched2 = fetched[:, :].rearrange("p (h k c d) -> p h k c d", h=2, k=K, c=2)
        gates = fetched[:, 0:8 * HC].rearrange("p (h g c) -> p h g c", h=2, g=4)
        hist = sb("hist", [P, 2 * K * 4 * D])
        hist1 = hist[:, 0:2 * K * D].rearrange("p (h k d) -> p h k d", h=2, k=K)
        hist4 = hist[:, :].rearrange("p (h k c d) -> p h k c d", h=2, k=K, c=4)
        wnat = hist[:, 4 * GC:4 * GC + W_IH * D].rearrange("p (s d) -> p s d", s=W_IH)
        hn = hist[:, 0:2 * GC].rearrange("p (h t d) -> p h t d", h=2, t=GT)
        aT = hist[:, 2 * GC:4 * GC].rearrange("p (h c) -> p h c", h=2)
        tstage = hist[:, 4 * GC:4 * GC + TS * T * D].rearrange("p (h c) -> p h c", h=TS)
        bT = hist[:, 4 * GC:6 * GC].rearrange("p (h c) -> p h c", h=2)
        bstage = hist[:, 6 * GC:8 * GC].rearrange("p (h t d) -> p h t d", h=2, t=GT)
        mean_sq = hist[:, 5 * GC:6 * GC].rearrange("p (t d) -> p t d", t=GT)
        wlate = rows[:, 0:(W_SLOTS - W_IH) * D].rearrange("p (s d) -> p s d", d=D)
        wpost = rows[:, W_SLOTS * D:(W_SLOTS + 13) * D].rearrange("p (c i) -> p c i", c=13)
        wT = sb("wT", [P, W_SLOTS, D])
        wcomb = sb("wcomb", [P, 4, 3, D])
        l2w = sb("l2w", [P, D])
        proj_b = sb("proj_b", [P, 1])
        b_ih = sb("b_ih", [P, 6])
        b_hh = sb("b_hh", [P, 6])
        b_rz = sb("b_rz", [P, 6])
        post_b = sb("post_b", [P, 1])
        post_bb = sb("post_bb", [P, D])
        bias_rows = sb("bias_rows", [P, 6, D])
        OUT_B, PRE_B, LIN_B, L2_B, SELF_B, NEIGH_B = range(6)
        ident = sb("ident", [P, P])
        ones = sb("ones", [P, P])
        prev_lane = sb("prev_lane", [P, P])
        next_lane = sb("next_lane", [P, P])
        corner = sb("corner", [P, P])
        idx_src = sb("idx_src", [P, STEPS + 2 * K], I32)
        idx_typ = sb("idx_typ", [P, STEPS + 2 * K], I32)
        masks = sb("masks", [P, STEPS + K, 2])
        idx_now = sb("idx_now", [P, 2, K], I32)
        mask_now = sb("mask_now", [P, 2, K, 2])
        dst_i = fetched[:, 0:STEPS].bitcast(I32)
        dstf = fetched[:, STEPS:2 * STEPS]
        e_tmp = fetched[:, 2 * STEPS:3 * STEPS]
        e_tmp2 = fetched[:, 3 * STEPS:4 * STEPS]
        signs = fetched[:, 4 * STEPS:4 * STEPS + RUNS]
        node_i = sb("node_i", [P, NT], I32)
        node_f = sb("node_f", [P, NT])
        lane_i = sb("lane_i", [P, 1], I32)
        lane_f = sb("lane_f", [P, 1])
        diag = sb("diag", [P, P])
        g_mul = sb("g_mul", [P, P])
        g_max = sb("g_max", [P, P])
        g_min = sb("g_min", [P, P])
        col = sb("col", [P, 12])
        C_CNT, C_WHOLE, C_LAST1, C_HEAD1, C_CONT, C_CONTM, C_G, C_FE, C_FE1 = range(9)
        first_end = sb("first_end", [P, 1], I32)
        near_row = sb("near_row", [P, NT], I32)
        near_f = sb("near_f", [P, NT])
        node_b = sb("node_b", [P, NT])
        coarse = sb("coarse", [P, NT])
        near_cnt = sb("near_cnt", [P, NT])
        starts = sb("starts", [P, NT + 1])
        ends = sb("ends", [P, NT])
        end_f = sb("end_f", [P, NT])
        end_row = sb("end_row", [P, NT], I32)
        deg = sb("deg", [P, NT])
        has = sb("has", [P, NT])
        degc = sb("degc", [P, NT])
        deg1 = sb("deg1", [P, NT])
        rdeg = sb("rdeg", [P, NT])
        amp = sb("amp", [P, NT])
        att = sb("att", [P, NT])
        bn6 = sb("bn6", [P, GT, 6])
        mv = sb("mv", [P, NT, 2])
        var_e = sb("var_e", [P, NT])
        std_l = sb("std_l", [P, NT])
        rstd = sb("rstd", [P, NT])
        shift = sb("shift", [P, NT])
        mend = sb("mend", [P, 4, D])
        normed_t = sb("normed_t", [P, D])
        normed_tT = sb("normed_tT", [P, D])
        norm_by = sb("norm_by", [P, 3])
        scan = sb("scan", [P, 4, P + 1])
        aggT4 = sb("aggT4", [P, 2, 4 * D])

        def ps(name, banks):
            return ctx.enter_context(nc.psum_tensor(name, [P, banks * 512], F32))

        pT = ps("pT", 2)
        pO = ps("pO", 2)
        pG = ps("pG", 4)

        s_clear = sem("s_clear")
        s_dst = sem("s_dst")
        s_edges = sem("s_edges")
        s_x0 = sem("s_x0")
        s_x = sem("s_x")
        s_heads = sem("s_heads")
        s_coarse = sem("s_coarse")
        s_w = sem("s_w")
        s_b = sem("s_b")
        s_wl = sem("s_wl")
        s_const = sem("s_const")
        s_pc = sem("s_pc")
        s_zero = sem("s_zero")
        s_dstf = sem("s_dstf")
        s_dstd = sem("s_dstd")
        s_wtr = sem("s_wtr")
        s_wcp = sem("s_wcp")
        s_wc = sem("s_wc")
        s_bpost = sem("s_bpost")
        s_wready = sem("s_wready")
        s_lane = sem("s_lane")
        s_lanep = sem("s_lanep")
        s_nearix = sem("s_nearix")
        s_near_used = sem("s_near_used")
        s_starts = sem("s_starts")
        s_ends = sem("s_ends")
        s_degs = sem("s_degs")
        s_log = sem("s_log")
        s_nodes = sem("s_nodes")
        s_v = sem("s_v")
        s_rows = [sem(f"s_rows{g}") for g in range(NG)]
        s_rows4 = [sem(f"s_rows4_{h}") for h in range(2)]
        s_out = sem("s_out")
        R = dict(
            fetched=[sem(f"fetched{h}{q}") for h in range(2) for q in range(2)],
            staged=sem("staged"),
            state=sem("state"),
            saved=[sem(f"saved{h}") for h in range(2)],
            squared=sem("squared"),
            go=sem("go"),
            tails=sem("tails"),
            scanned=sem("scanned"),
            carries=sem("carries"),
            mend_in=sem("mend_in"),
            mended=sem("mended"),
            mend_out=sem("mend_out"),
        )

        def state_per_batch(r):
            return 1 + K * (3 if ROUNDS[r][1] else 1)

        def saves(r):
            return 2 if ROUNDS[r][1] else 1

        BASE = [dict(
            fetched=r * ITERS * HK * SEM_DMA, staged=r * (4 * ITERS + 3), saved=sum(saves(q) for q in range(r)) * ITERS * SEM_DMA,
            state=sum(2 * ITERS * state_per_batch(q) for q in range(r)),
            once=r, dma=r * SEM_DMA,
        ) for r in range(len(ROUNDS))]
        LN = ("var", "std", "hn")
        TR = ("mm0", "mm1", "ev0", "ev1", "tb0", "tb1", "tb2", "tb3")
        GRU = ("tr", "cp", "gate_r", "gate_z", "gate_nh", "gate", "rz", "hmul", "hadd", "tanh", "hnew")
        A = sems("A", *LN, *TR, "tr", "cp", "proj", "h")
        B = sems("B", *GRU, *TR)
        C = sems("C", *GRU, *LN, "om", "xo", "tr2", "cp2", "bac", "bev", "shift", "norm2", "tr3", "cp3", "terms",
                 "tev", "tn0", "tn1")
        Dp = sems("D", *LN, "scaled", "sq", "agg", "pre", "std4", "tr", "cp", "fm", "xo", "tn0", "tn1")
        Ep = sems("E", *LN, "tr", "cp", "om", "xo", "shift", "norm2", "tr2", "cp2", "sm", "sev", "tn0", "tn1")
        Fp = sems("F", "tr", "cp", "om", "om_read", "fin")

        block = ctx.enter_context(nc.Block())

        def wait_table(eng, r):
            if ROUNDS[r][0] == "typed":
                ph = (A, B)[r]
                for k in range(TS):
                    eng.wait_ge(ph[f"tb{k}"], SEM_DMA * len(range(k, NT, TS)))
            else:
                ph = (C, Dp, Ep)[r - 2]
                for k in range(2):
                    eng.wait_ge(ph[f"tn{k}"], SEM_DMA * len(range(k, NG, 2)))

        def tiles(g):
            return x[:, g * GT:(g + 1) * GT, :]

        EARLY = [list(range(s, min(s + 4, W_IH))) for s in range(0, W_IH, 4)]
        LATE = [list(range(s, min(s + 4, W_X))) for s in range(W_IH, W_X, 4)] + [list(range(W_LIN, W_SLOTS))]

        @block.sync
        def _(sp):
            def load_edges(name, tile, signal):
                for lo, hi in ((0, 112), (112, P - 1)):
                    sp.dma_start(tile[lo:hi, 0:STEPS],
                                 a[name][lo * STEPS:hi * STEPS].rearrange("(p s) -> p s", s=STEPS)).then_inc(signal, SEM_DMA)
                sp.dma_start(tile[P - 1:P, 0:LAST],
                             a[name][(P - 1) * STEPS:E].rearrange("(p s) -> p s", p=1)).then_inc(signal, SEM_DMA)

            sp.wait_ge(s_clear, 1)
            load_edges("dst", dst_i, s_dst)
            sp.dma_start(x[:, 0:2 * GT, :], x_in[0:2 * GT * P, :].rearrange("(t p) d -> p t d", p=P)).then_inc(s_x0, SEM_DMA)
            sp.wait_ge(s_clear, 2)
            sp.dma_start(x[:, 2 * GT:NT - 1, :], x_in[2 * GT * P:(NT - 1) * P, :].rearrange("(t p) d -> p t d", p=P)).then_inc(s_x, SEM_DMA)
            sp.dma_start(x[0:TAIL, NT - 1, :], x_in[(NT - 1) * P:N, :]).then_inc(s_x, SEM_DMA)
            sp.wait_ge(s_dstf, 1)
            sp.dma_start(dst_rows.rearrange("(p j) s -> p (j s)", p=P), dstf).then_inc(s_dstd, SEM_DMA)
            sp.wait_ge(s_clear, 5)
            load_edges("src", idx_src, s_edges)
            load_edges("edge_type_8", idx_typ, s_edges)
            for hd, w in ((history, D), (history4, 4 * D)):
                sp.dma_start(hd[ZERO_ROW:ZERO_ROW + 1, :], mend[0:1].rearrange("p c d -> p (c d)")[:, 0:w]).then_inc(s_zero, SEM_DMA)
            sp.dma_start(post_b[:, :], a["L1_gnn_b_post"].rearrange("(o a) -> o a", a=1)).then_inc(s_b, SEM_DMA)
            sp.dma_start(b_ih[:, :], a["L0_gnn_gru_bih"].rearrange("l (c o) -> o (l c)", c=3)).then_inc(s_b, SEM_DMA)
            sp.dma_start(b_hh[:, :], a["L0_gnn_gru_bhh"].rearrange("l (c o) -> o (l c)", c=3)).then_inc(s_b, SEM_DMA)
            for i, n in enumerate(("L0_gnn_out_b", "L1_gnn_b_pre", "L1_gnn_b_lin", "L2_gnn_b", "L3_gnn_b_self", "L3_gnn_b_neigh")):
                sp.dma_start(bias_rows[:, i, :], a[n].rearrange("(o a) -> o a", o=1).to_broadcast([P, D])).then_inc(s_b, SEM_DMA)

            def store_typed(ph, g):
                for j in range(GT):
                    t = g * GT + j
                    sp.wait_ge(ph["ev0"], t + 1)
                    sp.wait_ge(ph["ev1"], t + 1)
                    sp.dma_start(typed_tiles[:, t, :], tstage[:, t % TS, :]).then_inc(ph[f"tb{t % TS}"], SEM_DMA)

            def save_history(r):
                h4 = ROUNDS[r][1]
                view = (history4 if h4 else history)[0:ZERO_ROW, :].rearrange("(p s) w -> p s w", p=P)
                per = state_per_batch(r)
                with sp.Fori(0, ITERS) as it:
                    for h in range(2):
                        if h4:
                            for q in range(2):
                                done = (3 * HK, per)[q]
                                sp.wait_ge(R["state"], it * (2 * per) + (BASE[r]["state"] + h * per + done))
                                sp.dma_start(view[:, bass.ds(it * (2 * K) + (h * K + q * HK), HK), :],
                                             hist4[:, h, q * HK:(q + 1) * HK].rearrange("p k c d -> p k (c d)")
                                             ).then_inc(R["saved"][h], SEM_DMA)
                            continue
                        sp.wait_ge(R["state"], it * (2 * per) + (BASE[r]["state"] + (h + 1) * per))
                        sp.dma_start(view[:, bass.ds(it * (2 * K) + h * K, K), :], hist1[:, h]).then_inc(R["saved"][h], SEM_DMA)

            def store_node(ph, g, ready, src):
                sp.wait_ge(ready[0], ready[1])
                sp.dma_start(node_tiles[:, g * GT:(g + 1) * GT, :], src).then_inc(ph[f"tn{g % 2}"], SEM_DMA)

            for g in range(NG):
                store_typed(A, g)
            save_history(0)
            for g in range(NG):
                store_typed(B, g)
            save_history(1)
            for g in range(NG):
                store_node(C, g, (C["bev"], g + 1), bstage[:, g % 2])
            save_history(2)
            for g in range(NG):
                store_node(Dp, g, (Dp["hn"], g + 1), hn[:, g % 2])
            save_history(3)
            for g in range(NG):
                store_node(Ep, g, (Ep["hn"], g + 1), hn[:, g % 2])
            save_history(4)
            for g in range(NG):
                sp.wait_ge(Fp["fin"], g + 1)
                full = min((g + 1) * GT, NT - 1)
                sp.dma_start(out[g * GT * P:full * P, :].rearrange("(t p) d -> p t d", p=P),
                             x[:, g * GT:full, :]).then_inc(s_out, SEM_DMA)
            sp.dma_start(out[(NT - 1) * P:N, :], x[0:TAIL, NT - 1, :]).then_inc(s_out, SEM_DMA)
            sp.wait_ge(s_out, SEM_DMA * (NG + 1))

        @block.gpsimd
        def _(pool):
            nc.gpsimd.iota(node_i[:, :], pattern=[[P, NT]], base=0, channel_multiplier=1)
            nc.gpsimd.iota(lane_i[:, :], pattern=[[0, 1]], base=0, channel_multiplier=1)
            nc.gpsimd.memset(ones[:, :], 1.0)
            nc.gpsimd.memset(scan[:, :, 0:1], 0.0).then_inc(s_const, 1)
            for n, (m, base, step) in enumerate(((ident, 0, 1), (prev_lane, 1, 1), (next_lane, -1, 1), (corner, P - 1, P))):
                nc.gpsimd.memset(m[:, :], 0.0).then_inc(s_pc, 1)
                pool.wait_ge(s_pc, n + 1)
                nc.gpsimd.affine_select(out=m[:, :], in_=m[:, :], compare_op=ALU.not_equal, fill=1.0,
                                        base=base, pattern=[[-1, P]], channel_multiplier=step).then_inc(s_const, 1)
            pool.wait_ge(s_dstd, SEM_DMA)
            pool.wait_ge(s_zero, 2 * SEM_DMA)
            for t in range(NT):
                if t % GT == 0:
                    pool.wait_ge(s_nearix, t // GT + 1)
                if t >= NEAR and t % GT == 0:
                    pool.wait_ge(s_near_used, t - NEAR + GT)
                pool.indirect_dma_start(near[:, t % NEAR, :], None, dst_rows,
                                        bass.IndirectOffsetOnAxis(ap=near_row[:, t:t + 1], axis=0)
                                        ).then_inc(s_rows[t // GT], SEM_DMA)

            def gather_round(r):
                wait_table(pool, r)
                table = table_typed if ROUNDS[r][0] == "typed" else table_node
                with pool.Fori(0, ITERS) as it:
                    for h in range(2):
                        for k in range(K):
                            if k % HK == 0:
                                pool.wait_ge(R["staged"], it * 4 + (BASE[r]["staged"] + 2 * h + k // HK + 1))
                                pool.sem_inc(R["go"], 1)
                            dest = fetched2[:, h, k, 0, :] if ROUNDS[r][1] else fetched1[:, h, k, :]
                            pool.indirect_dma_start(dest, None, table,
                                                    bass.IndirectOffsetOnAxis(ap=idx_now[:, h, k:k + 1], axis=0)
                                                    ).then_inc(R["fetched"][2 * h + k // HK], SEM_DMA)
                hd = history4 if ROUNDS[r][1] else history
                w = 4 * D if ROUNDS[r][1] else D
                m = mend[:, :, :].rearrange("p c d -> p (c d)")[:, 0:w]
                for h in range(2):
                    pool.wait_ge(R["saved"][h], BASE[r]["saved"] + saves(r) * SEM_DMA * ITERS)
                pool.indirect_dma_start(m, None, hd, bass.IndirectOffsetOnAxis(ap=first_end[:, 0:1], axis=0)
                                        ).then_inc(R["mend_in"], SEM_DMA)
                pool.wait_ge(R["mended"], BASE[r]["once"] + 1)
                pool.indirect_dma_start(hd, bass.IndirectOffsetOnAxis(ap=first_end[:, 0:1], axis=0), m, None
                                        ).then_inc(R["mend_out"], SEM_DMA)
                pool.wait_ge(R["mend_out"], BASE[r]["dma"] + SEM_DMA)

            def gather_nodes(r):
                for t in range(NT):
                    pool.indirect_dma_start(rows1[:, t, :], None, history,
                                            bass.IndirectOffsetOnAxis(ap=end_row[:, t:t + 1], axis=0)
                                            ).then_inc(s_rows[t // GT], SEM_DMA)

            gather_round(0)
            pool.wait_ge(s_nodes, 1)
            pool.wait_ge(s_wready, 1)
            gather_nodes(0)
            gather_round(1)
            gather_nodes(1)
            gather_round(2)
            for t in range(NT):
                g, j = divmod(t, GT)
                if g >= 2 and j == 0:
                    pool.wait_ge(Dp["tr"], t - 2 * GT + 4)
                if g >= 2 and j == 4:
                    pool.wait_ge(Dp["tr"], (g - 1) * GT)
                pool.indirect_dma_start(rows4[:, g % 2, t % GT].rearrange("p c d -> p (c d)"), None, history4,
                                        bass.IndirectOffsetOnAxis(ap=end_row[:, t:t + 1], axis=0)
                                        ).then_inc(s_rows4[g % 2], SEM_DMA)
            gather_round(3)
            gather_nodes(3)
            gather_round(4)
            pool.wait_ge(Ep["sev"], NG)
            gather_nodes(4)

        @block.scalar
        def _(act):
            def load(signal, dst, src):
                act.dma_start(dst, src).then_inc(signal, SEM_DMA)

            load(s_w, wnat[:, W_PROJ, :], a["L0_gnn_node_proj_w"])
            load(s_w, wnat[:, W_EDGE:W_IH, :], a["L0_gnn_edge_W"].rearrange("l t d h -> d (l t) h"))
            load(s_w, proj_b[:, :], a["L0_gnn_node_proj_b"].rearrange("(o a) -> o a", a=1))

            def late_weights():
                o = W_IH
                act.wait_ge(s_near_used, NT)
                act.wait_ge(s_coarse, NT)
                load(s_wl, wlate[:, W_IH - o:W_HH - o, :], a["L0_gnn_gru_wih"].rearrange("l (c o) h -> o (l c) h", c=3))
                load(s_wl, wlate[:, W_HH - o:W_OUT - o, :], a["L0_gnn_gru_whh"].rearrange("l (c o) h -> o (l c) h", c=3))
                load(s_wl, wlate[:, W_OUT - o, :], a["L0_gnn_out_w"])
                load(s_wl, wlate[:, W_SRC - o, :], a["L1_gnn_W_pre"][:, D:2 * D])
                load(s_wl, wlate[:, W_DST - o, :], a["L1_gnn_W_pre"][:, 0:D])
                load(s_wl, wlate[:, W_LIN - o, :], a["L1_gnn_W_lin"])
                load(s_wl, wlate[:, W_SELF - o, :], a["L3_gnn_W_self"])
                load(s_wl, wlate[:, W_NEIGH - o, :], a["L3_gnn_W_neigh"])
                load(s_wl, wpost, a["L1_gnn_W_post"].rearrange("o (c i) -> o c i", c=13))
                load(s_wl, l2w[:, :], a["L2_gnn_W"])
                for b in range(len(EARLY), len(EARLY) + len(LATE)):
                    part = LATE[b - len(EARLY)]
                    act.wait_ge(s_wtr, b + 1)
                    nc.scalar.activation(wT[:, part[0]:part[-1] + 1, :], pG[:, (b % 4) * 512:(b % 4) * 512 + len(part) * D],
                                         ACT.Copy).then_inc(s_wcp, 1)
                act.wait_ge(s_wc, 1)
                for q in range(3):
                    nc.scalar.activation(wcomb[:, :, q, :], pG[:, q * 512:(q + 1) * 512].rearrange("p (c d) -> p c d", c=4), ACT.Copy)
                nc.scalar.activation(wT[:, W_X, :], pG[:, 3 * 512:3 * 512 + D], ACT.Copy)
                nc.scalar.activation(bias_rows[:, LIN_B, :], pG[:, 3 * 512 + D:3 * 512 + 2 * D], ACT.Copy).then_inc(s_wready, 1)

            def ln_std(ph, n, lo, hi):
                act.wait_ge(ph["var"], n + 1)
                nc.scalar.activation(std_l[:, lo * GT:hi * GT], var_e[:, lo * GT:hi * GT], ACT.Sqrt).then_inc(ph["std"], 1)

            def copy_T(ph, tr, cp, g, dst, func=ACT.Copy):
                act.wait_ge(ph[tr], g + 1)
                nc.scalar.activation(dst[:, g % 2, :], pT[:, 0:GC], func).then_inc(ph[cp], 1)

            def evict_typed(ph, g, js):
                for j in js:
                    t = g * GT + j
                    act.wait_ge(ph["mm0"], t + 1)
                    if t >= TS:
                        act.wait_ge(ph[f"tb{t % TS}"], SEM_DMA * (t // TS))
                    nc.scalar.activation(tstage[:, t % TS, 0:512], pO[:, 0:512], ACT.Copy).then_inc(ph["ev0"], 1)

            def copy_agg(ph, g):
                if g >= 2:
                    act.wait_ge(ph["gate"], 2 * (g - 1))
                copy_T(ph, "tr", "cp", g, aT)

            def gates_rz(ph, layer, g, h):
                u = 2 * g + h
                act.wait_ge(ph["gate_r"], u + 1)
                if u >= 2:
                    act.wait_ge(ph["hnew"], u - 1)
                nc.scalar.activation(gates[:, h, 0, :], pG[:, 0:HC], ACT.Sigmoid, bias=b_rz[:, 3 * layer:3 * layer + 1]
                                     ).then_inc(ph["rz"], 1)
                act.wait_ge(ph["gate_z"], u + 1)
                nc.scalar.activation(gates[:, h, 1, :], pG[:, 512:512 + HC], ACT.Sigmoid,
                                     bias=b_rz[:, 3 * layer + 1:3 * layer + 2]).then_inc(ph["rz"], 1)

            def gate_n(ph, layer, g, h):
                act.wait_ge(ph["hadd"], 2 * g + h + 1)
                nc.scalar.activation(gates[:, h, 2, :], gates[:, h, 2, :], ACT.Tanh,
                                     bias=b_ih[:, 3 * layer + 2:3 * layer + 3]).then_inc(ph["tanh"], 1)

            def gru_first(ph, layer):
                copy_agg(ph, 0)
                gates_rz(ph, layer, 0, 0)
                copy_agg(ph, 1)
                gate_n(ph, layer, 0, 0)
                gates_rz(ph, layer, 0, 1)
                gate_n(ph, layer, 0, 1)

            def node_terms_and_squares():
                act.wait_ge(C["shift"], 1)
                with act.Fori(0, NT) as it:
                    for n in range(4):
                        h, ks = n // 2, slice((n % 2) * HK, (n % 2 + 1) * HK)
                        act.wait_ge(R["fetched"][n], it * (HK * SEM_DMA) + (BASE[2]["fetched"] + HK * SEM_DMA))
                        nc.scalar.activation(fetched2[:, h, ks, 1, :], fetched2[:, h, ks, 0, :], ACT.Square
                                             ).then_inc(R["squared"], 1)
                        if n == 0:
                            for i, column in enumerate((rstd, shift, has)):
                                last = nc.scalar.activation(norm_by[:, i:i + 1], column[:, bass.ds(it, 1)], ACT.Copy)
                            last.then_inc(C["norm2"], 1)
                            act.wait_ge(C["norm2"], it * 2 + 1)
                            nc.scalar.activation(normed_t[:, :], x[:, bass.ds(it, 1), :].rearrange("p o d -> p (o d)"), ACT.Relu,
                                                 bias=norm_by[:, 1:2], scale=norm_by[:, 0:1]).then_inc(C["norm2"], 1)
                        elif n == 1:
                            act.wait_ge(C["tr3"], it + 1)
                            nc.scalar.activation(normed_tT[:, :], pT[:, 0:D], ACT.Copy).then_inc(C["cp3"], 1)
                        elif n == 2:
                            act.wait_ge(C["terms"], it + 1)
                            nc.scalar.activation(node_term[:, bass.ds(it, 1), :].rearrange("p o d -> p (o d)"), pG[:, 0:D], ACT.Copy,
                                                 scale=norm_by[:, 2:3])
                            nc.scalar.activation(x[:, bass.ds(it, 1), :].rearrange("p o d -> p (o d)"), pG[:, D:2 * D], ACT.Copy
                                                 ).then_inc(C["tev"], 1)
                        else:
                            act.wait_ge(C["tev"], it + 1)

            def project(g):
                for h in range(2):
                    act.wait_ge(A["proj"], 2 * g + h + 1)
                    nc.scalar.activation(hT[:, g * GC + h * HC:g * GC + (h + 1) * HC], pG[:, h * 512:h * 512 + HC],
                                         ACT.Relu, bias=proj_b[:, 0:1]).then_inc(A["h"], 1)

            def copy_hn(g):
                if g >= 2:
                    act.wait_ge(A["proj"], 2 * (g - 1))
                copy_T(A, "tr", "cp", g, aT, ACT.Relu)

            def searches(i, j):
                first = 9 * i + j + (j > 2) + (j > 5)
                return range(min(first, NT), min(first + (2 if j in (2, 5) else 1), NT))

            def coarse_search(t):
                act.wait_ge(s_heads, 1)
                if t >= 1:
                    act.wait_ge(s_coarse, t)
                nc.scalar.activation(signs, heads, ACT.Sign, bias=node_b[:, t:t + 1], accum_out=coarse[:, t:t + 1]
                                     ).then_inc(s_coarse, 1)

            act.wait_ge(s_lanep, 1)
            nc.scalar.activation(heads, pO[:, 0:RUNS], ACT.Copy).then_inc(s_heads, 1)
            ln_std(A, 0, 0, 1)
            for b, part in enumerate(EARLY):
                act.wait_ge(s_wtr, b + 1)
                nc.scalar.activation(wT[:, part[0]:part[-1] + 1, :], pG[:, (b % 4) * 512:(b % 4) * 512 + len(part) * D],
                                     ACT.Copy).then_inc(s_wcp, 1)
            copy_hn(0)
            project(0)
            ln_std(A, 1, 1, 2)
            for i in range(NG):
                for j in range(GT):
                    evict_typed(A, i, range(j, j + 1))
                    for t in searches(i, j):
                        coarse_search(t)
                    if j == 0 and i + 2 < NG:
                        ln_std(A, i + 2, i + 2, i + 3)
                    if j == 1 and i + 1 < NG:
                        copy_hn(i + 1)
                    if j == 4 and i + 1 < NG:
                        project(i + 1)
            late_weights()
            act.wait_ge(s_degs, 1)
            nc.scalar.activation(amp[:, :], deg1[:, :], ACT.Ln).then_inc(s_log, 1)
            gru_first(B, 0)
            for i in range(NG):
                n = i + 1
                if n < NG:
                    gates_rz(B, 0, n, 0)
                evict_typed(B, i, range(0, 1))
                if n < NG:
                    gate_n(B, 0, n, 0)
                evict_typed(B, i, range(1, 4))
                if n + 1 < NG:
                    copy_agg(B, n + 1)
                if n < NG:
                    gates_rz(B, 0, n, 1)
                evict_typed(B, i, range(4, 5))
                if n < NG:
                    gate_n(B, 0, n, 1)
                evict_typed(B, i, range(5, GT))
            gru_first(C, 1)
            for i in range(NG - 1):
                n = i + 1
                gates_rz(C, 1, n, 0)
                gate_n(C, 1, n, 0)
                if n + 1 < NG:
                    copy_agg(C, n + 1)
                gates_rz(C, 1, n, 1)
                gate_n(C, 1, n, 1)
            ln_std(C, 0, 0, NG - 1)

            def copy_normed(b):
                if b >= 2:
                    act.wait_ge(C["bac"], b - 1)
                copy_T(C, "tr2", "cp2", b, bT, ACT.Relu)

            copy_normed(0)
            ln_std(C, 1, NG - 1, NG)
            for b in range(NG):
                if b + 1 < NG:
                    copy_normed(b + 1)
                if b >= 2:
                    act.wait_ge(C[f"tn{b % 2}"], SEM_DMA * (b // 2))
                act.wait_ge(C["bac"], b + 1)
                nc.scalar.activation(bstage[:, b % 2], pG[:, (b % 2) * 1024:(b % 2) * 1024 + GC].rearrange("p (t d) -> p t d", t=GT),
                                     ACT.Copy).then_inc(C["bev"], 1)
            node_terms_and_squares()
            def scale_sums(g, js):
                act.wait_ge(s_rows4[g % 2], GT * SEM_DMA * (g // 2 + 1))
                for j in js:
                    t = g * GT + j
                    last = nc.scalar.activation(rows4[:, g % 2, j, 0:2, :], rows4[:, g % 2, j, 0:2, :], ACT.Copy,
                                                scale=rdeg[:, t:t + 1])
                last.then_inc(Dp["scaled"], 1)

            def square_mean(g):
                act.wait_ge(Dp["scaled"], 2 * (g + 1))
                if g >= 1:
                    act.wait_ge(Dp["pre"], g)
                nc.scalar.activation(mean_sq, rows4[:, g % 2, :, 0, :], ACT.Square).then_inc(Dp["sq"], 1)

            def deviation(g):
                act.wait_ge(Dp["pre"], g + 1)
                nc.scalar.activation(rows4[:, g % 2, :, 1, :], rows4[:, g % 2, :, 1, :], ACT.Sqrt).then_inc(Dp["std4"], 1)

            scale_sums(0, range(4))
            scale_sums(0, range(4, GT))
            square_mean(0)
            deviation(0)
            for g in range(NG):
                n = g + 1
                for j in range(GT):
                    t = g * GT + j
                    act.wait_ge(Dp["tr"], t + 1)
                    if t >= 2:
                        act.wait_ge(Dp["fm"], t - 1)
                    nc.scalar.activation(aggT4[:, t % 2, :], pT[:, (t % 2) * 512:(t % 2) * 512 + 512], ACT.Copy
                                         ).then_inc(Dp["cp"], 1)
                    if j == 1 and g >= 1:
                        ln_std(Dp, g - 1, g - 1, g)
                    if n < NG:
                        if j == 0:
                            scale_sums(n, range(4))
                        elif j == 1:
                            scale_sums(n, range(4, GT))
                        elif j == 2:
                            square_mean(n)
                        elif j == 4:
                            deviation(n)
            ln_std(Dp, NG - 1, NG - 1, NG)
            copy_T(Ep, "tr", "cp", 0, aT)
            copy_T(Ep, "tr", "cp", 1, aT)
            for i in range(NG):
                ln_std(Ep, i, i, i + 1)
                if i + 2 < NG:
                    act.wait_ge(Ep["om"], i + 1)
                    copy_T(Ep, "tr", "cp", i + 2, aT)
            act.wait_ge(Ep["shift"], 1)
            act.wait_ge(Ep["tr"], NG)
            for t in range(NT):
                nc.scalar.activation(normed[:, t, :], x[:, t, :], ACT.Relu, bias=shift[:, t:t + 1], scale=rstd[:, t:t + 1]
                                     ).then_inc(Ep["norm2"], 1)
            for g in range(NG):
                act.wait_ge(Ep["tr2"], g + 1)
                if g >= 1:
                    act.wait_ge(Ep["sm"], g)
                nc.scalar.activation(normed_T, pT[:, 0:GC], ACT.Copy).then_inc(Ep["cp2"], 1)
                act.wait_ge(Ep["sm"], g + 1)
                nc.scalar.activation(node_term[:, g * GT:(g + 1) * GT, :], pG[:, 0:GC].rearrange("p (t d) -> p t d", t=GT), ACT.Copy
                                     ).then_inc(Ep["sev"], 1)
            for i in range(NG):
                if i >= 2:
                    act.wait_ge(Fp["om"], i - 1)
                copy_T(Fp, "tr", "cp", i, aT)

        @block.tensor
        def _(pe):
            mm = nc.tensor.matmul
            pe.wait_ge(s_const, 5)
            pe.wait_ge(s_lane, 1)
            mm(pO[:, 0:RUNS], ones[:, :], run_diag.rearrange("p j q -> p (j q)"), start=True, stop=True).then_inc(s_lanep, 1)
            pe.wait_ge(s_w, SEM_DMA * 3)

            def transpose_weights(banks, first, src, s0):
                for b, part in enumerate(banks, first):
                    if b >= 4:
                        pe.wait_ge(s_wcp, b - 3)
                    for n, s in enumerate(part):
                        last = nc.tensor.transpose(pG[:, (b % 4) * 512 + n * D:(b % 4) * 512 + n * D + D], src[:, s - s0, :], ident[:, :])
                    last.then_inc(s_wtr, 1)

            transpose_weights(EARLY, 0, wnat, 0)
            pe.wait_ge(s_wcp, len(EARLY))
            pe.wait_ge(s_heads, 1)

            def late_weights():
                pe.wait_ge(s_wl, SEM_DMA * 10)
                transpose_weights(LATE, len(EARLY), wlate, W_IH)
                pe.wait_ge(s_wcp, len(EARLY) + len(LATE))
                pe.wait_ge(s_bpost, 1)
                for c in range(12):
                    mm(pG[:, (c // 4) * 512 + (c % 4) * D:(c // 4) * 512 + (c % 4) * D + D], wpost[:, 1 + c, :], wT[:, W_LIN, :],
                       start=True, stop=True)
                mm(pG[:, 3 * 512:3 * 512 + D], wpost[:, 0, :], wT[:, W_LIN, :], start=True, stop=True)
                mm(pG[:, 3 * 512 + D:3 * 512 + 2 * D], post_bb[:, :], wT[:, W_LIN, :], start=True, stop=False)
                mm(pG[:, 3 * 512 + D:3 * 512 + 2 * D], ident[:, :], bias_rows[:, LIN_B, :], start=False, stop=True).then_inc(s_wc, 1)
                pe.wait_ge(s_wready, 1)

            def transposes(src, g):
                for j in range(GT):
                    last = nc.tensor.transpose(pT[:, j * D:(j + 1) * D], src(j), ident[:, :])
                return last

            def typed(ph, layer, g, js, ready):
                if js[0] == 0:
                    pe.wait_ge(ready, 2 * g + 2)
                w = wT[:, W_EDGE + T * layer:W_EDGE + T * (layer + 1), :].rearrange("p t d -> p (t d)")
                for j in js:
                    t = g * GT + j
                    for b in range(2):
                        if t >= 1:
                            pe.wait_ge(ph[f"ev{b}"], t)
                        mm(pO[:, b * 512:(b + 1) * 512], hT[:, t * P:(t + 1) * P], w[:, b * 512:(b + 1) * 512],
                           start=True, stop=True).then_inc(ph[f"mm{b}"], 1)

            def transpose_agg(ph, rnd, g):
                pe.wait_ge(s_rows[g], GT * SEM_DMA * (rnd + 1))
                if g >= 1:
                    pe.wait_ge(ph["cp"], g)
                transposes(lambda j: rows1[:, g * GT + j, :], g).then_inc(ph["tr"], 1)

            def gru_gates(ph, layer, g, h):
                ih, hh = W_IH + 3 * layer, W_HH + 3 * layer
                u = 2 * g + h
                if h == 0:
                    pe.wait_ge(ph["cp"], g + 1)
                ag = aT[:, g % 2, h * HC:(h + 1) * HC]
                hh_in = hT[:, g * GC + h * HC:g * GC + (h + 1) * HC]
                for c, signal in enumerate(("gate_r", "gate_z")):
                    if u >= 1:
                        pe.wait_ge(ph["rz"], 2 * u - 1 + c)
                    mm(pG[:, c * 512:c * 512 + HC], wT[:, hh + c, :], hh_in, start=True, stop=False)
                    mm(pG[:, c * 512:c * 512 + HC], wT[:, ih + c, :], ag, start=False, stop=True).then_inc(ph[signal], 1)
                if u >= 1:
                    pe.wait_ge(ph["hmul"], u)
                mm(pG[:, 3 * 512:3 * 512 + HC], wT[:, hh + 2, :], hh_in, start=True, stop=True).then_inc(ph["gate_nh"], 1)
                if u >= 1:
                    pe.wait_ge(ph["hadd"], u)
                mm(pG[:, 2 * 512:2 * 512 + HC], wT[:, ih + 2, :], ag, start=True, stop=True).then_inc(ph["gate"], 1)

            def gru_first(ph, layer):
                transpose_agg(ph, layer + 1, 0)
                gru_gates(ph, layer, 0, 0)
                transpose_agg(ph, layer + 1, 1)
                gru_gates(ph, layer, 0, 1)

            def carry(r):
                nb = 4 if ROUNDS[r][1] else 1
                pe.wait_ge(R["state"], BASE[r]["state"] + state_per_batch(r) * 2 * ITERS)
                for b in range(nb):
                    src = hist4[:, 1, K - 1, b, :] if nb == 4 else hist1[:, 1, K - 1, :]
                    last = nc.tensor.transpose(pT[:, b * D:(b + 1) * D], src, ident[:, :])
                last.then_inc(R["tails"], 1)
                pe.wait_ge(R["scanned"], BASE[r]["once"] + 1)
                for b in range(nb):
                    last = nc.tensor.transpose(pT[:, 512 + b * D:512 + (b + 1) * D], scan[:, b, 0:P], ident[:, :])
                last.then_inc(R["carries"], 1)

            def transpose_hn(g):
                pe.wait_ge(A["hn"], g + 1)
                if g >= 1:
                    pe.wait_ge(A["cp"], g)
                transposes(lambda j: hn[:, g % 2, j, :], g).then_inc(A["tr"], 1)

            def project(g):
                pe.wait_ge(A["cp"], g + 1)
                for h in range(2):
                    if g >= 1:
                        pe.wait_ge(A["h"], 2 * (g - 1) + h + 1)
                    mm(pG[:, h * 512:h * 512 + HC], wT[:, W_PROJ, :], aT[:, g % 2, h * HC:(h + 1) * HC],
                       start=True, stop=True).then_inc(A["proj"], 1)

            transpose_hn(0)
            project(0)
            for i in range(NG):
                typed(A, 0, i, range(2), A["h"])
                if i + 1 < NG:
                    transpose_hn(i + 1)
                typed(A, 0, i, range(2, 5), A["h"])
                if i + 1 < NG:
                    project(i + 1)
                typed(A, 0, i, range(5, GT), A["h"])
            pe.wait_ge(A["ev0"], NT)
            pe.wait_ge(A["ev1"], NT)
            pe.wait_ge(s_lane, 2)
            mm(pO[:, 0:1], prev_lane[:, :], col[:, C_LAST1:C_LAST1 + 1], start=True, stop=True).then_inc(s_lanep, 1)
            pe.wait_ge(s_lane, 3)
            mm(pO[:, 0:P], ones[:, :], diag[:, :], start=True, stop=True).then_inc(s_lanep, 1)
            pe.wait_ge(s_starts, 1)
            mm(pO[:, 512:512 + NT], next_lane[:, :], starts[:, 0:NT], start=True, stop=False)
            mm(pO[:, 512:512 + NT], corner[:, :], starts[:, 1:NT + 1], start=False, stop=True).then_inc(s_ends, 1)
            late_weights()
            carry(0)
            gru_first(B, 0)
            for i in range(NG):
                n = i + 1
                if n < NG:
                    gru_gates(B, 0, n, 0)
                typed(B, 1, i, range(4), B["hnew"])
                if n + 1 < NG:
                    transpose_agg(B, 1, n + 1)
                if n < NG:
                    gru_gates(B, 0, n, 1)
                typed(B, 1, i, range(4, GT), B["hnew"])
            carry(1)
            def source_terms(b):
                pe.wait_ge(C["cp2"], b + 1)
                if b == 0:
                    pe.wait_ge(C["hadd"], 2 * NG)
                    pe.wait_ge(C["rz"], 4 * NG)
                if b >= 2:
                    pe.wait_ge(C["bev"], b - 1)
                for j in range(GT):
                    o = (b % 2) * 1024 + j * D
                    last = mm(pG[:, o:o + D], bT[:, b % 2, j * D:(j + 1) * D], wT[:, W_SRC, :], start=True, stop=True)
                last.then_inc(C["bac"], 1)

            def node_terms():
                pe.wait_ge(C["bev"], NG)
                with pe.Fori(0, NT) as it:
                    pe.wait_ge(C["norm2"], it * 2 + 2)
                    nc.tensor.transpose(pT[:, 0:D], normed_t[:, :], ident[:, :]).then_inc(C["tr3"], 1)
                    pe.wait_ge(C["cp3"], it + 1)
                    mm(pG[:, 0:2 * D], normed_tT[:, :], wT[:, W_DST:W_X + 1, :].rearrange("p s d -> p (s d)"), start=True, stop=False)
                    mm(pG[:, 0:2 * D], ident[:, :], bias_rows[:, PRE_B:LIN_B + 1, :].rearrange("p s d -> p (s d)"),
                       start=False, stop=False)
                    mm(pG[:, D:2 * D], ident[:, :], x[:, bass.ds(it, 1), :].rearrange("p o d -> p (o d)"), start=False, stop=True
                       ).then_inc(C["terms"], 1)

            gru_first(C, 1)

            def out_product(g):
                pe.wait_ge(C["hnew"], 2 * g + 2)
                if g >= 1:
                    pe.wait_ge(C["xo"], g)
                for j in range(GT):
                    last = mm(pO[:, j * D:(j + 1) * D], hT[:, (g * GT + j) * P:(g * GT + j + 1) * P], wT[:, W_OUT, :],
                              start=True, stop=True)
                last.then_inc(C["om"], 1)

            for i in range(NG - 1):
                n = i + 1
                gru_gates(C, 1, n, 0)
                out_product(i)
                if n + 1 < NG:
                    transpose_agg(C, 2, n + 1)
                gru_gates(C, 1, n, 1)
            out_product(NG - 1)
            for b in range(NG + 1):
                if b < NG:
                    pe.wait_ge(C["hn"], b + 1)
                    if b >= 1:
                        pe.wait_ge(C["cp2"], b)
                    transposes(lambda j: hn[:, b % 2, j, :], b).then_inc(C["tr2"], 1)
                if b >= 1:
                    source_terms(b - 1)
            node_terms()
            carry(2)

            pe.wait_ge(C["tev"], NT)

            def dtrans(t):
                g, j = divmod(t, GT)
                if j == 0:
                    pe.wait_ge(Dp["agg"], g + 1)
                    pe.wait_ge(Dp["std4"], g + 1)
                if t >= 2:
                    pe.wait_ge(Dp["cp"], t - 1)
                for n, c in enumerate((2, 3, 0, 1)):
                    last = nc.tensor.transpose(pT[:, (t % 2) * 512 + n * D:(t % 2) * 512 + (n + 1) * D],
                                               rows4[:, g % 2, j, c, :], ident[:, :])
                last.then_inc(Dp["tr"], 1)

            dtrans(0)
            for t in range(NT):
                if t + 1 < NT:
                    dtrans(t + 1)
                pe.wait_ge(Dp["cp"], t + 1)
                if t >= 4:
                    pe.wait_ge(Dp["xo"], t - 3)
                for c in range(4):
                    last = mm(pG[:, (t % 4) * 512:(t % 4) * 512 + 3 * D], aggT4[:, t % 2, c * D:(c + 1) * D],
                              wcomb[:, c].rearrange("p v d -> p (v d)"), start=(c == 0), stop=(c == 3))
                last.then_inc(Dp["fm"], 1)
            carry(3)
            def transpose_rows(ph, rnd, g):
                pe.wait_ge(s_rows[g], GT * SEM_DMA * (rnd + 1))
                if g >= 1:
                    pe.wait_ge(ph["cp"], g)
                transposes(lambda j: rows1[:, g * GT + j, :], g).then_inc(ph["tr"], 1)

            transpose_rows(Ep, 3, 0)
            transpose_rows(Ep, 3, 1)
            for i in range(NG):
                pe.wait_ge(Ep["cp"], i + 1)
                if i >= 1:
                    pe.wait_ge(Ep["xo"], i)
                for j in range(GT):
                    last = mm(pO[:, j * D:(j + 1) * D], aT[:, i % 2, j * D:(j + 1) * D], l2w[:, :], start=True, stop=True)
                last.then_inc(Ep["om"], 1)
                if i + 2 < NG:
                    transpose_rows(Ep, 3, i + 2)
            pe.wait_ge(Ep["cp"], NG)
            for g in range(NG):
                pe.wait_ge(Ep["norm2"], GT * (g + 1))
                if g >= 1:
                    pe.wait_ge(Ep["cp2"], g)
                transposes(lambda j: normed[:, g * GT + j, :], g).then_inc(Ep["tr2"], 1)
                pe.wait_ge(Ep["cp2"], g + 1)
                if g >= 1:
                    pe.wait_ge(Ep["sev"], g)
                for j in range(GT):
                    mm(pG[:, j * D:(j + 1) * D], normed_T[:, j * D:(j + 1) * D], wT[:, W_SELF, :], start=True, stop=False)
                    last = mm(pG[:, j * D:(j + 1) * D], ident[:, :], bias_rows[:, SELF_B, :], start=False, stop=True)
                last.then_inc(Ep["sm"], 1)
            carry(4)
            transpose_rows(Fp, 4, 0)
            for i in range(NG):
                if i + 1 < NG:
                    transpose_rows(Fp, 4, i + 1)
                pe.wait_ge(Fp["cp"], i + 1)
                if i >= 1:
                    pe.wait_ge(Fp["om_read"], i)
                for j in range(GT):
                    last = mm(pO[:, j * D:(j + 1) * D], aT[:, i % 2, j * D:(j + 1) * D], wT[:, W_NEIGH, :], start=True, stop=True)
                last.then_inc(Fp["om"], 1)

        @block.vector
        def _(dve):
            v = nc.vector
            chain = [0]

            def link(ins):
                chain[0] += 1
                ins.then_inc(s_v, 1)
                dve.wait_ge(s_v, chain[0])

            def clear_padding(tile, value):
                v.memset(tile[P - 32:P, LAST:STEPS], value)
                return v.memset(tile[:, STEPS:STEPS + 2 * K], value)

            v.memset(dst_i[P - 32:P, LAST:STEPS], NO_NODE).then_inc(s_clear, 1)
            v.memset(x[:, NT - 1, :], 0.0).then_inc(s_clear, 1)
            v.memset(mend[0:1], 0.0).then_inc(s_clear, 1)
            clear_padding(idx_src, 0).then_inc(s_clear, 1)
            clear_padding(idx_typ, 0).then_inc(s_clear, 1)
            v.memset(masks[:, STEPS:STEPS + K, 0], 0.0)
            v.memset(starts[:, NT:NT + 1], float(E))
            link(v.memset(masks[:, 0, 0:1], 0.0))
            dve.wait_ge(s_const, 1)
            v.tensor_copy(lane_f[:, :], lane_i[:, :])
            link(v.tensor_copy(node_f[:, :], node_i[:, :]))
            link(v.tensor_scalar(node_b[:, :], node_f[:, :], -1.0, 0.5, ALU.mult, ALU.add))
            dve.wait_ge(s_dst, 3 * SEM_DMA)
            chain[0] += 1
            v.tensor_copy(dstf, dst_i[:, :]).then_inc(s_v, 1)
            dve.wait_ge(s_v, chain[0])
            dve.sem_inc(s_dstf, 1)
            c = lambda n: col[:, n:n + 1]
            dve.wait_ge(s_const, 5)
            v.tensor_tensor(run_diag, ident[:, :].unsqueeze(1).to_broadcast([P, LANE_RUNS, P]),
                            dstf.rearrange("p (j s) -> p j s", j=LANE_RUNS)[:, :, 0:1].to_broadcast([P, LANE_RUNS, P]), ALU.mult
                            ).then_inc(s_lane, 1)

            def lane_counts():
                v.tensor_scalar(e_tmp, dstf, dstf[:, 0:1], None, ALU.is_equal, ALU.add, accum_out=c(C_CNT))
                v.tensor_scalar_add(c(C_HEAD1), dstf[:, 0:1], 1.0)
                v.tensor_scalar_add(c(C_LAST1), dstf[:, STEPS - 1:STEPS], 1.0).then_inc(s_lane, 1)

            def edge_masks(part):
                if part == 0:
                    link(v.tensor_tensor(masks[:, 1:STEPS, 0], dstf[:, 1:STEPS], dstf[:, 0:STEPS - 1], ALU.is_equal))
                elif part == 1:
                    v.tensor_scalar(masks[:, :, 1], masks[:, :, 0], -1.0, BIG, ALU.add, ALU.mult)
                elif part == 2:
                    dve.wait_ge(s_edges, 6 * SEM_DMA)
                    v.tensor_copy(e_tmp, idx_src[:, 0:STEPS])
                elif part == 3:
                    link(v.tensor_copy(e_tmp2, idx_typ[:, 0:STEPS]))
                elif part == 4:
                    link(v.scalar_tensor_tensor(e_tmp2, e_tmp, float(T), e_tmp2, ALU.mult, ALU.add))
                elif part == 5:
                    link(v.tensor_copy(idx_typ[:, 0:STEPS], e_tmp2))
                else:
                    lane_counts()

            def lane_columns():
                v.tensor_scalar(c(C_WHOLE), c(C_CNT), float(STEPS), None, ALU.is_equal)
                link(v.scalar_tensor_tensor(c(C_FE), lane_f[:, :], float(STEPS), c(C_CNT), ALU.mult, ALU.add))
                link(v.tensor_scalar_add(c(C_FE1), c(C_FE), -1.0))
                v.tensor_copy(first_end[:, :], c(C_FE1))
                dve.wait_ge(s_lanep, 2)
                link(v.tensor_tensor(c(C_CONT), pO[:, 0:1], c(C_HEAD1), ALU.is_equal))
                v.tensor_scalar(c(C_CONTM), c(C_CONT), -1.0, BIG, ALU.add, ALU.mult)
                link(v.tensor_tensor(c(C_G), c(C_CONT), c(C_WHOLE), ALU.mult))
                v.tensor_scalar(diag[:, :], ident[:, :], c(C_G), None, ALU.mult).then_inc(s_lane, 1)

            def near_runs(g):
                ts = slice(g * GT, (g + 1) * GT)
                dve.wait_ge(s_coarse, (g + 1) * GT)
                link(v.tensor_scalar(near_f[:, ts], coarse[:, ts], -0.5, RUNS / 2 - 1.0, ALU.mult, ALU.add))
                link(v.tensor_scalar_max(near_f[:, ts], near_f[:, ts], 0.0))
                v.tensor_copy(near_row[:, ts], near_f[:, ts]).then_inc(s_nearix, 1)

            def ln_stats(g):
                for j in range(GT):
                    last = v.bn_stats(bn6[:, j, :], x[:, g * GT + j, :])
                link(last)
                ln_aggr(g)

            def ln_aggr(g):
                for j in range(GT):
                    last = v.bn_aggr(mv[:, g * GT + j, :], bn6[:, j, :])
                link(last)

            def ln_var(ph, lo, hi):
                v.tensor_scalar_add(var_e[:, lo * GT:hi * GT], mv[:, lo * GT:hi * GT, 1], EPS).then_inc(ph["var"], 1)

            def ln_recip(ph, n, lo, hi):
                dve.wait_ge(ph["std"], n + 1)
                link(v.reciprocal(rstd[:, lo * GT:hi * GT], std_l[:, lo * GT:hi * GT]))

            def ln_rstd(ph, n, lo, hi):
                ln_var(ph, lo, hi)
                ln_recip(ph, n, lo, hi)

            def norm_tile(g, j):
                t = g * GT + j
                return v.tensor_scalar(hn[:, g % 2, j, :], x[:, t, :], mv[:, t, 0:1], rstd[:, t:t + 1], ALU.subtract, ALU.mult)

            def ln_norm(ph, g, stored, read):
                if g >= 2:
                    dve.wait_ge(ph[read], g - 1)
                    if stored:
                        dve.wait_ge(ph[f"tn{g % 2}"], SEM_DMA * (g // 2))
                for j in range(GT):
                    last = norm_tile(g, j)
                if stored:
                    link(last)
                    last = v.tensor_scalar_max(hn[:, g % 2], hn[:, g % 2], 0.0)
                last.then_inc(ph["hn"], 1)

            def evict_typed(ph, g, js):
                for j in js:
                    t = g * GT + j
                    dve.wait_ge(ph["mm1"], t + 1)
                    if t >= TS:
                        dve.wait_ge(ph[f"tb{t % TS}"], SEM_DMA * (t // TS))
                    v.tensor_copy(tstage[:, t % TS, 512:1024], pO[:, 512:1024]).then_inc(ph["ev1"], 1)

            def count_starts(t):
                dve.wait_ge(s_rows[t // GT], SEM_DMA * GT)
                v.tensor_scalar(near[:, t % NEAR, :], near[:, t % NEAR, :], node_f[:, t:t + 1], None, ALU.is_lt, ALU.add,
                                accum_out=near_cnt[:, t:t + 1]).then_inc(s_near_used, 1)

            def add_mean_product(terms, g):
                for j in range(GT):
                    t = g * GT + j
                    last = v.scalar_tensor_tensor(terms[:, t, :], pO[:, j * D:(j + 1) * D], rdeg[:, t:t + 1], terms[:, t, :],
                                                  ALU.mult, ALU.add)
                return last

            def gru_add(ph, layer, g, h):
                u = 2 * g + h
                dve.wait_ge(ph["rz"], 2 * u + 1)
                dve.wait_ge(ph["gate_nh"], u + 1)
                v.scalar_tensor_tensor(gates[:, h, 2, :], pG[:, 3 * 512:3 * 512 + HC],
                                       b_hh[:, 3 * layer + 2:3 * layer + 3], gates[:, h, 0, :], ALU.add, ALU.mult
                                       ).then_inc(ph["hmul"], 1)
                dve.wait_ge(ph["hmul"], u + 1)
                dve.wait_ge(ph["gate"], u + 1)
                v.tensor_tensor(gates[:, h, 2, :], gates[:, h, 2, :], pG[:, 2 * 512:2 * 512 + HC], ALU.add
                                ).then_inc(ph["hadd"], 1)

            def gru_new(ph, g, h):
                hs = hT[:, g * GC + h * HC:g * GC + (h + 1) * HC]
                d = gates[:, h, 3, :]
                dve.wait_ge(ph["tanh"], 2 * g + h + 1)
                link(v.tensor_tensor(d, hs, gates[:, h, 2, :], ALU.subtract))
                link(v.tensor_tensor(d, d, gates[:, h, 1, :], ALU.mult))
                link(v.tensor_tensor(d, d, gates[:, h, 2, :], ALU.add))
                v.tensor_scalar_max(hs, d, 0.0).then_inc(ph["hnew"], 1)

            def gru_first(ph, layer):
                gru_add(ph, layer, 0, 0)
                gru_new(ph, 0, 0)
                gru_add(ph, layer, 0, 1)
                gru_new(ph, 0, 1)

            def add_bias(terms, i):
                link(v.tensor_tensor(terms, terms, bias_rows[:, i:i + 1, :].to_broadcast([P, NT, D]), ALU.add))

            def stage_first(r):
                idx = idx_typ if ROUNDS[r][0] == "typed" else idx_src
                for h in range(2):
                    for q in range(2):
                        v.tensor_copy(idx_now[:, h, q * HK:(q + 1) * HK], idx[:, h * K + q * HK:h * K + (q + 1) * HK]
                                      ).then_inc(R["staged"], 1)

            def walk(r):
                s, at, many = R, BASE[r], ROUNDS[r][1]
                idx = idx_typ if ROUNDS[r][0] == "typed" else idx_src
                per = state_per_batch(r)
                wait_table(dve, r)
                if many:
                    first = hist4[:, 1, K - 1].rearrange("p c d -> p (c d)")
                else:
                    first = hist1[:, 1, K - 1, :]
                link(v.memset(first, 0.0))

                link(v.tensor_copy(mask_now[:, 0], masks[:, 0:K, :]))
                ops = 3 if many else 1

                def stage(it, h, q):
                    v.tensor_copy(idx_now[:, h, q * HK:(q + 1) * HK], idx[:, bass.ds(it * (2 * K) + ((h + 2) * K + q * HK), HK)]
                                  ).then_inc(s["staged"], 1)

                def turn(it, again):
                    for h in range(2):
                        base = it * (2 * per) + (at["state"] + h * per)
                        if again:
                            dve.wait_ge(s["saved"][h], it * (saves(r) * SEM_DMA) + at["saved"])
                        for k in range(K):
                            if k % HK == 0:
                                n = 2 * h + k // HK
                                if many:
                                    dve.wait_ge(s["squared"], it * 4 + n + 1)
                                else:
                                    dve.wait_ge(s["fetched"][n], it * (HK * SEM_DMA) + (at["fetched"] + HK * SEM_DMA))
                            ph, pk = (h, k - 1) if k else (1 - h, K - 1)
                            keep, low = mask_now[:, h, k, 0:1], mask_now[:, h, k, 1:2]

                            def wait_before(op):
                                if k or h or again:
                                    dve.wait_ge(s["state"], base + (ops * (k - 1) + op + (1 if k - 1 > HK else 0)))

                            wait_before(1)
                            if not many:
                                v.scalar_tensor_tensor(hist1[:, h, k, :], hist1[:, ph, pk, :], keep, fetched1[:, h, k, :],
                                                       ALU.mult, ALU.add).then_inc(s["state"], 1)
                            else:
                                v.scalar_tensor_tensor(hist4[:, h, k, 0:2, :], hist4[:, ph, pk, 0:2, :], keep, fetched2[:, h, k],
                                                       ALU.mult, ALU.add).then_inc(s["state"], 1)
                                wait_before(2)
                                v.scalar_tensor_tensor(hist4[:, h, k, 2, :], hist4[:, ph, pk, 2, :], low, fetched2[:, h, k, 0, :],
                                                       ALU.add, ALU.max).then_inc(s["state"], 1)
                                wait_before(3)
                                v.scalar_tensor_tensor(hist4[:, h, k, 3, :], hist4[:, ph, pk, 3, :], low, fetched2[:, h, k, 0, :],
                                                       ALU.subtract, ALU.min).then_inc(s["state"], 1)
                            if k == 0 and h == 1:
                                stage(it, 0, 1)
                            elif k == 0 and again:
                                stage(it - 1, 1, 1)
                            elif k == HK:
                                stage(it, h, 0)
                                v.tensor_copy(mask_now[:, 1 - h], masks[:, bass.ds(it * (2 * K) + (h + 1) * K, K), :]
                                              ).then_inc(s["state"], 1)

                turn(0, False)
                with dve.Fori(1, ITERS) as it:
                    turn(it, True)

                nb = 4 if many else 1
                dve.wait_ge(s["tails"], at["once"] + 1)
                for b in range(nb):
                    mask, op0, op1 = ((g_mul, ALU.mult, ALU.add), (g_mul, ALU.mult, ALU.add),
                                      (g_max, ALU.add, ALU.max), (g_min, ALU.add, ALU.min))[b]
                    last = v.tensor_tensor_scan(scan[:, b, 1:P + 1], mask[:, :], pT[:, b * D:(b + 1) * D], 0.0, op0, op1)
                last.then_inc(s["scanned"], 1)
                dve.wait_ge(s["carries"], at["once"] + 1)
                dve.wait_ge(s["mend_in"], at["dma"] + SEM_DMA)
                for b in range(nb):
                    scal, op0, op1 = ((c(C_CONT), ALU.mult, ALU.add), (c(C_CONT), ALU.mult, ALU.add),
                                      (c(C_CONTM), ALU.add, ALU.max), (c(C_CONTM), ALU.subtract, ALU.min))[b]
                    last = v.scalar_tensor_tensor(mend[:, b, :], pT[:, 512 + b * D:512 + (b + 1) * D], scal, mend[:, b, :], op0, op1)
                last.then_inc(s["mended"], 1)

            dve.wait_ge(s_x0, SEM_DMA)
            ln_stats(0)
            ln_rstd(A, 0, 0, 1)
            ln_norm(A, 0, False, "tr")
            ln_stats(1)
            ln_rstd(A, 1, 1, 2)
            ln_norm(A, 1, False, "tr")
            dve.wait_ge(s_x, 2 * SEM_DMA)
            ln_stats(2)
            ln_var(A, 2, 3)
            for i in range(NG):
                for j in range(GT):
                    evict_typed(A, i, range(j, j + 1))
                    if i + 2 < NG:
                        if j == 0:
                            ln_recip(A, i + 2, i + 2, i + 3)
                            dve.wait_ge(A["tr"], i + 1)
                        last = norm_tile(i + 2, j)
                        if j == GT - 1:
                            last.then_inc(A["hn"], 1)
                    if i + 3 < NG:
                        last = v.bn_stats(bn6[:, j, :], x[:, (i + 3) * GT + j, :])
                        if j == GT - 1:
                            link(last)
                            ln_aggr(i + 3)
                            ln_var(A, i + 3, i + 4)
                    if i >= 2:
                        count_starts((i - 2) * GT + j)
                    if i == 1:
                        edge_masks(j)
                    if j == 0 and i >= 1:
                        near_runs(min(i - 1, 3) if i < 5 else i)
                        if i == 4:
                            near_runs(4)
                    if j == 1 and i == NG - 1:
                        stage_first(0)
            lane_columns()
            for t in range((NG - 2) * GT, NT):
                count_starts(t)
            dve.wait_ge(s_lanep, 3)
            link(v.tensor_copy(g_mul[:, :], pO[:, 0:P]))
            v.tensor_scalar(g_max[:, :], g_mul[:, :], -1.0, BIG, ALU.add, ALU.mult)
            v.tensor_scalar(g_min[:, :], g_mul[:, :], -1.0, -BIG, ALU.add, ALU.mult)
            dve.wait_ge(s_near_used, NT)
            v.scalar_tensor_tensor(starts[:, 0:NT], near_f[:, :], float(RUN), near_cnt[:, :], ALU.mult, ALU.add
                                   ).then_inc(s_starts, 1)
            dve.wait_ge(s_starts, 1)
            dve.wait_ge(s_b, 9 * SEM_DMA)
            v.tensor_copy(post_bb[:, :], post_b[:, 0:1].to_broadcast([P, D])).then_inc(s_bpost, 1)
            v.tensor_tensor(b_rz[:, :], b_ih[:, :], b_hh[:, :], ALU.add)
            v.tensor_tensor(bias_rows[:, SELF_B, :], bias_rows[:, SELF_B, :], bias_rows[:, NEIGH_B, :], ALU.add)
            dve.wait_ge(s_ends, 1)
            link(v.tensor_copy(ends[:, :], pO[:, 512:512 + NT]))
            v.tensor_scalar_add(end_f[:, :], ends[:, :], -1.0 - ZERO_ROW)
            link(v.tensor_tensor(deg[:, :], ends[:, :], starts[:, 0:NT], ALU.subtract))
            v.tensor_scalar_min(has[:, :], deg[:, :], 1.0)
            link(v.tensor_scalar_max(degc[:, :], deg[:, :], 1.0))
            link(v.tensor_tensor(end_f[:, :], end_f[:, :], has[:, :], ALU.mult))
            link(v.tensor_scalar_add(end_f[:, :], end_f[:, :], float(ZERO_ROW)))
            v.tensor_copy(end_row[:, :], end_f[:, :])
            v.tensor_scalar_add(deg1[:, :], degc[:, :], 1.0).then_inc(s_degs, 1)
            link(v.reciprocal(deg[:, :], degc[:, :]))
            v.tensor_tensor(rdeg[:, :], deg[:, :], has[:, :], ALU.mult).then_inc(s_nodes, 1)
            walk(0)
            dve.wait_ge(s_log, 1)
            link(v.reciprocal(att[:, :], amp[:, :]))
            gru_first(B, 0)
            stage_first(1)
            for i in range(NG):
                n = i + 1
                if n < NG:
                    gru_add(B, 0, n, 0)
                evict_typed(B, i, range(0, 2))
                if n < NG:
                    gru_new(B, n, 0)
                evict_typed(B, i, range(2, 4))
                if n < NG:
                    gru_add(B, 0, n, 1)
                evict_typed(B, i, range(4, 6))
                if n < NG:
                    gru_new(B, n, 1)
                evict_typed(B, i, range(6, GT))
            add_bias(x[:, :, :], OUT_B)
            walk(1)
            gru_first(C, 1)
            stage_first(2)

            def add_out(g):
                dve.wait_ge(C["om"], g + 1)
                v.tensor_tensor(tiles(g), tiles(g), pO[:, 0:GC].rearrange("p (t d) -> p t d", t=GT), ALU.add
                                ).then_inc(C["xo"], 1)
                dve.wait_ge(C["xo"], g + 1)
                ln_stats(g)

            for i in range(NG - 1):
                n = i + 1
                gru_add(C, 1, n, 0)
                gru_new(C, n, 0)
                add_out(i)
                if n == NG - 1:
                    ln_var(C, 0, NG - 1)
                gru_add(C, 1, n, 1)
                gru_new(C, n, 1)
            ln_recip(C, 0, 0, NG - 1)
            ln_norm(C, 0, False, "tr2")
            ln_norm(C, 1, False, "tr2")
            add_out(NG - 1)
            ln_rstd(C, 1, NG - 1, NG)
            link(v.scalar_tensor_tensor(shift[:, :], mv[:, :, 0], -1.0, rstd[:, :], ALU.mult, ALU.mult))
            for b in range(2, NG):
                ln_norm(C, b, False, "tr2")
            dve.sem_inc(C["shift"], 1)
            walk(2)
            dve.wait_ge(C["tev"], NT)

            def variance(g):
                r1 = rows4[:, g % 2, :, 1, :]
                dve.wait_ge(Dp["sq"], g + 1)
                link(v.tensor_tensor(r1, r1, mean_sq, ALU.subtract))
                v.tensor_scalar(r1, r1, 0.0, EPS, ALU.max, ALU.add).then_inc(Dp["pre"], 1)

            def add_terms(g, which):
                for n in which:
                    last = v.tensor_tensor(rows4[:, g % 2, :, n, :], rows4[:, g % 2, :, n, :],
                                           node_term[:, g * GT:(g + 1) * GT, :], ALU.add)
                return last

            def extremes(g):
                dve.wait_ge(s_rows4[g % 2], GT * SEM_DMA * (g // 2 + 1))
                add_terms(g, (2, 3))

            def mean(g):
                add_terms(g, (0,)).then_inc(Dp["agg"], 1)

            stage_first(3)
            extremes(0)
            variance(0)
            mean(0)
            for g in range(NG):
                n = g + 1
                for j in range(GT):
                    t = g * GT + j
                    dve.wait_ge(Dp["fm"], t + 1)
                    bank = (t % 4) * 512
                    xt = x[:, t, :]
                    link(v.tensor_tensor(xt, xt, pG[:, bank:bank + D], ALU.add))
                    link(v.scalar_tensor_tensor(xt, pG[:, bank + D:bank + 2 * D], amp[:, t:t + 1], xt, ALU.mult, ALU.add))
                    v.scalar_tensor_tensor(xt, pG[:, bank + 2 * D:bank + 3 * D], att[:, t:t + 1], xt, ALU.mult, ALU.add
                                           ).then_inc(Dp["xo"], 1)
                    if j == 1 and g >= 1:
                        ln_recip(Dp, g - 1, g - 1, g)
                        ln_norm(Dp, g - 1, True, "hn")
                    if n < NG:
                        if j == 2:
                            variance(n)
                        elif j == 3:
                            extremes(n)
                        elif j == 4:
                            mean(n)
                dve.wait_ge(Dp["xo"], GT * n)
                ln_stats(g)
                ln_var(Dp, g, n)
            ln_recip(Dp, NG - 1, NG - 1, NG)
            ln_norm(Dp, NG - 1, True, "hn")
            dve.wait_ge(Dp["hn"], NG)
            add_bias(x[:, :, :], L2_B)
            walk(3)
            stage_first(4)
            for i in range(NG):
                dve.wait_ge(Ep["om"], i + 1)
                add_mean_product(x, i).then_inc(Ep["xo"], 1)
                dve.wait_ge(Ep["xo"], i + 1)
                ln_stats(i)
                ln_rstd(Ep, i, i, i + 1)
                ln_norm(Ep, i, True, "hn")
            v.scalar_tensor_tensor(shift[:, :], mv[:, :, 0], -1.0, rstd[:, :], ALU.mult, ALU.mult).then_inc(Ep["shift"], 1)
            walk(4)
            dve.wait_ge(Ep["sev"], NG)
            for i in range(NG):
                dve.wait_ge(Fp["om"], i + 1)
                nt = node_term[:, i * GT:(i + 1) * GT, :]
                add_mean_product(node_term, i).then_inc(Fp["om_read"], 1)
                dve.wait_ge(Fp["om_read"], i + 1)
                v.scalar_tensor_tensor(tiles(i), nt, 0.0, tiles(i), ALU.max, ALU.add).then_inc(Fp["fin"], 1)


_INS = ["x", "src", "dst", "edge_type_8", "L0_gnn_node_proj_w", "L0_gnn_node_proj_b", "L0_gnn_edge_W",
        "L0_gnn_gru_wih", "L0_gnn_gru_whh", "L0_gnn_gru_bih", "L0_gnn_gru_bhh", "L0_gnn_out_w", "L0_gnn_out_b",
        "L1_gnn_W_pre", "L1_gnn_b_pre", "L1_gnn_W_post", "L1_gnn_b_post", "L1_gnn_W_lin", "L1_gnn_b_lin",
        "L2_gnn_W", "L2_gnn_b", "L3_gnn_W_self", "L3_gnn_b_self", "L3_gnn_W_neigh", "L3_gnn_b_neigh"]


def kernel(**inputs):
    import numpy as _np
    import concourse.bacc as _bacc
    from concourse import mybir as _mybir
    from concourse.bass_utils import run_bass_kernel_spmd as _run

    nc = _bacc.Bacc("TRN2", target_bir_lowering=False, num_devices=1)
    arrays, args = {}, {}
    for name in _INS:
        arr = _np.ascontiguousarray(inputs[name])
        arrays[f"in_{name}"] = arr
        args[name] = nc.dram_tensor(f"in_{name}", arr.shape, _mybir.dt.from_np(arr.dtype), kind="ExternalInput").ap()
    out = nc.dram_tensor("out_0", (N, D), _mybir.dt.float32, kind="ExternalOutput").ap()
    gnn_kernel(nc, args, out)
    r = _run(nc, [arrays], core_ids=[0])
    return r.results[0]["out_0"]
```
